# Optimizing a Trainium2 kernel written in Bass

```python
import numpy as np
import jax
import jax.numpy as jnp

def _softmax(x, axis=-1):
    return jax.nn.softmax(x, axis=axis)
def _gelu(x):
    return jax.nn.gelu(x, approximate=True)
def _silu(x):
    return jax.nn.silu(x)
def _sigmoid(x):
    return jax.nn.sigmoid(x)
def _layernorm(x, axis=-1, eps=1e-5):
    m = jnp.mean(x, axis=axis, keepdims=True)
    v = jnp.var(x, axis=axis, keepdims=True)
    return (x - m) / jnp.sqrt(v + eps)
def _scatter_add(tgt, idx, src, axis=0):
    return tgt.at[idx].add(src)
def _segment_sum(src, seg, n):
    return jax.ops.segment_sum(src, seg, n)

kernel_name = 'mk_adj_preln_d4_adj_512_411138'

def setup_inputs(seed: int = 0):
    np.random.seed(seed)
    _w = jnp.asarray
    def _rec_inputs():
        import jax
        import jax.numpy as jnp
        _gk = jax.random.key(seed)
        x = 7.22e-05 + 1 * jax.random.normal(jax.random.fold_in(_gk, 1), (128, 64, 512), jnp.float32)
        _w = (1.0 + jnp.arange(64, dtype=jnp.float32)) ** -0.5
        _w = _w / _w.mean()
        _pij = jnp.clip(0.0625 * _w[:, None] * _w[None, :], 0.0, 1.0)
        _a = jax.random.uniform(jax.random.fold_in(_gk, 2), (128, 64, 64)) < _pij
        _a = jnp.logical_or(_a, jnp.swapaxes(_a, -1, -2))
        _a = jnp.logical_or(_a, jnp.eye(64, dtype=bool))
        _af = _a.astype(jnp.float32)
        _af = _af * jax.random.uniform(jax.random.fold_in(_gk, 3), (128, 64, 64), jnp.float32, 0.05, 1)
        adj = _af
        return x, adj
    x, adj = _rec_inputs()
    def _L0_gnn_setup():
        import jax, jax.numpy as jnp
        import numpy as np
        EPS_LN = 1e-05

        def hypergraph_conv(x, adj, W, b):
            N, C, _ = adj.shape
            H = (adj != 0).astype(x.dtype)
            w = adj.reshape(N, -1)[:, :C]
            xw = jnp.einsum('ncd,hd->nch', x, W)
            Dn = jnp.einsum('nce,ne->nc', H, w)
            Dn = jnp.where(Dn > 0, 1.0 / Dn, 0.0)
            Be = H.sum(axis=1)
            Be = jnp.where(Be > 0, 1.0 / Be, 0.0)
            m = Be[:, :, None] * jnp.einsum('nce,nch->neh', H, xw)
            out = Dn[:, :, None] * jnp.einsum('nce,neh->nch', H, m)
            return out + b

        def layer_norm(x, g, b):
            mu = jnp.mean(x, axis=-1, keepdims=True)
            var = jnp.var(x, axis=-1, keepdims=True)
            return (x - mu) * jax.lax.rsqrt(var + EPS_LN) * g + b
        key = jax.random.key(seed)
        ks = jax.random.split(key, 4)
        N, C, Din, Dh, Dout = (16, 1024, 512, 1024, 512)
        x = jax.random.normal(ks[0], (N, C, Din), dtype=jnp.float32)
        adj = jax.random.uniform(ks[1], (N, C, C), dtype=jnp.float32, minval=0.1, maxval=1.0)
        W1 = jax.random.normal(ks[2], (Dh, Din), dtype=jnp.float32) * (1.0 / np.sqrt(Din))
        b1 = jnp.zeros((Dh,), dtype=jnp.float32)
        gamma = jnp.ones((Dh,), dtype=jnp.float32)
        beta = jnp.zeros((Dh,), dtype=jnp.float32)
        W2 = jax.random.normal(ks[3], (Dout, Dh), dtype=jnp.float32) * (1.0 / np.sqrt(Dh))
        b2 = jnp.zeros((Dout,), dtype=jnp.float32)
        return {'x': x, 'adj': adj, 'W1': W1, 'b1': b1, 'gamma': gamma, 'beta': beta, 'W2': W2, 'b2': b2}
    _L0_gnn_all = _L0_gnn_setup()
    _L0_gnn_in = {k: v for k, v in _L0_gnn_all.items() if k in ('W1', 'b1', 'gamma', 'beta', 'W2', 'b2', )}
    del _L0_gnn_all

    def _L1_gnn_setup():
        import jax, jax.numpy as jnp
        import numpy as np
        B, N, F_IN, F_HID, F_OUT = (32, 1024, 512, 512, 512)

        def _gcn_layer(x, adj, W, b):
            support = jnp.einsum('bnf,fh->bnh', x, W)
            return jnp.einsum('bnm,bmh->bnh', adj, support) + b
        key = jax.random.key(seed)
        ks = jax.random.split(key, 8)

        def xavier(k, fan_in, fan_out):
            bound = float(np.sqrt(6.0 / (fan_in + fan_out)))
            return jax.random.uniform(k, (fan_in, fan_out), jnp.float32, -bound, bound)
        return {'batch_graph': jax.random.normal(ks[0], (B, N, F_IN), jnp.float32), 'adj': jax.random.uniform(ks[1], (B, N, N), jnp.float32), 'W1': xavier(ks[2], F_IN, F_HID), 'b1': jnp.zeros((F_HID,), jnp.float32), 'W2': xavier(ks[3], F_HID, F_HID), 'b2': jnp.zeros((F_HID,), jnp.float32), 'W3': xavier(ks[4], F_HID, F_OUT), 'b3': jnp.zeros((F_OUT,), jnp.float32)}
    _L1_gnn_all = _L1_gnn_setup()
    _L1_gnn_in = {k: v for k, v in _L1_gnn_all.items() if k in ('W1', 'b1', 'W2', 'b2', 'W3', 'b3', )}
    del _L1_gnn_all

    def _L2_gnn_setup():
        import jax, jax.numpy as jnp
        import numpy as np
        B, N, DIN, DOUT, K = (4, 2048, 512, 512, 3)
        key = jax.random.key(seed)
        ks = jax.random.split(key, 8)
        X = jax.random.normal(ks[0], (B, N, DIN), dtype=jnp.float32)
        A = jax.random.uniform(ks[1], (B, N, N), dtype=jnp.float32)
        Wv = jax.random.normal(ks[2], (DIN, DOUT), dtype=jnp.float32) * 0.02
        bv = jax.random.normal(ks[3], (DOUT,), dtype=jnp.float32) * 0.02
        aw = jax.random.normal(ks[4], (2 * DOUT, 1), dtype=jnp.float32) * 0.05
        ab = jax.random.normal(ks[5], (1,), dtype=jnp.float32) * 0.05
        Wk = jax.random.normal(ks[6], (K, DIN, DOUT), dtype=jnp.float32) * 0.02
        bk = jax.random.normal(ks[7], (K, DOUT), dtype=jnp.float32) * 0.02
        return {'X': X, 'A': A, 'Wv': Wv, 'bv': bv, 'aw': aw, 'ab': ab, 'Wk': Wk, 'bk': bk}
    _L2_gnn_all = _L2_gnn_setup()
    _L2_gnn_in = {k: v for k, v in _L2_gnn_all.items() if k in ('Wv', 'bv', 'aw', 'ab', 'Wk', 'bk', )}
    del _L2_gnn_all

    def _L3_gnn_setup():
        import jax, jax.numpy as jnp
        import numpy as np
        EPS = 1e-06
        key = jax.random.key(seed)
        k1, k2, k3 = jax.random.split(key, 3)
        B, N, F, O = (8, 4096, 512, 512)
        x = jax.random.normal(k1, (B, N, F), dtype=jnp.float32)
        adj = jax.random.uniform(k2, (B, N, N), dtype=jnp.float32)
        W = jax.random.normal(k3, (O, 2 * F), dtype=jnp.float32) * (1.0 / np.sqrt(2 * F))
        return {'x': x, 'adj': adj, 'W': W}
    _L3_gnn_all = _L3_gnn_setup()
    _L3_gnn_in = {k: v for k, v in _L3_gnn_all.items() if k in ('W', )}
    del _L3_gnn_all

    return {
        "x": x,
        "adj": adj,
        "L0_gnn_W1": _L0_gnn_in["W1"],
        "L0_gnn_b1": _L0_gnn_in["b1"],
        "L0_gnn_gamma": _L0_gnn_in["gamma"],
        "L0_gnn_beta": _L0_gnn_in["beta"],
        "L0_gnn_W2": _L0_gnn_in["W2"],
        "L0_gnn_b2": _L0_gnn_in["b2"],
        "L1_gnn_W1": _L1_gnn_in["W1"],
        "L1_gnn_b1": _L1_gnn_in["b1"],
        "L1_gnn_W2": _L1_gnn_in["W2"],
        "L1_gnn_b2": _L1_gnn_in["b2"],
        "L1_gnn_W3": _L1_gnn_in["W3"],
        "L1_gnn_b3": _L1_gnn_in["b3"],
        "L2_gnn_Wv": _L2_gnn_in["Wv"],
        "L2_gnn_bv": _L2_gnn_in["bv"],
        "L2_gnn_aw": _L2_gnn_in["aw"],
        "L2_gnn_ab": _L2_gnn_in["ab"],
        "L2_gnn_Wk": _L2_gnn_in["Wk"],
        "L2_gnn_bk": _L2_gnn_in["bk"],
        "L3_gnn_W": _L3_gnn_in["W"],
    }

def reference(x, adj, L0_gnn_W1, L0_gnn_b1, L0_gnn_gamma, L0_gnn_beta, L0_gnn_W2, L0_gnn_b2, L1_gnn_W1, L1_gnn_b1, L1_gnn_W2, L1_gnn_b2, L1_gnn_W3, L1_gnn_b3, L2_gnn_Wv, L2_gnn_bv, L2_gnn_aw, L2_gnn_ab, L2_gnn_Wk, L2_gnn_bk, L3_gnn_W):
    import jax
    import jax.numpy as jnp
    def _L0_gnn_ref(x, adj, W1, b1, gamma, beta, W2, b2):
        import jax, jax.numpy as jnp
        import numpy as np
        EPS_LN = 1e-05

        def hypergraph_conv(x, adj, W, b):
            N, C, _ = adj.shape
            H = (adj != 0).astype(x.dtype)
            w = adj.reshape(N, -1)[:, :C]
            xw = jnp.einsum('ncd,hd->nch', x, W)
            Dn = jnp.einsum('nce,ne->nc', H, w)
            Dn = jnp.where(Dn > 0, 1.0 / Dn, 0.0)
            Be = H.sum(axis=1)
            Be = jnp.where(Be > 0, 1.0 / Be, 0.0)
            m = Be[:, :, None] * jnp.einsum('nce,nch->neh', H, xw)
            out = Dn[:, :, None] * jnp.einsum('nce,neh->nch', H, m)
            return out + b

        def layer_norm(x, g, b):
            mu = jnp.mean(x, axis=-1, keepdims=True)
            var = jnp.var(x, axis=-1, keepdims=True)
            return (x - mu) * jax.lax.rsqrt(var + EPS_LN) * g + b
        h = jax.nn.relu(hypergraph_conv(x, adj, W1, b1))
        h = layer_norm(h, gamma, beta)
        y = hypergraph_conv(h, adj, W2, b2)
        return y + x

    def _L1_gnn_ref(batch_graph, adj, W1, b1, W2, b2, W3, b3):
        import jax, jax.numpy as jnp
        import numpy as np
        B, N, F_IN, F_HID, F_OUT = (32, 1024, 512, 512, 512)

        def _gcn_layer(x, adj, W, b):
            support = jnp.einsum('bnf,fh->bnh', x, W)
            return jnp.einsum('bnm,bmh->bnh', adj, support) + b
        x = jax.nn.relu(_gcn_layer(batch_graph, adj, W1, b1))
        x = jax.nn.relu(_gcn_layer(x, adj, W2, b2))
        out = _gcn_layer(x, adj, W3, b3)
        return out

    def _L2_gnn_ref(X, A, Wv, bv, aw, ab, Wk, bk):
        import jax, jax.numpy as jnp
        import numpy as np
        B, N, DIN, DOUT, K = (4, 2048, 512, 512, 3)
        d = Wv.shape[1]
        Xw = X @ Wv + bv
        sj = Xw @ aw[:d, 0]
        si = Xw @ aw[d:, 0]
        e = jax.nn.leaky_relu(sj[:, None, :] + si[:, :, None] + ab[0], negative_slope=0.2)
        alpha_matrix = A * jnp.exp(e)
        transition = alpha_matrix / (jnp.sum(alpha_matrix, axis=-1, keepdims=True) + 1e-12)
        H = jnp.zeros(X.shape[:-1] + (d,), dtype=X.dtype)
        Xk = X
        for k in range(Wk.shape[0]):
            H = H + Xk @ Wk[k] + bk[k]
            Xk = jnp.einsum('bij,bjd->bid', transition, Xk)
        return jax.nn.relu(H)

    def _L3_gnn_ref(x, adj, W):
        import jax, jax.numpy as jnp
        import numpy as np
        EPS = 1e-06
        deg = jnp.sum(adj, axis=-1, keepdims=True)
        agg = jnp.einsum('bij,bjf->bif', adj, x) / jnp.maximum(deg, EPS)
        cat = jnp.concatenate([x, agg], axis=2)
        out = jnp.einsum('bnf,of->bno', cat, W)
        return jax.nn.relu(out)

    h = jnp.maximum(_layernorm(x, axis=-1), 0.0)
    x = x + _L0_gnn_ref(h, adj, L0_gnn_W1, L0_gnn_b1, L0_gnn_gamma, L0_gnn_beta, L0_gnn_W2, L0_gnn_b2)
    h = jnp.maximum(_layernorm(x, axis=-1), 0.0)
    x = x + _L1_gnn_ref(h, adj, L1_gnn_W1, L1_gnn_b1, L1_gnn_W2, L1_gnn_b2, L1_gnn_W3, L1_gnn_b3)
    h = jnp.maximum(_layernorm(x, axis=-1), 0.0)
    x = x + _L2_gnn_ref(h, adj, L2_gnn_Wv, L2_gnn_bv, L2_gnn_aw, L2_gnn_ab, L2_gnn_Wk, L2_gnn_bk)
    h = jnp.maximum(_layernorm(x, axis=-1), 0.0)
    x = x + _L3_gnn_ref(h, adj, L3_gnn_W)
    return x


_drawn_inputs = setup_inputs


def setup_inputs(seed=0):
    import zlib

    import numpy as np

    out = dict(_drawn_inputs(seed))
    spreads = {'L0_gnn_b1': (0.0, 0.1),
     'L0_gnn_gamma': (1.0, 0.2),
     'L0_gnn_beta': (0.0, 0.1),
     'L0_gnn_b2': (0.0, 0.284),
     'L1_gnn_b1': (0.0, 0.336),
     'L1_gnn_b2': (0.0, 0.8),
     'L1_gnn_b3': (0.0, 2.0)}
    factors = {'L2_gnn_Wv': 8.0,
     'L2_gnn_bv': 64.0,
     'L2_gnn_aw': 8.0,
     'L2_gnn_Wk': 8.0,
     'L2_gnn_bk': 64.0,
     'L3_gnn_W': 8.0}
    for name, (base, spread) in spreads.items():
        noise = np.random.default_rng([zlib.crc32(name.encode()), seed]).standard_normal(out[name].shape)
        drawn = base * np.exp(spread * noise) if base else spread * noise
        out[name] = jnp.asarray(drawn.astype(out[name].dtype))
    for name, factor in factors.items():
        out[name] = (out[name] * factor).astype(out[name].dtype)
    return out
```

```python
from contextlib import ExitStack

import numpy as np

import concourse.bass as bass
from concourse import mybir

P = 128
SLOTS = 4
F32 = mybir.dt.float32
F32R = mybir.dt.float32r
ALU = mybir.AluOpType
ACT = mybir.ActivationFunctionType
AX_X = mybir.AxisListType.X
EPS_LN = 1e-5
EPS_ALPHA = 1e-12
EPS_DEG = 1e-6
LEAK = 0.2


def order_hyper():
    return [
        ("lin1", 0), ("adj0", 3), ("lin1", 1), ("mid", 0), ("midsplit", 0), ("lin1", 2), ("mid", 1), ("midsplit", 1),
        ("lin1", 3), ("adja", 0), ("mid", 2), ("adja", 1), ("midsplit", 2), ("mid", 3), ("lina", 0), ("adjb", 0),
        ("midsplit", 3), ("resid", 0), ("lina", 1), ("adjb", 1), ("resid", 1), ("adja", 2), ("residb", 0), ("linb", 0),
        ("resid", 2), ("adja", 3), ("hprep_n", 0), ("hprep_n", 1), ("hprep_n", 2), ("hprep_n", 3), ("resid", 3),
        ("residb", 1), ("linb", 1), ("stats_n", 0), ("hyp_n", 0), ("hyp_n", 1), ("stats_n", 1), ("lina", 2), ("adjb", 2),
        ("norm_n", 0), ("split_n", 0), ("norm_n", 1), ("split_n", 1), ("lina", 3), ("residb", 2), ("stats_n", 2),
        ("adjb", 3), ("adj0_n", 0), ("residb", 3), ("linb", 2), ("hyp_n", 2), ("norm_n", 2), ("split_n", 2),
        ("stats_n", 3), ("adj0_n", 1), ("linb", 3), ("hyp_n", 3), ("norm_n", 3), ("split_n", 3), ("adj0_n", 2),
    ]


def order_gcn():
    steps = []
    for c in range(3):
        for t in range(SLOTS):
            if c == 2 and t < 3:
                steps += [("asplit_n", t), ("split_n", t)]
            steps.append((f"lin{c}", t))
            if t == 0:
                steps.append((f"adj{c}", 3))
            else:
                steps.append((f"adj{c + 1}", t - 1) if c < 2 else ("adj0_n", t - 1))
            if c == 0:
                steps.append(("resid", t))
            if c == 1:
                steps += [("stats_n", t)] + ([("norm_n", t - 1)] if t else [])
            if c == 2 and t == 0:
                steps.append(("norm_n", 3))
            if c == 2 and t == 3:
                steps += [("asplit_n", 3), ("split_n", 3)]
    return steps


def order_diffuse():
    return [
        ("lin2", 0), ("tr", 3), ("sj", 0), ("lin2", 1), ("sj", 1), ("tt", 0), ("lin2", 2), ("sj", 2), ("tt", 1),
        ("lin2", 3), ("sj", 3), ("tt", 2), ("lin1", 0), ("resid", 0), ("tt", 3), ("adj1", 0), ("lin1", 1),
        ("adj1", 1), ("resid", 1), ("lin1", 2), ("adj1", 2), ("stats_n", 0), ("resid", 2),
        ("lin1", 3), ("adj1", 3), ("norm_n", 0), ("stats_n", 1), ("resid", 3),
        ("lin0", 0), ("adj0", 0), ("norm_n", 1), ("stats_n", 2), ("lin0", 1), ("adj0", 1), ("tr_n", 0),
        ("norm_n", 2), ("stats_n", 3), ("lin0", 2), ("adj0", 2), ("tr_n", 1), ("norm_n", 3),
        ("lin0", 3), ("adj0", 3), ("tr_n", 2),
    ]


def order_mean():
    return [
        ("wb", 0), ("tr", 3), ("asplit", 0), ("wb", 1), ("asplit", 1), ("resid", 0), ("wb", 2), ("asplit", 2),
        ("resid", 1), ("wb", 3), ("asplit", 3), ("resid", 2), ("resid", 3),
        ("wa", 0), ("stats_n", 0), ("ag", 0), ("norm_n", 0), ("wa", 1), ("stats_n", 1), ("ag", 1), ("norm_n", 1),
        ("tr_n", 0), ("wa", 2), ("stats_n", 2), ("ag", 2), ("norm_n", 2), ("tr_n", 1), ("wa", 3), ("stats_n", 3),
        ("ag", 3), ("norm_n", 3), ("tr_n", 2),
    ]


ORDERS = [order_hyper(), order_gcn(), order_diffuse(), order_mean()]
RENAMED = [{"hprep_n": None, "hyp_n": None}, {"asplit_n": None, "split_n": None, "adj0_n": "tr_n"}, {},
           {"stats_n": None, "norm_n": None, "tr_n": None}]
LAST = [[(ren.get(name, name), t) for name, t in order if ren.get(name, name)] for order, ren in zip(ORDERS, RENAMED)]
LAST[0] = [step for name, t in LAST[0] for step in ([("asplit_n", t)] if name == "split_n" else []) + [(name, t)]]
SPLIT_AFTER = [
    [("lin1", 1), ("lin1", 2), ("lin1", 3), ("adja", 0), ("adja", 1), ("adjb", 0), ("adjb", 1), ("adja", 2),
     ("adja", 3), ("adjb", 2), ("adjb", 3), ("linb", 2)],
    [(f"lin{c}", t) for c in range(3) for t in range(SLOTS)],
    [(f"lin{c}", t) for c in (2, 1) for t in range(SLOTS)],
    [],
]
PLACE = [[0, 1, 2, 3], [4, 5, 0], [3, 2, 1], [4, 5]]
RAW = 4


def graph_stack(nc, x, adj, adj_t, w0a, w0b, gamma_c, b0a, beta_c, b0b, w1, b1, wv_t, bv_c, aw_c, ab, wk, bk, w3_t, out):
    rows, F = x.shape
    N = adj.shape[1]
    HID = w0a.shape[1]
    TILES = rows // P
    GROUPS = TILES // SLOTS
    KB = F // P
    assert 2 * N == P and HID == 2 * F and F == 512 and TILES % SLOTS == 0

    with ExitStack() as ctx:
        def sb(name, shape, dt=F32):
            return ctx.enter_context(nc.sbuf_tensor(name, shape, dt))

        def sem(name):
            return ctx.enter_context(nc.semaphore(name))

        def sems(prefix, names):
            return {k: sem(prefix + k) for k in names.split()}

        w_hi = sb("w_hi", [P, 6, KB, F], F32R)
        w_lo = sb("w_lo", [P, 6, KB, F], F32R)
        raw = sb("raw", [P, RAW, F])
        x_in = sb("x_in", [P, SLOTS, F])
        x_res = sb("x_res", [P, SLOTS, F])
        normed = sb("normed", [P, SLOTS, F])
        wide = sb("wide", [P, SLOTS, HID])
        row_hi = sb("row_hi", [P, SLOTS, F], F32R)
        row_lo = sb("row_lo", [P, SLOTS, F], F32R)
        col_hi = sb("col_hi", [P, SLOTS, F], F32R)
        col_lo = sb("col_lo", [P, SLOTS, F], F32R)
        adj_in = sb("adj_in", [P, SLOTS, P])
        adj_hi = sb("adj_hi", [P, SLOTS, P], F32R)
        adj_lo = sb("adj_lo", [P, SLOTS, P], F32R)
        inc_t = sb("inc_t", [P, SLOTS, P], F32R)
        binc_hi = sb("binc_hi", [P, SLOTS, P], F32R)
        binc_lo = sb("binc_lo", [P, SLOTS, P], F32R)
        b0a_bc = sb("b0a_bc", [P, 2, F])
        b0b_bc = sb("b0b_bc", [P, F])
        beta_bc = sb("beta_bc", [P, F])
        b1_bc = sb("b1_bc", [P, F])
        vj_bc = sb("vj_bc", [P, F])
        vi_bc = sb("vi_bc", [P, F])
        bk_bc = sb("bk_bc", [P, F])
        ident = sb("ident", [P, P])
        ones = sb("ones", [P, P])
        block_ones = sb("block_ones", [P, P])
        spread = sb("spread", [P, 2, P])
        cols = sb("cols", [P, 29])
        gamma_col, beta_col = cols[:, 0:8], cols[:, 8:16]
        bv_col, aw_col, ab_col = cols[:, 16:20], cols[:, 20:28], cols[:, 28:29]
        consts = sb("consts", [P, 4])
        eps_ln = sb("eps_ln", [P, 1])
        half_neg, c_bias, cj_tmp = consts[:, 0:1], consts[:, 1:2], consts[:, 2:3]
        stats = sb("stats", [P, SLOTS, 12])
        moments = sb("moments", [P, SLOTS, 2])
        var_eps = sb("var_eps", [P, SLOTS])
        rstd = sb("rstd", [P, SLOTS])
        stats2 = sb("stats2", [P, SLOTS, 12])
        moments2 = sb("moments2", [P, SLOTS, 2])
        var_eps2 = sb("var_eps2", [P, SLOTS])
        rstd2 = sb("rstd2", [P, SLOTS])
        size = sb("size", [P, 4, SLOTS])
        w_sum = sb("w_sum", [P, SLOTS])
        size_r = sb("size_r", [P, 2, SLOTS], F32R)
        w_r = sb("w_r", [P, SLOTS, 2], F32R)
        deg = sb("deg", [P, 8, SLOTS])
        D_SUM, D_POS, D_ZERO, D_SAFE, D_INV, D_OUT, M_SUM, DM_SUM = range(8)
        score = sb("score", [P, 6, SLOTS])
        S_J, S_I, S_IB, S_SUM, S_EPS, S_INV = range(6)
        ps = ctx.enter_context(nc.psum_tensor("ps", [P, SLOTS, 2, F], F32))

        def edge(t):
            return wide[:, t, F:F + P]

        def diag(t):
            return wide[:, t, F + P:F + 2 * P]

        def f32(ap):
            return ap.bitcast(F32)

        x_loaded = [sem(f"x_loaded{t}") for t in range(SLOTS)]
        x_stored = [sem(f"x_stored{t}") for t in range(SLOTS)]
        raw_loaded = [sem(f"raw_loaded{i}") for i in range(RAW)]
        s = sems("", "adj_loaded rows_loaded stats moments var_eps rstd norm relu resid split_hi split_lo "
                     "final raw_hi raw_lo raw_scaled cols_loaded vec_loaded b1_loaded pool_const ready spread "
                     "spread_used vec_const vec_out bk_loaded bk_sum")
        s0 = sems("l0_", "inc w_sum w_hi w_lo size_max size_inv size_hi size_lo binc hyp m_hi m_lo d_sum d_pos d_zero d_safe "
                         "d_inv d_out dm_sum adj0 adj0_hi adj0_lo lin1 affine relu2 stats2 moments2 var_eps2 rstd2 "
                         "norm2 rowa_hi rowa_lo adja adja_hi adja_lo rowb_hi rowb_lo adjb adjb_hi adjb_lo linb "
                         "res_b res_beta")
        s1 = sems("l1_", "asplit_hi asplit_lo " + " ".join(
            f"adj{c} adj{c}_hi adj{c}_lo lin{c} bias{c} row{c}_hi row{c}_lo" for c in range(3)))
        s2 = sems("l2_", "s_j s_i s_ib diag tr tr_hi tr_lo lin2 row2_hi row2_lo sj score leak exp alpha s_eps s_inv trans "
                         "tt tt_hi tt_lo adj1 row1_hi row1_lo adj0 biased")
        s3 = sems("l3_", "asplit_hi asplit_lo deg deg_max deg_inv tr tr_hi tr_lo wb row_hi row_lo wa ag scaled summed")

        def n(g, t):
            return g * SLOTS + t + 1

        def nl(layer, g, t):
            return g * SLOTS + (layer * TILES + t + 1)

        def target(layer, g, name):
            if not name.endswith("_n"):
                return layer, g
            return (layer + 1, 0) if isinstance(g, int) and g + 1 == GROUPS else (layer, g + 1)

        def first(g):
            return isinstance(g, int) and g == 0

        FULL = GROUPS - 1

        scores_blocks = [wv_t[k * P:(k + 1) * P, :] for k in range(KB)]
        layer_blocks = [
            [(PLACE[0][u], k, w0a[k * P:(k + 1) * P, u * F:(u + 1) * F]) for u in range(2) for k in range(KB)]
            + [(PLACE[0][2 + u], k, w0b[(u * KB + k) * P:(u * KB + k + 1) * P, :]) for u in range(2) for k in range(KB)],
            [(PLACE[1][c], k, w1[c][k * P:(k + 1) * P, :]) for c in range(3) for k in range(KB)],
            [(PLACE[2][c], k, wk[c, k * P:(k + 1) * P, :]) for c in (2, 1, 0) for k in range(KB)],
            [(PLACE[3][u], k, w3_t[(u * KB + k) * P:(u * KB + k + 1) * P, :]) for u in (1, 0) for k in range(KB)],
        ]
        split_blocks = [b for blocks in layer_blocks for b in blocks]
        block_end = [sum(len(b) for b in layer_blocks[:layer + 1]) for layer in range(4)]
        BETA0 = 2 * KB

        def start_block(eng, q):
            if q < KB:
                src = scores_blocks[q]
            else:
                src = split_blocks[q - KB][2]
                if q - RAW >= KB:
                    eng.wait_ge(s["raw_lo"], q - RAW - KB + 1)
                elif q >= RAW:
                    eng.wait_ge(s["spread_used"], 2 * (q - RAW) + 2)
            eng.dma_start(raw[:, q % RAW, :], src).then_inc(raw_loaded[q % RAW], 16)

        def wait_block(eng, q):
            eng.wait_ge(raw_loaded[q % RAW], 16 * (q // RAW + 1))

        block = ctx.enter_context(nc.Block())

        def groups(eng, layer, body):
            body(layer, 0, ORDERS[layer])
            with eng.Fori(1, GROUPS - 1) as g:
                body(layer, g, ORDERS[layer])
            body(layer, GROUPS - 1, LAST[layer])

        x_tiles = x.rearrange("(n p) f -> n p f", p=P)
        out_tiles = out.rearrange("(n p) f -> n p f", p=P)
        adj_rows = adj.rearrange("(n h) i j -> h i n j", h=2)
        adj_cols = adj_t.rearrange("(n h) j i -> h j n i", h=2)

        @block.sync
        def _(sp):
            def load_x(layer, g, t):
                if layer > 0 or not first(g):
                    sp.wait_ge(s["resid"], nl(layer, g, t) - SLOTS)
                if layer > 0:
                    sp.wait_ge(x_stored[t], 16 * ((layer - 1) * GROUPS + 1) + 16 * g)
                src = (x_tiles if layer == 0 else out_tiles)[bass.ds(g * SLOTS + t, 1)]
                sp.dma_start(x_in[:, t, :], src.rearrange("n p f -> p (n f)")).then_inc(x_loaded[t], 16)

            def load_adj(layer, g):
                before = layer - 1 if first(g) else layer
                if before >= 0:
                    groups_before = GROUPS if first(g) else g
                    if before == 0:
                        sp.wait_ge(s0["w_sum"], groups_before)
                    else:
                        used = {1: s1["asplit_lo"], 2: s2["alpha"], 3: s3["asplit_lo"]}[before]
                        sp.wait_ge(used, groups_before * SLOTS)
                src = adj_rows if layer == 2 else adj_cols
                for h in range(2):
                    sp.dma_start(adj_in[h * N:(h + 1) * N, :, h * N:(h + 1) * N],
                                 src[h, :, bass.ds(g * SLOTS, SLOTS), :]).then_inc(s["adj_loaded"], 16)
                if layer == 3:
                    sp.wait_ge(s2["tt"] if first(g) else s3["deg"], TILES if first(g) else g * SLOTS)
                    for h in range(2):
                        sp.dma_start(wide[h * N:(h + 1) * N, :, F + h * N:F + (h + 1) * N],
                                     adj_rows[h, :, bass.ds(g * SLOTS, SLOTS), :]).then_inc(s["rows_loaded"], 16)

            def store_x(layer, g, t):
                sp.wait_ge(s["final"], nl(layer, g, t))
                sp.dma_start(out_tiles[bass.ds(g * SLOTS + t, 1)].rearrange("n p f -> p (n f)"), x_res[:, t, :]
                             ).then_inc(x_stored[t], 16)

            sp.wait_ge(s["ready"], 1)
            load_adj(0, 0)
            for t in range(SLOTS):
                load_x(0, 0, t)
            for a, b, v in ((0, 8, gamma_c), (8, 16, beta_c), (16, 20, bv_c), (20, 28, aw_c)):
                sp.dma_start(cols[:, a:b], v).then_inc(s["cols_loaded"], 16)
            sp.dma_start(ab_col, ab.to_broadcast([P, 1])).then_inc(s["cols_loaded"], 16)
            for q in range(KB + BETA0):
                start_block(sp, q)
            for c in range(3):
                sp.dma_start(x_res[:, c, :], bk[c:c + 1, :].to_broadcast([P, F])).then_inc(s["bk_loaded"], 16)
            for u in range(2):
                sp.dma_start(b0a_bc[:, u, :], b0a[:, u * F:(u + 1) * F].to_broadcast([P, F])).then_inc(s["vec_loaded"], 16)
            sp.dma_start(b0b_bc[:], b0b.to_broadcast([P, F])).then_inc(s["vec_loaded"], 16)
            sp.dma_start(b1_bc[:], b1[2].to_broadcast([P, F])).then_inc(s["vec_loaded"], 16)
            for q in range(KB + BETA0, KB + block_end[0]):
                start_block(sp, q)

            def body(layer, g, order):
                nxt = target(layer, g, "_n")
                if nxt[0] < 4 and nxt[0] < 2:
                    load_adj(*nxt)
                if nxt[0] < 4:
                    for t in range(SLOTS):
                        load_x(*nxt, t)
                if nxt[0] in (2, 3):
                    load_adj(*nxt)
                for t in range(SLOTS):
                    store_x(layer, g, t)
            for layer in range(4):
                groups(sp, layer, body)
            for t in range(SLOTS):
                sp.wait_ge(x_stored[t], 16 * 4 * GROUPS)

        @block.tensor
        def _(pe):
            def product(out_ap, lhs_hi, lhs_lo, rhs_hi, rhs_lo, start=True, stop=True):
                nc.tensor.matmul(out_ap, lhs_hi, rhs_hi, start=start, stop=False)
                nc.tensor.matmul(out_ap, lhs_hi, rhs_lo, start=False, stop=False)
                return nc.tensor.matmul(out_ap, lhs_lo, rhs_hi, start=False, stop=stop)

            def linear(bank, t, place, start=True, stop=True):
                for k in range(KB):
                    last = product(ps[:, t, bank, :], col_hi[:, t, k * P:(k + 1) * P], col_lo[:, t, k * P:(k + 1) * P],
                                   w_hi[:, place, k, :], w_lo[:, place, k, :],
                                   start=start and k == 0, stop=stop and k == KB - 1)
                return last

            def mix_transposed(t):
                for k in range(KB):
                    last = product(ps[:, t, 0, k * P:(k + 1) * P],
                                   row_hi[:, t, k * P:(k + 1) * P], row_lo[:, t, k * P:(k + 1) * P],
                                   adj_hi[:, t, :], adj_lo[:, t, :])
                return last

            def mix(bank, t, start=True):
                return product(ps[:, t, bank, :], adj_hi[:, t, :], adj_lo[:, t, :], row_hi[:, t, :], row_lo[:, t, :],
                               start=start)

            def transposes(t):
                for k in range(KB):
                    last = nc.tensor.transpose(ps[:, t, 0, k * P:(k + 1) * P], normed[:, t, k * P:(k + 1) * P], ident[:])
                return last

            def hyper(g, name, t, i):
                if name == "hyp":
                    pe.wait_ge(s0["binc"], g * SLOTS + SLOTS)
                    if not first(g):
                        pe.wait_ge(s0["adjb_lo"], i - SLOTS)
                    nc.tensor.matmul(ps[:, t, 0, 0:P], inc_t[:, t, :], binc_hi[:, t, :], start=True, stop=False)
                    nc.tensor.matmul(ps[:, t, 0, 0:P], inc_t[:, t, :], binc_lo[:, t, :], start=False, stop=True)
                    nc.tensor.matmul(ps[:, t, 0, P:P + 2], inc_t[:, t, :], w_r[:, t, :], start=True, stop=True
                                     ).then_inc(s0["hyp"], 1)
                if name == "adj0":
                    pe.wait_ge(s0["d_sum"], i)
                    pe.wait_ge(s["split_lo"], nl(0, g, t))
                    mix_transposed(t).then_inc(s0["adj0"], 1)
                if name == "lin1":
                    pe.wait_ge(s0["adj0_lo"], i)
                    if first(g):
                        pe.wait_ge(s["raw_lo"], block_end[0])
                    else:
                        pe.wait_ge(s["final"], i - SLOTS)
                    linear(0, t, PLACE[0][0])
                    linear(1, t, PLACE[0][1]).then_inc(s0["lin1"], 1)
                if name == "adja":
                    pe.wait_ge(s0["rowa_lo"], i)
                    mix_transposed(t).then_inc(s0["adja"], 1)
                if name == "lina":
                    pe.wait_ge(s0["adja_lo"], i)
                    linear(1, t, PLACE[0][2], stop=False)
                if name == "adjb":
                    pe.wait_ge(s0["rowb_lo"], i)
                    mix_transposed(t).then_inc(s0["adjb"], 1)
                if name == "linb":
                    pe.wait_ge(s0["adjb_lo"], i)
                    linear(1, t, PLACE[0][3], start=False).then_inc(s0["linb"], 1)

            def gcn(g, name, t, i):
                c = int(name[3])
                if name == "adj0":
                    pe.wait_ge(s["split_lo"], nl(1, g, t))
                    pe.wait_ge(s1["asplit_lo"], i)
                    if first(g):
                        pe.wait_ge(s0["adjb_lo"], n(FULL, t))
                elif name in ("adj1", "adj2"):
                    pe.wait_ge(s1[f"row{c - 1}_lo"], i)
                if name.startswith("adj"):
                    mix_transposed(t).then_inc(s1[name], 1)
                else:
                    pe.wait_ge(s1[f"adj{c}_lo"], i)
                    if c == 0:
                        pe.wait_ge(s["final"], nl(1, g, t) - SLOTS)
                        if first(g):
                            pe.wait_ge(s["raw_lo"], block_end[1])
                    linear(1, t, PLACE[1][c]).then_inc(s1[name], 1)

            def diffuse(g, name, t, i):
                if name == "tr":
                    pe.wait_ge(s["norm"], nl(2, g, t))
                    if first(g):
                        pe.wait_ge(s1["adj2_lo"], n(FULL, t))
                    transposes(t).then_inc(s2["tr"], 1)
                if name == "lin2":
                    pe.wait_ge(s2["tr_lo"], i)
                    pe.wait_ge(s["final"], nl(2, g, t) - SLOTS)
                    if first(g):
                        pe.wait_ge(s["raw_lo"], block_end[2])
                    linear(1, t, PLACE[2][2]).then_inc(s2["lin2"], 1)
                if name == "sj":
                    pe.wait_ge(s2["s_ib"], i)
                    nc.tensor.matmul(ps[:, t, 0, 0:P], block_ones[:], diag(t), start=True, stop=True
                                     ).then_inc(s2["sj"], 1)
                if name == "tt":
                    pe.wait_ge(s2["trans"], i)
                    nc.tensor.transpose(ps[:, t, 0, 0:P], edge(t), ident[:]).then_inc(s2["tt"], 1)
                if name == "lin1":
                    pe.wait_ge(s2["tt_lo"], i)
                    linear(0, t, PLACE[2][1], stop=False)
                if name == "adj1":
                    pe.wait_ge(s2["row2_lo"], i)
                    mix(0, t, start=False).then_inc(s2["adj1"], 1)
                if name == "lin0":
                    linear(1, t, PLACE[2][0], stop=False)
                if name == "adj0":
                    pe.wait_ge(s2["row1_lo"], i)
                    mix(1, t, start=False).then_inc(s2["adj0"], 1)

            def mean(g, name, t, i):
                if name == "tr":
                    pe.wait_ge(s["norm"], nl(3, g, t))
                    if not first(g):
                        pe.wait_ge(s3["summed"], i - SLOTS)
                    transposes(t).then_inc(s3["tr"], 1)
                if name == "wb":
                    pe.wait_ge(s3["tr_lo"], i)
                    pe.wait_ge(s["final"], nl(3, g, t) - SLOTS)
                    if first(g):
                        pe.wait_ge(s["raw_lo"], block_end[3])
                    linear(1, t, PLACE[3][1]).then_inc(s3["wb"], 1)
                if name == "wa":
                    linear(0, t, PLACE[3][0])
                if name == "ag":
                    pe.wait_ge(s3["row_lo"], i)
                    pe.wait_ge(s3["asplit_lo"], i)
                    mix(1, t).then_inc(s3["ag"], 1)

            WORK = [(hyper, ("hyp", "adj0", "lin1", "adja", "lina", "adjb", "linb")),
                    (gcn, ("adj0", "adj1", "adj2", "lin0", "lin1", "lin2")),
                    (diffuse, ("tr", "lin2", "sj", "tt", "lin1", "adj1", "lin0", "adj0")),
                    (mean, ("tr", "wb", "wa", "ag"))]

            def body(layer, g, order):
                for name, t in order:
                    L, G = target(layer, g, name)
                    work, names = WORK[L]
                    if name.removesuffix("_n") in names:
                        work(G, name.removesuffix("_n"), t, n(G, t))

            for b in range(KB):
                wait_block(pe, b)
                for h in range(2):
                    pe.wait_ge(s["spread"], 2 * b + h + 1)
                    nc.tensor.matmul(ps[:, h, 1, :], spread[:, h, :], raw[:, b % RAW, :],
                                     start=b == 0, stop=b == KB - 1)
                    nc.tensor.matmul(ps[:, 2 + h, 1, 0:1], spread[:, h, :], bv_col[:, b:b + 1],
                                     start=b == 0, stop=b == KB - 1).then_inc(s["spread_used"], 1)
            for t in range(SLOTS):
                hyper(0, "hyp", t, n(0, t))
            for t in range(SLOTS - 1):
                hyper(0, "adj0", t, n(0, t))
            pe.wait_ge(s["vec_out"], 1)
            for j in range(2 * KB):
                q = KB + BETA0 + j
                wait_block(pe, q)
                pe.wait_ge(s["spread"], 2 * KB + j + 1)
                nc.tensor.matmul(ps[:, 3, 1, :], spread[:, j % 2, :], raw[:, q % RAW, :],
                                 start=j == 0, stop=j == 2 * KB - 1).then_inc(s["spread_used"], 1)
            pe.wait_ge(s["vec_out"], 2)
            for layer in range(4):
                groups(pe, layer, body)

        @block.scalar
        def _(act):
            def relu(out_ap, in_ap):
                return nc.scalar.activation(out_ap, in_ap, ACT.Relu)

            def copy(out_ap, in_ap):
                return nc.scalar.activation(out_ap, in_ap, ACT.Copy)

            def split_weights(b):
                place, k, _ = split_blocks[b]
                if BETA0 <= b < block_end[0]:
                    act.wait_ge(s["raw_scaled"], b - BETA0 + 1)
                else:
                    wait_block(act, KB + b)
                copy(w_hi[:, place, k, :], raw[:, (KB + b) % RAW, :]).then_inc(s["raw_hi"], 1)

            def split(layer, g, t):
                act.wait_ge(s["norm"], nl(layer, g, t))
                relu(normed[:, t, :], normed[:, t, :]).then_inc(s["relu"], 1)
                act.wait_ge(s["relu"], nl(layer, g, t))
                if layer == 0 and not first(g):
                    act.wait_ge(s0["adjb"], n(g, t) - SLOTS)
                elif layer == 1 and first(g):
                    act.wait_ge(s0["adjb"], n(FULL, t))
                elif layer == 1:
                    act.wait_ge(s1["adj2"], n(g, t) - SLOTS)
                copy(row_hi[:, t, :], normed[:, t, :]).then_inc(s["split_hi"], 1)

            def hyper(g, name, t, i):
                if name == "split":
                    split(0, g, t)
                if name == "hyp":
                    act.wait_ge(s0["hyp"], i)
                    if not first(g):
                        act.wait_ge(s0["dm_sum"], g)
                    nc.scalar.activation(adj_hi[:, t, :], ps[:, t, 0, 0:P], ACT.Copy,
                                         accum_out=deg[:, M_SUM, t:t + 1]).then_inc(s0["m_hi"], 1)
                if name in ("adj0", "adja", "adjb"):
                    act.wait_ge(s0[name], i)
                    copy(col_hi[:, t, :], ps[:, t, 0, :]).then_inc(s0[name + "_hi"], 1)
                if name == "lin1":
                    act.wait_ge(s0["affine"], i)
                    relu(wide[:, t, :], wide[:, t, :]).then_inc(s0["relu2"], 1)
                if name == "midsplit":
                    act.wait_ge(s0["norm2"], i)
                    copy(row_hi[:, t, :], wide[:, t, 0:F]).then_inc(s0["rowa_hi"], 1)
                if name == "adja":
                    copy(row_hi[:, t, :], wide[:, t, F:HID]).then_inc(s0["rowb_hi"], 1)

            def gcn(g, name, t, i):
                if name == "split":
                    split(1, g, t)
                if name == "asplit":
                    act.wait_ge(s["adj_loaded"], 32 * (GROUPS + 1) + 32 * g)
                    if first(g):
                        act.wait_ge(s0["adjb"], n(FULL, t))
                    else:
                        act.wait_ge(s1["adj2"], i - SLOTS)
                    copy(adj_hi[:, t, :], adj_in[:, t, :]).then_inc(s1["asplit_hi"], 1)
                if name in ("adj0", "adj1", "adj2"):
                    act.wait_ge(s1[name], i)
                    copy(col_hi[:, t, :], ps[:, t, 0, :]).then_inc(s1[name + "_hi"], 1)
                if name in ("lin0", "lin1"):
                    c = int(name[3])
                    act.wait_ge(s1[f"bias{c}"], i)
                    relu(row_hi[:, t, :], wide[:, t, 0:F]).then_inc(s1[f"row{c}_hi"], 1)

            def diffuse(g, name, t, i):
                if name == "tr":
                    act.wait_ge(s2["tr"], i)
                    relu(col_hi[:, t, :], ps[:, t, 0, :]).then_inc(s2["tr_hi"], 1)
                if name == "lin2":
                    act.wait_ge(s2["lin2"], i)
                    copy(row_hi[:, t, :], ps[:, t, 1, :]).then_inc(s2["row2_hi"], 1)
                if name == "sj":
                    act.wait_ge(s2["leak"], i)
                    nc.scalar.activation(edge(t), edge(t), ACT.Exp).then_inc(s2["exp"], 1)
                if name == "tt":
                    act.wait_ge(s2["tt"], i)
                    copy(adj_hi[:, t, :], ps[:, t, 0, 0:P]).then_inc(s2["tt_hi"], 1)
                if name == "adj1":
                    act.wait_ge(s2["adj1"], i)
                    copy(row_hi[:, t, :], ps[:, t, 0, :]).then_inc(s2["row1_hi"], 1)

            def mean(g, name, t, i):
                if name == "tr":
                    act.wait_ge(s3["tr"], i)
                    relu(col_hi[:, t, :], ps[:, t, 0, :]).then_inc(s3["tr_hi"], 1)
                if name == "wb":
                    act.wait_ge(s3["wb"], i)
                    copy(row_hi[:, t, :], ps[:, t, 1, :]).then_inc(s3["row_hi"], 1)
                if name == "asplit":
                    act.wait_ge(s["adj_loaded"], 32 * (3 * GROUPS + 1) + 32 * g)
                    if first(g):
                        act.wait_ge(s2["adj0"], n(FULL, t))
                    else:
                        act.wait_ge(s3["ag"], i - SLOTS)
                    copy(adj_hi[:, t, :], adj_in[:, t, :]).then_inc(s3["asplit_hi"], 1)

            WORK = [hyper, gcn, diffuse, mean]

            def body(layer, g, order):
                last = isinstance(g, int) and g == GROUPS - 1 and layer < 3
                b = block_end[layer]
                if last:
                    if layer == 1:
                        act.wait_ge(s0["linb"], TILES)
                    if layer == 2:
                        act.wait_ge(s1["lin1"], TILES)
                    start_block(act, KB + b)
                for name, t in order:
                    L, G = target(layer, g, name)
                    WORK[L](G, name.removesuffix("_n"), t, n(G, t))
                    if last and layer == 0 and (name, t) == ("mid", 3):
                        for c in range(2):
                            act.dma_start(b0a_bc[:, c, :], b1[c].to_broadcast([P, F])).then_inc(s["b1_loaded"], 16)
                    if last and (name, t) in SPLIT_AFTER[layer]:
                        if b + 1 < block_end[layer + 1]:
                            start_block(act, KB + b + 1)
                        split_weights(b)
                        b += 1

            for t in range(SLOTS):
                hyper(0, "split", t, n(0, t))
                hyper(0, "hyp", t, n(0, t))
            for t in range(SLOTS - 1):
                hyper(0, "adj0", t, n(0, t))
            for b in range(block_end[0]):
                split_weights(b)
            for layer in range(4):
                groups(act, layer, body)

        @block.vector
        def _(dve):
            V = nc.vector

            def lo_of(out_ap, full, hi):
                return V.tensor_tensor(out_ap, full, f32(hi), ALU.subtract)

            def carry_wait():
                V.memset(consts[:, 3:4], 0.0)

            def statistics(layer, g, t):
                dve.wait_ge(x_loaded[t], 16 * (layer * GROUPS + 1) + 16 * g)
                V.bn_stats(stats[:, t, 0:6], x_in[:, t, :]).then_inc(s["stats"], 1)
                dve.wait_ge(s["stats"], nl(layer, g, t))
                carry_wait()
                V.bn_aggr(moments[:, t, :], stats[:, t, 0:6]).then_inc(s["moments"], 1)

            def normalise(layer, g, t):
                dve.wait_ge(s["rstd"], nl(layer, g, t))
                i = n(g, t)
                if layer == 0 and not first(g):
                    dve.wait_ge(s["resid"], i - SLOTS)
                if layer == 1 and first(g):
                    dve.wait_ge(s["resid"], n(FULL, t))
                if layer == 1 and not first(g) or layer == 2 and first(g):
                    dve.wait_ge(s["split_lo"], nl(layer, g, t) - SLOTS)
                if layer == 2 and not first(g):
                    dve.wait_ge(s2["tr"], i - SLOTS)
                if layer == 3:
                    dve.wait_ge(s2["tr"] if first(g) else s3["tr"], n(FULL, t) if first(g) else i - SLOTS)
                V.tensor_scalar(normed[:, t, :], x_in[:, t, :], moments[:, t, 0:1], rstd[:, t:t + 1],
                                ALU.subtract, ALU.mult).then_inc(s["norm"], 1)

            def hyper(g, name, t, i):
                if name == "stats":
                    statistics(0, g, t)
                if name == "norm":
                    normalise(0, g, t)
                if name == "hprep":
                    if t == 0:
                        dve.wait_ge(s["adj_loaded"], 32 * (g + 1))
                        if not first(g):
                            dve.wait_ge(s0["hyp"], g * SLOTS)
                    V.tensor_scalar(inc_t[:, t, :], adj_in[:, t, :], 0.0, 0.0, ALU.not_equal, ALU.add,
                                    accum_out=size[:, 0, t:t + 1]).then_inc(s0["inc"], 1)
                if name == "hprep" and t == SLOTS - 1:
                    V.tensor_tensor(w_sum[:], adj_in[:, :, 0], adj_in[:, :, N], ALU.add).then_inc(s0["w_sum"], 1)
                    dve.wait_ge(s0["inc"], i)
                    V.tensor_scalar_max(size[:, 1, :], size[:, 0, :], 1.0).then_inc(s0["size_max"], 1)
                    dve.wait_ge(s0["w_sum"], g + 1)
                    V.tensor_copy(w_r[:, :, 0], w_sum[:]).then_inc(s0["w_hi"], 1)
                    dve.wait_ge(s0["size_max"], g + 1)
                    V.reciprocal(size[:, 2, :], size[:, 1, :]).then_inc(s0["size_inv"], 1)
                    dve.wait_ge(s0["w_hi"], g + 1)
                    lo_of(w_r[:, :, 1], w_sum[:], w_r[:, :, 0]).then_inc(s0["w_lo"], 1)
                    dve.wait_ge(s0["size_inv"], g + 1)
                    V.tensor_copy(size_r[:, 0, :], size[:, 2, :]).then_inc(s0["size_hi"], 1)
                    dve.wait_ge(s0["size_hi"], g + 1)
                    lo_of(size_r[:, 1, :], size[:, 2, :], size_r[:, 0, :]).then_inc(s0["size_lo"], 1)
                    dve.wait_ge(s0["size_lo"], g + 1)
                    for u in range(SLOTS):
                        V.tensor_scalar(binc_hi[:, u, :], f32(inc_t[:, u, :]), f32(size_r[:, 0, u:u + 1]), None, ALU.mult)
                        V.tensor_scalar(binc_lo[:, u, :], f32(inc_t[:, u, :]), f32(size_r[:, 1, u:u + 1]), None, ALU.mult
                                        ).then_inc(s0["binc"], 1)
                if name == "hyp":
                    dve.wait_ge(s0["m_hi"], i)
                    lo_of(adj_lo[:, t, :], ps[:, t, 0, 0:P], adj_hi[:, t, :])
                    V.reduce_sum(deg[:, D_SUM, t:t + 1], ps[:, t, 0, P:P + 2], AX_X).then_inc(s0["d_sum"], 1)
                if name == "hyp" and t == SLOTS - 1:
                    dve.wait_ge(s0["d_sum"], i)
                    V.tensor_scalar(deg[:, D_POS, :], deg[:, D_SUM, :], 0.0, None, ALU.is_gt).then_inc(s0["d_pos"], 1)
                    dve.wait_ge(s0["d_pos"], g + 1)
                    V.tensor_scalar(deg[:, D_ZERO, :], deg[:, D_POS, :], -1.0, 1.0, ALU.mult, ALU.add
                                    ).then_inc(s0["d_zero"], 1)
                    dve.wait_ge(s0["d_zero"], g + 1)
                    V.scalar_tensor_tensor(deg[:, D_SAFE, :], deg[:, D_SUM, :], 0.0, deg[:, D_ZERO, :],
                                           ALU.max, ALU.add).then_inc(s0["d_safe"], 1)
                    dve.wait_ge(s0["d_safe"], g + 1)
                    V.reciprocal(deg[:, D_INV, :], deg[:, D_SAFE, :]).then_inc(s0["d_inv"], 1)
                    dve.wait_ge(s0["d_inv"], g + 1)
                    V.tensor_tensor(deg[:, D_OUT, :], deg[:, D_INV, :], deg[:, D_POS, :], ALU.mult
                                    ).then_inc(s0["d_out"], 1)
                    dve.wait_ge(s0["d_out"], g + 1)
                    V.tensor_tensor(deg[:, DM_SUM, :], deg[:, D_OUT, :], deg[:, M_SUM, :], ALU.mult
                                    ).then_inc(s0["dm_sum"], 1)
                if name in ("adj0", "adja", "adjb"):
                    dve.wait_ge(s0[name + "_hi"], i)
                    lo_of(col_lo[:, t, :], ps[:, t, 0, :], col_hi[:, t, :]).then_inc(s0[name + "_lo"], 1)
                if name == "lin1":
                    dve.wait_ge(s0["lin1"], i)
                    if first(g):
                        dve.wait_ge(s["vec_loaded"], 64)
                    else:
                        dve.wait_ge(s0["rowb_lo"], i - SLOTS)
                    V.scalar_tensor_tensor(wide[:, t, :], ps[:, t, :, :].rearrange("p a f -> p (a f)"),
                                           deg[:, D_OUT, t:t + 1], b0a_bc[:].rearrange("p a f -> p (a f)"),
                                           ALU.mult, ALU.add).then_inc(s0["affine"], 1)
                if name == "mid":
                    dve.wait_ge(s0["relu2"], i)
                    for h in range(2):
                        V.bn_stats(stats2[:, t, 6 * h:6 * h + 6], wide[:, t, h * F:(h + 1) * F]).then_inc(s0["stats2"], 1)
                    dve.wait_ge(s0["stats2"], 2 * i)
                    carry_wait()
                    V.bn_aggr(moments2[:, t, :], stats2[:, t, :]).then_inc(s0["moments2"], 1)
                    dve.wait_ge(s0["rstd2"], i)
                    V.tensor_scalar(wide[:, t, :], wide[:, t, :], moments2[:, t, 0:1], rstd2[:, t:t + 1],
                                    ALU.subtract, ALU.mult).then_inc(s0["norm2"], 1)
                if name == "residb":
                    dve.wait_ge(s0["res_b"], i)
                    V.scalar_tensor_tensor(x_res[:, t, :], beta_bc[:], deg[:, DM_SUM, t:t + 1], x_res[:, t, :],
                                           ALU.mult, ALU.add).then_inc(s0["res_beta"], 1)
                if name == "linb":
                    dve.wait_ge(s0["linb"], i)
                    dve.wait_ge(s0["res_beta"], i)
                    V.scalar_tensor_tensor(x_res[:, t, :], ps[:, t, 1, :], deg[:, D_OUT, t:t + 1], x_res[:, t, :],
                                           ALU.mult, ALU.add).then_inc(s["final"], 1)

            def gcn(g, name, t, i):
                if name == "stats":
                    statistics(1, g, t)
                if name == "norm":
                    normalise(1, g, t)
                if name in ("adj0", "adj1", "adj2"):
                    dve.wait_ge(s1[name + "_hi"], i)
                    lo_of(col_lo[:, t, :], ps[:, t, 0, :], col_hi[:, t, :]).then_inc(s1[name + "_lo"], 1)
                if name in ("lin0", "lin1"):
                    c = int(name[3])
                    dve.wait_ge(s1[name], i)
                    if c == 0 and first(g):
                        dve.wait_ge(s["b1_loaded"], 32)
                        dve.wait_ge(s0["rowb_lo"], n(FULL, t))
                    V.tensor_tensor(wide[:, t, 0:F], ps[:, t, 1, :], b0a_bc[:, c, :], ALU.add).then_inc(s1[f"bias{c}"], 1)
                    dve.wait_ge(s1[f"row{c}_hi"], i)
                    V.scalar_tensor_tensor(row_lo[:, t, :], wide[:, t, 0:F], 0.0, f32(row_hi[:, t, :]),
                                           ALU.max, ALU.subtract).then_inc(s1[f"row{c}_lo"], 1)
                if name == "lin2":
                    dve.wait_ge(s1[name], i)
                    dve.wait_ge(s["resid"], nl(1, g, t))
                    V.tensor_tensor(x_res[:, t, :], ps[:, t, 1, :], x_res[:, t, :], ALU.add).then_inc(s["final"], 1)

            def diffuse(g, name, t, i):
                if name == "stats":
                    statistics(2, g, t)
                if name == "norm":
                    normalise(2, g, t)
                    dve.wait_ge(s["norm"], nl(2, g, t))
                    for v, at, done in ((vj_bc, S_J, "s_j"), (vi_bc, S_I, "s_i")):
                        V.scalar_tensor_tensor(wide[:, t, 0:F], normed[:, t, :], 0.0, v[:], ALU.max, ALU.mult,
                                               accum_out=score[:, at, t:t + 1]).then_inc(s2[done], 1)
                        dve.wait_ge(s2[done], i)
                if name == "tr":
                    dve.wait_ge(s2["tr_hi"], i)
                    V.scalar_tensor_tensor(col_lo[:, t, :], ps[:, t, 0, :], 0.0, f32(col_hi[:, t, :]),
                                           ALU.max, ALU.subtract).then_inc(s2["tr_lo"], 1)
                    if not first(g):
                        dve.wait_ge(s2["sj"], i - SLOTS)
                    V.tensor_scalar(diag(t), ident[:], score[:, S_J, t:t + 1], None, ALU.mult)
                    V.tensor_tensor(score[:, S_IB, t:t + 1], score[:, S_I, t:t + 1], c_bias, ALU.add
                                    ).then_inc(s2["s_ib"], 1)
                if name == "lin2":
                    dve.wait_ge(s2["row2_hi"], i)
                    lo_of(row_lo[:, t, :], ps[:, t, 1, :], row_hi[:, t, :]).then_inc(s2["row2_lo"], 1)
                if name == "sj":
                    dve.wait_ge(s2["sj"], i)
                    dve.wait_ge(s2["s_ib"], i)
                    if not first(g):
                        dve.wait_ge(s2["tt"], i - SLOTS)
                    V.scalar_tensor_tensor(edge(t), ps[:, t, 0, 0:P], score[:, S_IB, t:t + 1], block_ones[:],
                                           ALU.add, ALU.mult).then_inc(s2["score"], 1)
                    dve.wait_ge(s2["score"], i)
                    V.scalar_tensor_tensor(edge(t), edge(t), LEAK, edge(t), ALU.mult, ALU.max).then_inc(s2["leak"], 1)
                    dve.wait_ge(s2["exp"], i)
                    if t == 0:
                        dve.wait_ge(s["adj_loaded"], 32 * (2 * GROUPS + 1) + 32 * g)
                    V.scalar_tensor_tensor(edge(t), edge(t), 1.0, adj_in[:, t, :], ALU.mult, ALU.mult,
                                           accum_out=score[:, S_SUM, t:t + 1]).then_inc(s2["alpha"], 1)
                    dve.wait_ge(s2["alpha"], i)
                    V.tensor_scalar_add(score[:, S_EPS, t:t + 1], score[:, S_SUM, t:t + 1], EPS_ALPHA
                                        ).then_inc(s2["s_eps"], 1)
                    dve.wait_ge(s2["s_eps"], i)
                    V.reciprocal(score[:, S_INV, t:t + 1], score[:, S_EPS, t:t + 1]).then_inc(s2["s_inv"], 1)
                    dve.wait_ge(s2["s_inv"], i)
                    V.tensor_scalar(edge(t), edge(t), score[:, S_INV, t:t + 1], None, ALU.mult).then_inc(s2["trans"], 1)
                if name == "tt":
                    dve.wait_ge(s2["tt_hi"], i)
                    lo_of(adj_lo[:, t, :], ps[:, t, 0, 0:P], adj_hi[:, t, :]).then_inc(s2["tt_lo"], 1)
                if name == "adj1":
                    dve.wait_ge(s2["row1_hi"], i)
                    lo_of(row_lo[:, t, :], ps[:, t, 0, :], row_hi[:, t, :]).then_inc(s2["row1_lo"], 1)
                if name == "adj0":
                    dve.wait_ge(s2["adj0"], i)
                    V.tensor_tensor(wide[:, t, 0:F], ps[:, t, 1, :], bk_bc[:], ALU.add).then_inc(s2["biased"], 1)
                    dve.wait_ge(s2["biased"], i)
                    dve.wait_ge(s["resid"], nl(2, g, t))
                    V.scalar_tensor_tensor(x_res[:, t, :], wide[:, t, 0:F], 0.0, x_res[:, t, :], ALU.max, ALU.add
                                           ).then_inc(s["final"], 1)

            def mean(g, name, t, i):
                if name == "stats":
                    statistics(3, g, t)
                if name == "norm":
                    normalise(3, g, t)
                if name == "tr":
                    dve.wait_ge(s3["tr_hi"], i)
                    V.scalar_tensor_tensor(col_lo[:, t, :], ps[:, t, 0, :], 0.0, f32(col_hi[:, t, :]),
                                           ALU.max, ALU.subtract).then_inc(s3["tr_lo"], 1)
                if name == "wb":
                    dve.wait_ge(s3["row_hi"], i)
                    lo_of(row_lo[:, t, :], ps[:, t, 1, :], row_hi[:, t, :]).then_inc(s3["row_lo"], 1)
                if name == "asplit":
                    if t == 0:
                        dve.wait_ge(s["rows_loaded"], 32 * (g + 1))
                    V.reduce_sum(deg[:, D_SUM, t:t + 1], edge(t), AX_X).then_inc(s3["deg"], 1)
                if name == "asplit" and t == SLOTS - 1:
                    dve.wait_ge(s3["deg"], i)
                    V.tensor_scalar_max(deg[:, D_SAFE, :], deg[:, D_SUM, :], EPS_DEG).then_inc(s3["deg_max"], 1)
                    dve.wait_ge(s3["deg_max"], g + 1)
                    V.reciprocal(deg[:, D_OUT, :], deg[:, D_SAFE, :]).then_inc(s3["deg_inv"], 1)
                if name == "ag":
                    dve.wait_ge(s3["ag"], i)
                    dve.wait_ge(s3["deg_inv"], g + 1)
                    V.tensor_scalar(wide[:, t, 0:F], ps[:, t, 1, :], deg[:, D_OUT, t:t + 1], None, ALU.mult
                                    ).then_inc(s3["scaled"], 1)
                    dve.wait_ge(s3["scaled"], i)
                    V.tensor_tensor(wide[:, t, 0:F], ps[:, t, 0, :], wide[:, t, 0:F], ALU.add).then_inc(s3["summed"], 1)
                    dve.wait_ge(s3["summed"], i)
                    dve.wait_ge(s["resid"], nl(3, g, t))
                    V.scalar_tensor_tensor(x_res[:, t, :], wide[:, t, 0:F], 0.0, x_res[:, t, :], ALU.max, ALU.add
                                           ).then_inc(s["final"], 1)

            WORK = [hyper, gcn, diffuse, mean]

            def body(layer, g, order):
                for name, t in order:
                    L, G = target(layer, g, name)
                    WORK[L](G, name.removesuffix("_n"), t, n(G, t))

            dve.wait_ge(s["ready"], 1)
            dve.wait_ge(s["cols_loaded"], 16 * 5)
            for b in range(KB):
                for h in range(2):
                    if b:
                        dve.wait_ge(s["spread_used"], 2 * (b - 1) + h + 1)
                    V.tensor_scalar(spread[:, h, :], ones[:], aw_col[:, h * KB + b:h * KB + b + 1], None, ALU.mult
                                    ).then_inc(s["spread"], 1)
            for t in range(SLOTS):
                hyper(0, "stats", t, n(0, t))
                hyper(0, "hprep", t, n(0, t))
            for t in range(SLOTS):
                hyper(0, "norm", t, n(0, t))
            dve.wait_ge(s["spread_used"], 2 * KB)
            V.tensor_copy(vj_bc[:], ps[:, 0, 1, :])
            V.tensor_copy(vi_bc[:], ps[:, 1, 1, :])
            V.tensor_tensor(cj_tmp, ps[:, 2, 1, 0:1], ab_col, ALU.add).then_inc(s["vec_const"], 1)
            dve.wait_ge(s["vec_const"], 1)
            V.tensor_tensor(c_bias, ps[:, 3, 1, 0:1], cj_tmp, ALU.add).then_inc(s["vec_out"], 1)
            for t in range(SLOTS):
                hyper(0, "hyp", t, n(0, t))
            for t in range(SLOTS - 1):
                hyper(0, "adj0", t, n(0, t))
            for j in range(2):
                V.tensor_scalar(spread[:, j, :], ones[:], beta_col[:, j:j + 1], None, ALU.mult).then_inc(s["spread"], 1)
            for j in range(2 * KB):
                q = KB + BETA0 + j
                dve.wait_ge(s["spread_used"], 2 * KB + j + 1)
                if j + 2 < 2 * KB:
                    V.tensor_scalar(spread[:, j % 2, :], ones[:], beta_col[:, j + 2:j + 3], None, ALU.mult
                                    ).then_inc(s["spread"], 1)
                V.tensor_scalar(raw[:, q % RAW, :], raw[:, q % RAW, :], gamma_col[:, j:j + 1], None, ALU.mult
                                ).then_inc(s["raw_scaled"], 1)
            V.tensor_copy(beta_bc[:], ps[:, 3, 1, :]).then_inc(s["vec_out"], 1)
            for layer in range(4):
                groups(dve, layer, body)

        @block.gpsimd
        def _(pool):
            Q = nc.gpsimd

            def lo_of(out_ap, full, hi):
                return Q.tensor_tensor(out_ap, full, f32(hi), ALU.subtract)

            def split_weights(b):
                place, k, _ = split_blocks[b]
                pool.wait_ge(s["raw_hi"], b + 1)
                lo_of(w_lo[:, place, k, :], raw[:, (KB + b) % RAW, :], w_hi[:, place, k, :]).then_inc(s["raw_lo"], 1)

            def reciprocal_deviation(layer, g, t):
                pool.wait_ge(s["moments"], nl(layer, g, t))
                if layer > 0 or not first(g):
                    pool.wait_ge(s["norm"], nl(layer, g, t) - SLOTS)
                Q.tensor_tensor(var_eps[:, t:t + 1], moments[:, t, 1:2], eps_ln[:], ALU.add
                                ).then_inc(s["var_eps"], 1)
                pool.wait_ge(s["var_eps"], nl(layer, g, t))
                Q.tensor_tensor(rstd[:, t:t + 1], var_eps[:, t:t + 1], half_neg, ALU.pow).then_inc(s["rstd"], 1)

            def split(layer, g, t):
                pool.wait_ge(s["split_hi"], nl(layer, g, t))
                lo_of(row_lo[:, t, :], normed[:, t, :], row_hi[:, t, :]).then_inc(s["split_lo"], 1)

            def stored(layer, g, t):
                if layer > 0 or not first(g):
                    pool.wait_ge(x_stored[t], 16 * layer * GROUPS + 16 * g)

            def hyper(g, name, t, i):
                if name == "stats":
                    reciprocal_deviation(0, g, t)
                if name == "split":
                    split(0, g, t)
                if name == "mid":
                    pool.wait_ge(s0["moments2"], i)
                    Q.tensor_tensor(var_eps2[:, t:t + 1], moments2[:, t, 1:2], eps_ln[:], ALU.add
                                    ).then_inc(s0["var_eps2"], 1)
                    pool.wait_ge(s0["var_eps2"], i)
                    Q.tensor_tensor(rstd2[:, t:t + 1], var_eps2[:, t:t + 1], half_neg, ALU.pow).then_inc(s0["rstd2"], 1)
                if name == "midsplit":
                    pool.wait_ge(s0["rowa_hi"], i)
                    lo_of(row_lo[:, t, :], wide[:, t, 0:F], row_hi[:, t, :]).then_inc(s0["rowa_lo"], 1)
                if name == "resid":
                    stored(0, g, t)
                    if first(g) and t == 0:
                        pool.wait_ge(s["vec_loaded"], 64)
                    pool.wait_ge(s["relu"], i)
                    Q.tensor_tensor(x_res[:, t, :], x_in[:, t, :], normed[:, t, :], ALU.add).then_inc(s["resid"], 1)
                    pool.wait_ge(s["resid"], i)
                    Q.tensor_tensor(x_res[:, t, :], x_res[:, t, :], b0b_bc[:], ALU.add).then_inc(s0["res_b"], 1)
                if name == "adja":
                    pool.wait_ge(s0["rowb_hi"], i)
                    lo_of(row_lo[:, t, :], wide[:, t, F:HID], row_hi[:, t, :]).then_inc(s0["rowb_lo"], 1)

            def gcn(g, name, t, i):
                if name == "stats":
                    reciprocal_deviation(1, g, t)
                if name == "split":
                    split(1, g, t)
                if name == "asplit":
                    pool.wait_ge(s1["asplit_hi"], i)
                    lo_of(adj_lo[:, t, :], adj_in[:, t, :], adj_hi[:, t, :]).then_inc(s1["asplit_lo"], 1)
                if name == "resid":
                    stored(1, g, t)
                    pool.wait_ge(s["norm"], nl(1, g, t))
                    Q.tensor_tensor(x_res[:, t, :], x_in[:, t, :], b1_bc[:], ALU.add).then_inc(s["resid"], 1)

            def diffuse(g, name, t, i):
                if name == "stats":
                    reciprocal_deviation(2, g, t)
                if name == "resid":
                    stored(2, g, t)
                    pool.wait_ge(s["norm"], nl(2, g, t))
                    Q.tensor_tensor(x_res[:, t, :], x_in[:, t, :], ones[:, 0:1].to_broadcast([P, F]), ALU.mult).then_inc(s["resid"], 1)

            def mean(g, name, t, i):
                if name == "stats":
                    reciprocal_deviation(3, g, t)
                if name == "resid":
                    stored(3, g, t)
                    pool.wait_ge(s["norm"], nl(3, g, t))
                    Q.tensor_tensor(x_res[:, t, :], x_in[:, t, :], ones[:, 0:1].to_broadcast([P, F]), ALU.mult).then_inc(s["resid"], 1)
                if name == "asplit":
                    pool.wait_ge(s3["asplit_hi"], i)
                    lo_of(adj_lo[:, t, :], adj_in[:, t, :], adj_hi[:, t, :]).then_inc(s3["asplit_lo"], 1)

            WORK = [hyper, gcn, diffuse, mean]

            def body(layer, g, order):
                last = isinstance(g, int) and g == GROUPS - 1 and layer < 3
                b = block_end[layer]
                for name, t in order:
                    L, G = target(layer, g, name)
                    WORK[L](G, name.removesuffix("_n"), t, n(G, t))
                    if last and (name, t) in SPLIT_AFTER[layer]:
                        split_weights(b)
                        b += 1

            Q.memset(adj_in[:], 0.0)
            Q.memset(ones[:], 1.0)
            Q.memset(eps_ln[:], EPS_LN)
            Q.memset(ident[:], 0.0)
            Q.memset(block_ones[:], 0.0)
            Q.memset(half_neg, -0.5).then_inc(s["pool_const"], 1)
            pool.wait_ge(s["pool_const"], 1)
            for h in range(2):
                Q.memset(block_ones[h * N:(h + 1) * N, h * N:(h + 1) * N], 1.0).then_inc(s["pool_const"], 1)
            pool.wait_ge(s["pool_const"], 3)
            Q.affine_select(out=ident[:], in_=ident[:], compare_op=ALU.not_equal, fill=1.0, base=0,
                            pattern=[[-1, P]], channel_multiplier=1).then_inc(s["ready"], 1)
            for t in range(SLOTS):
                hyper(0, "stats", t, n(0, t))
            for t in range(SLOTS):
                hyper(0, "split", t, n(0, t))
            for b in range(block_end[0]):
                split_weights(b)
            pool.wait_ge(s["bk_loaded"], 48)
            Q.tensor_tensor(bk_bc[:], x_res[:, 0, :], x_res[:, 1, :], ALU.add).then_inc(s["bk_sum"], 1)
            pool.wait_ge(s["bk_sum"], 1)
            Q.tensor_tensor(bk_bc[:], bk_bc[:], x_res[:, 2, :], ALU.add).then_inc(s["bk_sum"], 1)
            for layer in range(4):
                groups(pool, layer, body)


def kernel(x, adj, L0_gnn_W1, L0_gnn_b1, L0_gnn_gamma, L0_gnn_beta, L0_gnn_W2, L0_gnn_b2, L1_gnn_W1, L1_gnn_b1,
           L1_gnn_W2, L1_gnn_b2, L1_gnn_W3, L1_gnn_b3, L2_gnn_Wv, L2_gnn_bv, L2_gnn_aw, L2_gnn_ab, L2_gnn_Wk,
           L2_gnn_bk, L3_gnn_W):
    import concourse.bacc as bacc
    from concourse.bass_utils import run_bass_kernel_spmd

    def a(v):
        return np.ascontiguousarray(v)

    def row(v):
        return a(np.asarray(v).reshape(1, -1))

    def columns(v):
        return a(np.asarray(v).reshape(-1, P).T)

    x = np.asarray(x)
    arrays = {
        "x": a(x.reshape(-1, x.shape[-1])),
        "adj": a(adj),
        "adj_t": a(np.swapaxes(np.asarray(adj), 1, 2)),
        "w0a": a(np.asarray(L0_gnn_W1).T), "w0b": a(np.asarray(L0_gnn_W2).T),
        "gamma_c": columns(L0_gnn_gamma), "b0a": row(L0_gnn_b1), "beta_c": columns(L0_gnn_beta), "b0b": row(L0_gnn_b2),
        "w1_0": a(L1_gnn_W1), "w1_1": a(L1_gnn_W2), "w1_2": a(L1_gnn_W3),
        "b1_0": row(L1_gnn_b1), "b1_1": row(L1_gnn_b2), "b1_2": row(L1_gnn_b3),
        "wv_t": a(np.asarray(L2_gnn_Wv).T), "bv_c": columns(L2_gnn_bv), "aw_c": columns(L2_gnn_aw),
        "ab": row(L2_gnn_ab), "wk": a(L2_gnn_Wk), "bk": a(L2_gnn_bk),
        "w3_t": a(np.asarray(L3_gnn_W).T),
    }
    nc = bacc.Bacc("TRN2", target_bir_lowering=False, num_devices=1)
    ins = {k: nc.dram_tensor(k, v.shape, mybir.dt.from_np(v.dtype), kind="ExternalInput").ap() for k, v in arrays.items()}
    out = nc.dram_tensor("out", arrays["x"].shape, F32, kind="ExternalOutput").ap()
    graph_stack(nc, ins["x"], ins["adj"], ins["adj_t"], ins["w0a"], ins["w0b"], ins["gamma_c"], ins["b0a"],
                ins["beta_c"], ins["b0b"], [ins[f"w1_{c}"] for c in range(3)], [ins[f"b1_{c}"] for c in range(3)],
                ins["wv_t"], ins["bv_c"], ins["aw_c"], ins["ab"], ins["wk"], ins["bk"], ins["w3_t"], out)
    r = run_bass_kernel_spmd(nc, [arrays], core_ids=[0])
    return r.results[0]["out"].reshape(x.shape)
```

```python
from contextlib import ExitStack

import numpy as np

import concourse.bass as bass
from concourse import mybir

P = 128
SLOTS = 4
F32 = mybir.dt.float32
F32R = mybir.dt.float32r
ALU = mybir.AluOpType
ACT = mybir.ActivationFunctionType
AX_X = mybir.AxisListType.X
EPS_LN = 1e-5
EPS_ALPHA = 1e-12
EPS_DEG = 1e-6
LEAK = 0.2


def order_hyper():
    return [
        ("lin1", 0), ("residb", 0), ("resid", 0), ("resid", 1), ("resid", 2), ("stats_n", 0), ("mid", 0), ("adj0", 3),
        ("hprep_n", 0), ("midnorm", 0), ("residb", 1), ("adj0hi", 3), ("midsplit", 0), ("lin1", 1), ("mid", 1),
        ("lin1", 2), ("hprep_n", 1), ("midnorm", 1), ("midsplit", 1), ("mid", 2), ("rowb", 0), ("adja", 0),
        ("midsplit", 2), ("hprep_n", 2), ("midnorm", 2), ("rowb", 1), ("lin1", 3), ("hprep_n", 3), ("adja", 1),
        ("resid", 3), ("adjahi", 0), ("adjb", 0), ("mid", 3), ("adjb", 1), ("adjahi", 1), ("midnorm", 3), ("adja", 2),
        ("rowb", 2), ("adjbhi", 0), ("norm_n", 0), ("lina", 0), ("lina", 1), ("midsplit", 3), ("adjahi", 2),
        ("binc_n", 0), ("binc_n", 1), ("binc_n", 2), ("stats_n", 1), ("split_n", 0), ("adjb", 2), ("adja", 3),
        ("stats_n", 2), ("rowb", 3), ("linb", 0), ("norm_n", 1), ("lina", 2), ("adjbhi", 1), ("hyp_n", 0),
        ("adjbhi", 2), ("stats_n", 3), ("hyp_n", 1), ("adjahi", 3), ("adjb", 3), ("linb", 1), ("split_n", 1),
        ("adj0_n", 0), ("norm_n", 2), ("split_n", 2), ("lina", 3), ("adjbhi", 3), ("norm_n", 3), ("hyp_n", 2),
        ("adj0_n", 1), ("binc_n", 3), ("residb", 2), ("adj0hi_n", 0), ("linb", 2), ("split_n", 3), ("residb", 3),
        ("linb", 3), ("adj0hi_n", 1), ("hyp_n", 3), ("adj0_n", 2), ("adj0hi_n", 2), ("deg_n", 0),
    ]


def order_gcn():
    return [
        ("lin0", 0), ("resid", 0), ("adj0", 3), ("resid", 1), ("lin0hi", 0), ("adj0hi", 3), ("lin0", 1),
        ("lin0hi", 1), ("adj1", 0), ("lin0", 2), ("adj1hi", 0), ("adj1", 1), ("lin0hi", 2), ("adj1hi", 1),
        ("lin0", 3), ("stats_n", 0), ("lin0hi", 3), ("adj1", 2), ("resid", 2), ("lin1", 0), ("lin1hi", 0),
        ("adj1", 3), ("adj1hi", 2), ("lin1", 1), ("resid", 3), ("adj1hi", 3), ("lin1hi", 1), ("stats_n", 1),
        ("adj2", 0), ("lin1", 2), ("stats_n", 2), ("adj2hi", 0), ("lin1hi", 2), ("adj2", 1), ("adj2hi", 1),
        ("asplit_n", 0), ("stats_n", 3), ("norm_n", 0), ("lin1", 3), ("split_n", 0), ("lin1hi", 3), ("adj2", 2),
        ("adj2hi", 2), ("lin2", 0), ("norm_n", 1), ("norm_n", 2), ("asplit_n", 1), ("asplit_n", 2), ("adj2", 3),
        ("split_n", 1), ("split_n", 2), ("adj2hi", 3), ("lin2", 1), ("norm_n", 3), ("lin2", 2), ("adj0_n", 0),
        ("adj0_n", 1), ("adj0hi_n", 0), ("asplit_n", 3), ("adj0hi_n", 1), ("adj0_n", 2), ("split_n", 3),
        ("adj0hi_n", 2), ("lin2", 3),
    ]


def order_diffuse():
    return [
        ("lin2", 0), ("tr", 3), ("sj", 0), ("diag", 3), ("resid", 0), ("alpha", 0), ("sj", 1), ("alpha", 1),
        ("lin2", 1), ("lin2", 2), ("tt", 0), ("resid", 1), ("sj", 2), ("alpha", 2), ("lin2", 3), ("tt", 1), ("sj", 3),
        ("alpha", 3), ("lin1", 0), ("stats_n", 0), ("resid", 2), ("norm_n", 0), ("tt", 2), ("adj1", 0), ("lin0", 0),
        ("score_n", 0), ("lin1", 1), ("adj1", 1), ("lin1", 2), ("stats_n", 1), ("adj0", 0), ("lin0", 1),
        ("stats_n", 2), ("resid", 3), ("tt", 3), ("adj1", 2), ("tr_n", 0), ("norm_n", 1), ("lin1", 3), ("score_n", 1),
        ("norm_n", 2), ("lin0", 2), ("diag_n", 0), ("stats_n", 3), ("score_n", 2), ("adj0", 1), ("adj1", 3),
        ("tr_n", 1), ("diag_n", 1), ("adj0", 2), ("norm_n", 3), ("lin0", 3), ("tr_n", 2), ("score_n", 3), ("adj0", 3),
        ("diag_n", 2),
    ]


def order_mean():
    return [
        ("asplit", 0), ("resid", 0), ("wb", 0), ("asplit", 1), ("wa", 0), ("asplit", 2), ("tr", 3), ("stats_n", 0),
        ("asplit", 3), ("resid", 1), ("wb", 1), ("ag", 0), ("norm_n", 0), ("wb", 2), ("wb", 3), ("wa", 1),
        ("resid", 2), ("stats_n", 1), ("stats_n", 2), ("ag", 1), ("norm_n", 1), ("norm_n", 2), ("resid", 3),
        ("wa", 2), ("ag", 2), ("tr_n", 0), ("tr_n", 1), ("stats_n", 3), ("wa", 3), ("ag", 3), ("tr_n", 2),
        ("norm_n", 3),
    ]


ORDERS = [order_hyper(), order_gcn(), order_diffuse(), order_mean()]
RENAMED = [{"hprep_n": None, "binc_n": None, "hyp_n": None, "deg_n": None}, {"asplit_n": None, "split_n": None, "adj0_n": "tr_n", "adj0hi_n": "diag_n"}, {"score_n": None, "diag_n": None},
           {"stats_n": None, "norm_n": None, "tr_n": None}]
LAST = [[(ren.get(name, name), t) for name, t in order if ren.get(name, name)] for order, ren in zip(ORDERS, RENAMED)]
LAST[1] = [step for name, t in LAST[1] for step in ([("score_n", t)] if name == "diag_n" else []) + [(name, t)]]
LAST[1].append(("score_n", SLOTS - 1))
LAST[0] = [step for name, t in LAST[0] for step in ([("asplit_n", t)] if name == "split_n" else []) + [(name, t)]]
SPLIT_AFTER = [
    [("lin1", 1), ("lin1", 2), ("lin1", 3), ("adja", 0), ("adja", 1), ("adjb", 0), ("adjb", 1), ("adja", 2),
     ("adja", 3), ("adjb", 2), ("adjb", 3), ("linb", 2)],
    [(f"lin{c}", t) for c in range(3) for t in range(SLOTS)],
    [(f"lin{c}", t) for c in (2, 1) for t in range(SLOTS)],
    [],
]
PLACE = [[0, 1, 2, 3], [4, 5, 0], [3, 2, 1], [4, 5]]
RAW = 4


def graph_stack(nc, x, adj, adj_t, w0a, w0b, gamma_c, b0a, beta_c, b0b, w1, b1, wv_t, bv_c, aw_c, ab, wk, bk, w3_t, out):
    rows, F = x.shape
    N = adj.shape[1]
    HID = w0a.shape[1]
    TILES = rows // P
    GROUPS = TILES // SLOTS
    KB = F // P
    assert 2 * N == P and HID == 2 * F and F == 512 and TILES % SLOTS == 0

    with ExitStack() as ctx:
        def sb(name, shape, dt=F32):
            return ctx.enter_context(nc.sbuf_tensor(name, shape, dt))

        def sem(name):
            return ctx.enter_context(nc.semaphore(name))

        def sems(prefix, names):
            return {k: sem(prefix + k) for k in names.split()}

        w_hi = sb("w_hi", [P, 6, KB, F], F32R)
        w_lo = sb("w_lo", [P, 6, KB, F], F32R)
        raw = sb("raw", [P, RAW, F])
        x_in = sb("x_in", [P, SLOTS, F])
        x_res = sb("x_res", [P, SLOTS, F])
        normed = sb("normed", [P, SLOTS, F])
        wide = sb("wide", [P, SLOTS, HID])
        row_hi = sb("row_hi", [P, SLOTS, F], F32R)
        row_lo = sb("row_lo", [P, SLOTS, F], F32R)
        col_hi = sb("col_hi", [P, SLOTS, F], F32R)
        col_lo = sb("col_lo", [P, SLOTS, F], F32R)
        adj_in = sb("adj_in", [P, SLOTS, P])
        adj_both = sb("adj_both", [P, SLOTS, 2, P], F32R)
        adj_hi, adj_lo = adj_both[:, :, 0, :], adj_both[:, :, 1, :]
        inc_t = sb("inc_t", [P, SLOTS, P], F32R)
        binc_w = sb("binc_w", [P, SLOTS, P + 2], F32R)
        binc_hi, w_r = binc_w[:, :, 0:P], binc_w[:, :, P:P + 2]
        binc_lo = sb("binc_lo", [P, SLOTS, P], F32R)
        b0a_bc = sb("b0a_bc", [P, 2, F])
        b0b_bc = sb("b0b_bc", [P, F])
        beta_bc = sb("beta_bc", [P, F])
        b1_bc = sb("b1_bc", [P, F])
        vj_bc = sb("vj_bc", [P, F])
        vi_bc = sb("vi_bc", [P, F])
        bk_bc = sb("bk_bc", [P, F])
        ident = sb("ident", [P, P])
        ones = sb("ones", [P, P])
        block_ones = sb("block_ones", [P, P], F32R)
        aw_sum = sb("aw_sum", [P, KB])
        spread = sb("spread", [P, 2, P])
        cols = sb("cols", [P, 29])
        gamma_col, beta_col = cols[:, 0:8], cols[:, 8:16]
        bv_col, aw_col, ab_col = cols[:, 16:20], cols[:, 20:28], cols[:, 28:29]
        consts = sb("consts", [P, 4])
        eps_ln = sb("eps_ln", [P, 1])
        half_neg, c_bias, cj_tmp = consts[:, 0:1], consts[:, 1:2], consts[:, 2:3]
        stats = sb("stats", [P, SLOTS, 12])
        moments = sb("moments", [P, SLOTS, 2])
        var_eps = sb("var_eps", [P, SLOTS])
        rstd = sb("rstd", [P, SLOTS])
        stats2 = sb("stats2", [P, SLOTS, 12])
        moments2 = sb("moments2", [P, SLOTS, 2])
        var_eps2 = sb("var_eps2", [P, SLOTS])
        rstd2 = sb("rstd2", [P, SLOTS])
        size = sb("size", [P, 4, SLOTS])
        w_sum = sb("w_sum", [P, SLOTS])
        size_r = sb("size_r", [P, 2, SLOTS], F32R)
        deg = sb("deg", [P, 8, SLOTS])
        D_SUM, D_POS, D_ZERO, D_SAFE, D_INV, D_OUT, M_SUM, DM_SUM = range(8)
        score = sb("score", [P, 6, SLOTS])
        S_J, S_I, S_IB, S_SUM, S_EPS, S_INV = range(6)
        ps = ctx.enter_context(nc.psum_tensor("ps", [P, SLOTS, 2, F], F32))

        def edge(t):
            return wide[:, t, F:F + P]

        diag_hi, diag_lo = inc_t, binc_lo

        def halves(t):
            both = ps[:, t, :, :].rearrange("p a (k h n) -> p (a k) h n", h=2, n=P)
            return both[:, :, 0, :], both[:, :, 1, :]

        def blocks(ap):
            return ap.rearrange("p (k n) -> p k n", n=P)

        def f32(ap):
            return ap.bitcast(F32)

        x_loaded = [sem(f"x_loaded{t}") for t in range(SLOTS)]
        x_stored = [sem(f"x_stored{t}") for t in range(SLOTS)]
        raw_loaded = [sem(f"raw_loaded{i}") for i in range(RAW)]
        s = sems("", "adj_loaded rows_loaded stats moments var_eps rstd norm relu resid split_hi split_lo "
                     "final raw_hi raw_lo raw_lo_v raw_scaled cols_loaded vec_loaded b1_loaded pool_const ready spread "
                     "spread_used vec_const vec_out aw_sum const_cols const_sum bk_loaded bk_sum")
        s0 = sems("l0_", "inc w_sum w_hi w_lo size binc hyp m_hi d_sum degree "
                         "dm_sum adj0 adj0_rest adj0_sum adj0_hi adj0_lo lin1 affine relu2 stats2 moments2 var_eps2 rstd2 "
                         "norm2 rowa_hi rowa_lo adja adja_rest adja_sum adja_hi adja_lo rowb_hi rowb_lo lina adjb adjb_rest adjb_sum adjb_hi adjb_lo linb "
                         "res_b res_beta")
        s1 = sems("l1_", "asplit_hi asplit_lo " + " ".join(
            f"adj{c} adj{c}_rest adj{c}_sum adj{c}_hi adj{c}_lo lin{c} bias{c} row{c}_hi row{c}_lo" for c in range(3)))
        s2 = sems("l2_", "s_j s_i s_ib diag tr tr_hi tr_lo lin2 row2_hi row2_lo sj score leak exp alpha s_eps s_inv trans "
                         "tt tt_hi tt_lo adj1 row1_hi row1_lo adj0 biased")
        s3 = sems("l3_", "asplit_hi asplit_lo deg deg_max deg_inv tr tr_hi tr_lo wb row_hi row_lo wa ag scaled summed")

        def n(g, t):
            return g * SLOTS + t + 1

        def nl(layer, g, t):
            return g * SLOTS + (layer * TILES + t + 1)

        def target(layer, g, name):
            if not name.endswith("_n"):
                return layer, g
            return (layer + 1, 0) if isinstance(g, int) and g + 1 == GROUPS else (layer, g + 1)

        def first(g):
            return isinstance(g, int) and g == 0

        FULL = GROUPS - 1

        scores_blocks = [wv_t[k * P:(k + 1) * P, :] for k in range(KB)]
        layer_blocks = [
            [(PLACE[0][u], k, w0a[k * P:(k + 1) * P, u * F:(u + 1) * F]) for u in range(2) for k in range(KB)]
            + [(PLACE[0][2 + u], k, w0b[(u * KB + k) * P:(u * KB + k + 1) * P, :]) for u in range(2) for k in range(KB)],
            [(PLACE[1][c], k, w1[c][k * P:(k + 1) * P, :]) for c in range(3) for k in range(KB)],
            [(PLACE[2][c], k, wk[c, k * P:(k + 1) * P, :]) for c in (2, 1, 0) for k in range(KB)],
            [(PLACE[3][u], k, w3_t[(u * KB + k) * P:(u * KB + k + 1) * P, :]) for u in (1, 0) for k in range(KB)],
        ]
        split_blocks = [b for blocks in layer_blocks for b in blocks]
        block_end = [sum(len(b) for b in layer_blocks[:layer + 1]) for layer in range(4)]
        BETA0 = 2 * KB


        def loads(b):
            return b if b < BETA0 else b + KB

        def wait_split(eng, blocks):
            by_vector = min(blocks, block_end[0]) // 2
            eng.wait_ge(s["raw_lo"], blocks - by_vector)
            if by_vector:
                eng.wait_ge(s["raw_lo_v"], by_vector)

        def start_block(eng, q):
            before = q - RAW
            if BETA0 <= before < BETA0 + KB:
                eng.wait_ge(s["spread_used"], 2 * (before - BETA0) + 2)
            elif before >= 0:
                wait_split(eng, (before if before < BETA0 else before - KB) + 1)
            if BETA0 <= q < BETA0 + KB:
                src = scores_blocks[q - BETA0]
            else:
                src = split_blocks[q if q < BETA0 else q - KB][2]
            eng.dma_start(raw[:, q % RAW, :], src).then_inc(raw_loaded[q % RAW], 16)

        def wait_block(eng, q):
            eng.wait_ge(raw_loaded[q % RAW], 16 * (q // RAW + 1))

        block = ctx.enter_context(nc.Block())

        def groups(eng, layer, body):
            body(layer, 0, ORDERS[layer])
            with eng.Fori(1, GROUPS - 1) as g:
                body(layer, g, ORDERS[layer])
            body(layer, GROUPS - 1, LAST[layer])

        x_tiles = x.rearrange("(n p) f -> n p f", p=P)
        out_tiles = out.rearrange("(n p) f -> n p f", p=P)
        adj_rows = adj.rearrange("(n h) i j -> h i n j", h=2)
        adj_cols = adj_t.rearrange("(n h) j i -> h j n i", h=2)

        @block.sync
        def _(sp):
            def load_x(layer, g, t):
                if layer > 0 or not first(g):
                    sp.wait_ge(s["resid"], nl(layer, g, t) - SLOTS)
                if layer > 0:
                    sp.wait_ge(x_stored[t], 16 * ((layer - 1) * GROUPS + 1) + 16 * g)
                src = (x_tiles if layer == 0 else out_tiles)[bass.ds(g * SLOTS + t, 1)]
                sp.dma_start(x_in[:, t, :], src.rearrange("n p f -> p (n f)")).then_inc(x_loaded[t], 16)

            def load_adj(layer, g):
                before = layer - 1 if first(g) else layer
                if before >= 0:
                    groups_before = GROUPS if first(g) else g
                    if before == 0:
                        sp.wait_ge(s0["w_sum"], groups_before)
                    else:
                        used = {1: s1["asplit_lo"], 2: s2["alpha"], 3: s3["asplit_lo"]}[before]
                        sp.wait_ge(used, groups_before * SLOTS)
                src = adj_rows if layer == 2 else adj_cols
                for h in range(2):
                    sp.dma_start(adj_in[h * N:(h + 1) * N, :, h * N:(h + 1) * N],
                                 src[h, :, bass.ds(g * SLOTS, SLOTS), :]).then_inc(s["adj_loaded"], 16)
                if layer == 3:
                    sp.wait_ge(s2["tt"] if first(g) else s3["deg"], TILES if first(g) else g * SLOTS)
                    for h in range(2):
                        sp.dma_start(wide[h * N:(h + 1) * N, :, F + h * N:F + (h + 1) * N],
                                     adj_rows[h, :, bass.ds(g * SLOTS, SLOTS), :]).then_inc(s["rows_loaded"], 16)

            def store_x(layer, g, t):
                sp.wait_ge(s["final"], nl(layer, g, t))
                sp.dma_start(out_tiles[bass.ds(g * SLOTS + t, 1)].rearrange("n p f -> p (n f)"), x_res[:, t, :]
                             ).then_inc(x_stored[t], 16)

            sp.wait_ge(s["ready"], 1)
            load_adj(0, 0)
            for t in range(SLOTS):
                load_x(0, 0, t)
                start_block(sp, t)
            for a, b, v in ((0, 8, gamma_c), (8, 16, beta_c), (16, 20, bv_c), (20, 28, aw_c)):
                sp.dma_start(cols[:, a:b], v).then_inc(s["cols_loaded"], 16)
            sp.dma_start(ab_col, ab.to_broadcast([P, 1])).then_inc(s["cols_loaded"], 16)
            for q in range(SLOTS, BETA0 + KB):
                start_block(sp, q)
            for q in range(BETA0 + KB, KB + block_end[0]):
                start_block(sp, q)
            for c in range(3):
                sp.dma_start(x_res[:, c, :], bk[c:c + 1, :].to_broadcast([P, F])).then_inc(s["bk_loaded"], 16)
            for u in range(2):
                sp.dma_start(b0a_bc[:, u, :], b0a[:, u * F:(u + 1) * F].to_broadcast([P, F])).then_inc(s["vec_loaded"], 16)
            sp.dma_start(b0b_bc[:], b0b.to_broadcast([P, F])).then_inc(s["vec_loaded"], 16)
            sp.dma_start(b1_bc[:], b1[2].to_broadcast([P, F])).then_inc(s["vec_loaded"], 16)

            def body(layer, g, order):
                nxt = target(layer, g, "_n")
                if nxt[0] < 4 and nxt[0] < 2:
                    load_adj(*nxt)
                if nxt[0] < 4:
                    for t in range(SLOTS):
                        load_x(*nxt, t)
                if nxt[0] in (2, 3):
                    load_adj(*nxt)
                for t in range(SLOTS):
                    store_x(layer, g, t)
            for layer in range(4):
                groups(sp, layer, body)
            for t in range(SLOTS):
                sp.wait_ge(x_stored[t], 16 * 4 * GROUPS)

        @block.tensor
        def _(pe):
            def product(out_ap, lhs_hi, lhs_lo, rhs_hi, rhs_lo, start=True, stop=True):
                nc.tensor.matmul(out_ap, lhs_hi, rhs_hi, start=start, stop=False)
                nc.tensor.matmul(out_ap, lhs_hi, rhs_lo, start=False, stop=False)
                return nc.tensor.matmul(out_ap, lhs_lo, rhs_hi, start=False, stop=stop)

            def linear(bank, t, place, start=True, stop=True):
                for k in range(KB):
                    last = product(ps[:, t, bank, :], col_hi[:, t, k * P:(k + 1) * P], col_lo[:, t, k * P:(k + 1) * P],
                                   w_hi[:, place, k, :], w_lo[:, place, k, :],
                                   start=start and k == 0, stop=stop and k == KB - 1)
                return last

            def mix_transposed(t):
                for k in range(KB):
                    at = ps[:, t, k // 2, (k % 2) * 2 * P:(k % 2 + 1) * 2 * P]
                    nc.tensor.matmul(at, row_hi[:, t, k * P:(k + 1) * P],
                                     adj_both[:, t, :, :].rearrange("p h n -> p (h n)"), start=True, stop=False)
                    last = nc.tensor.matmul(at[:, 0:P], row_lo[:, t, k * P:(k + 1) * P], adj_hi[:, t, :],
                                            start=False, stop=True)
                return last

            def mix(bank, t, start=True):
                return product(ps[:, t, bank, :], adj_hi[:, t, :], adj_lo[:, t, :], row_hi[:, t, :], row_lo[:, t, :],
                               start=start)

            def transposes(t):
                for k in range(KB):
                    last = nc.tensor.transpose(ps[:, t, 0, k * P:(k + 1) * P], normed[:, t, k * P:(k + 1) * P], ident[:])
                return last

            def hyper(g, name, t, i):
                if name == "hyp":
                    pe.wait_ge(s0["binc"], i)
                    if not first(g):
                        pe.wait_ge(s0["adjb_lo"], i - SLOTS)
                    nc.tensor.matmul(ps[:, t, 0, 0:P + 2], inc_t[:, t, :], binc_w[:, t, :], start=True, stop=False)
                    nc.tensor.matmul(ps[:, t, 0, 0:P], inc_t[:, t, :], binc_lo[:, t, :], start=False, stop=True
                                     ).then_inc(s0["hyp"], 1)
                if name == "adj0":
                    pe.wait_ge(s0["d_sum"], i)
                    pe.wait_ge(s["split_lo"], nl(0, g, t))
                    if not first(g):
                        pe.wait_ge(s["final"], i - SLOTS)
                    mix_transposed(t).then_inc(s0["adj0"], 1)
                if name == "lin1":
                    pe.wait_ge(s0["adj0_lo"], i)
                    if first(g):
                        wait_split(pe, BETA0)
                    linear(0, t, PLACE[0][0])
                    linear(1, t, PLACE[0][1]).then_inc(s0["lin1"], 1)
                if name == "adja":
                    pe.wait_ge(s0["rowa_lo"], i)
                    mix_transposed(t).then_inc(s0["adja"], 1)
                if name == "lina":
                    pe.wait_ge(s0["adja_lo"], i)
                    pe.wait_ge(s0["adjb_sum"], i)
                    if first(g):
                        wait_split(pe, block_end[0])
                    linear(1, t, PLACE[0][2], stop=False).then_inc(s0["lina"], 1)
                if name == "adjb":
                    pe.wait_ge(s0["rowb_lo"], i)
                    pe.wait_ge(s0["adja_sum"], i)
                    mix_transposed(t).then_inc(s0["adjb"], 1)
                if name == "linb":
                    pe.wait_ge(s0["adjb_lo"], i)
                    linear(1, t, PLACE[0][3], start=False).then_inc(s0["linb"], 1)

            def gcn(g, name, t, i):
                c = int(name[3])
                if name == "adj0":
                    pe.wait_ge(s["split_lo"], nl(1, g, t))
                    pe.wait_ge(s1["asplit_lo"], i)
                    pe.wait_ge(s["final"], nl(1, g, t) - SLOTS)
                    if first(g):
                        pe.wait_ge(s0["adjb_lo"], n(FULL, t))
                elif name in ("adj1", "adj2"):
                    pe.wait_ge(s1[f"row{c - 1}_lo"], i)
                if name.startswith("adj"):
                    mix_transposed(t).then_inc(s1[name], 1)
                else:
                    pe.wait_ge(s1[f"adj{c}_lo"], i)
                    if c == 0 and first(g):
                        wait_split(pe, block_end[1])
                    linear(1, t, PLACE[1][c]).then_inc(s1[name], 1)

            def diffuse(g, name, t, i):
                if name == "tr":
                    pe.wait_ge(s["norm"], nl(2, g, t))
                    if first(g):
                        pe.wait_ge(s1["adj2_lo"], n(FULL, t))
                    transposes(t).then_inc(s2["tr"], 1)
                if name == "lin2":
                    pe.wait_ge(s2["tr_lo"], i)
                    pe.wait_ge(s["final"], nl(2, g, t) - SLOTS)
                    if first(g):
                        wait_split(pe, block_end[2])
                    linear(1, t, PLACE[2][2]).then_inc(s2["lin2"], 1)
                if name == "sj":
                    pe.wait_ge(s2["s_ib"], i)
                    nc.tensor.matmul(ps[:, t, 0, 0:P], block_ones[:], diag_hi[:, t, :], start=True, stop=False)
                    nc.tensor.matmul(ps[:, t, 0, 0:P], block_ones[:], diag_lo[:, t, :], start=False, stop=True
                                     ).then_inc(s2["sj"], 1)
                if name == "tt":
                    pe.wait_ge(s2["trans"], i)
                    nc.tensor.transpose(ps[:, t, 0, 0:P], edge(t), ident[:]).then_inc(s2["tt"], 1)
                if name == "lin1":
                    pe.wait_ge(s2["tt_lo"], i)
                    linear(0, t, PLACE[2][1], stop=False)
                if name == "adj1":
                    pe.wait_ge(s2["row2_lo"], i)
                    mix(0, t, start=False).then_inc(s2["adj1"], 1)
                if name == "lin0":
                    linear(1, t, PLACE[2][0], stop=False)
                if name == "adj0":
                    pe.wait_ge(s2["row1_lo"], i)
                    mix(1, t, start=False).then_inc(s2["adj0"], 1)

            def mean(g, name, t, i):
                if name == "tr":
                    pe.wait_ge(s["norm"], nl(3, g, t))
                    if not first(g):
                        pe.wait_ge(s3["summed"], i - SLOTS)
                    transposes(t).then_inc(s3["tr"], 1)
                if name == "wb":
                    pe.wait_ge(s3["tr_lo"], i)
                    pe.wait_ge(s["final"], nl(3, g, t) - SLOTS)
                    if first(g):
                        wait_split(pe, block_end[3])
                    linear(1, t, PLACE[3][1]).then_inc(s3["wb"], 1)
                if name == "wa":
                    linear(0, t, PLACE[3][0])
                if name == "ag":
                    pe.wait_ge(s3["row_lo"], i)
                    pe.wait_ge(s3["asplit_lo"], i)
                    mix(1, t).then_inc(s3["ag"], 1)

            WORK = [(hyper, ("hyp", "adj0", "lin1", "adja", "lina", "adjb", "linb")),
                    (gcn, ("adj0", "adj1", "adj2", "lin0", "lin1", "lin2")),
                    (diffuse, ("tr", "lin2", "sj", "tt", "lin1", "adj1", "lin0", "adj0")),
                    (mean, ("tr", "wb", "wa", "ag"))]

            def body(layer, g, order):
                for name, t in order:
                    L, G = target(layer, g, name)
                    work, names = WORK[L]
                    if name.removesuffix("_n") in names:
                        work(G, name.removesuffix("_n"), t, n(G, t))

            for t in range(SLOTS):
                hyper(0, "hyp", t, n(0, t))
            pe.wait_ge(s["const_cols"], 1)
            nc.tensor.matmul(ps[:, 3, 1, 0:1], ones[:], cj_tmp, start=True, stop=True).then_inc(s["const_sum"], 1)
            for t in range(SLOTS - 1):
                hyper(0, "adj0", t, n(0, t))
            pe.wait_ge(s["vec_const"], 1)
            pe.wait_ge(s0["d_sum"], SLOTS)
            for b in range(KB):
                wait_block(pe, BETA0 + b)
                for h in range(2):
                    pe.wait_ge(s["spread"], 2 * b + h + 1)
                    nc.tensor.matmul(ps[:, 3, h, :], spread[:, h, :], raw[:, (BETA0 + b) % RAW, :],
                                     start=b == 0, stop=b == KB - 1).then_inc(s["spread_used"], 1)
            pe.wait_ge(s["vec_out"], 1)
            for j in range(2 * KB):
                q = BETA0 + KB + j
                wait_block(pe, q)
                pe.wait_ge(s["spread"], 2 * KB + j + 1)
                nc.tensor.matmul(ps[:, 3, 1, :], spread[:, j % 2, :], raw[:, q % RAW, :],
                                 start=j == 0, stop=j == 2 * KB - 1).then_inc(s["spread_used"], 1)
            pe.wait_ge(s["vec_out"], 2)
            for layer in range(4):
                groups(pe, layer, body)

        @block.scalar
        def _(act):
            def relu(out_ap, in_ap):
                return nc.scalar.activation(out_ap, in_ap, ACT.Relu)

            def copy(out_ap, in_ap):
                return nc.scalar.activation(out_ap, in_ap, ACT.Copy)

            def split_weights(b):
                place, k, _ = split_blocks[b]
                if BETA0 <= b < block_end[0]:
                    act.wait_ge(s["raw_scaled"], b - BETA0 + 1)
                else:
                    wait_block(act, loads(b))
                copy(w_hi[:, place, k, :], raw[:, loads(b) % RAW, :]).then_inc(s["raw_hi"], 1)

            def split(layer, g, t):
                act.wait_ge(s["norm"], nl(layer, g, t))
                relu(normed[:, t, :], normed[:, t, :]).then_inc(s["relu"], 1)
                act.wait_ge(s["relu"], nl(layer, g, t))
                if layer == 0 and not first(g):
                    act.wait_ge(s0["adjb"], n(g, t) - SLOTS)
                elif layer == 1 and first(g):
                    act.wait_ge(s0["adjb"], n(FULL, t))
                elif layer == 1:
                    act.wait_ge(s1["adj2"], n(g, t) - SLOTS)
                copy(row_hi[:, t, :], normed[:, t, :]).then_inc(s["split_hi"], 1)

            def hyper(g, name, t, i):
                if name == "split":
                    split(0, g, t)
                if name == "hyp":
                    act.wait_ge(s0["hyp"], i)
                    if not first(g):
                        act.wait_ge(s0["dm_sum"], g)
                    nc.scalar.activation(adj_hi[:, t, :], ps[:, t, 0, 0:P], ACT.Copy,
                                         accum_out=deg[:, M_SUM, t:t + 1]).then_inc(s0["m_hi"], 1)
                if name in ("adj0", "adja"):
                    act.wait_ge(s0[name], i)
                    if name == "adj0" and not first(g):
                        act.wait_ge(s0["adja_lo"], i - SLOTS)
                    copy(blocks(wide[:, t, 0:F]), halves(t)[1]).then_inc(s0[name + "_rest"], 1)
                if name in ("adj0hi", "adjahi"):
                    act.wait_ge(s0[name[:4] + "_sum"], i)
                    copy(col_hi[:, t, :], wide[:, t, 0:F]).then_inc(s0[name[:4] + "_hi"], 1)
                if name == "adjb":
                    act.wait_ge(s0["adjb"], i)
                    copy(blocks(wide[:, t, F:HID]), halves(t)[1]).then_inc(s0["adjb_rest"], 1)
                if name == "adjbhi":
                    act.wait_ge(s0["adjb_sum"], i)
                    act.wait_ge(s0["lina"], i)
                    copy(col_hi[:, t, :], wide[:, t, F:HID]).then_inc(s0["adjb_hi"], 1)
                if name == "lin1":
                    act.wait_ge(s0["affine"], i)
                    relu(wide[:, t, :], wide[:, t, :]).then_inc(s0["relu2"], 1)
                if name == "midsplit":
                    act.wait_ge(s0["norm2"], i)
                    copy(row_hi[:, t, :], wide[:, t, 0:F]).then_inc(s0["rowa_hi"], 1)
                if name == "rowb":
                    act.wait_ge(s0["adja"], i)
                    copy(row_hi[:, t, :], wide[:, t, F:HID]).then_inc(s0["rowb_hi"], 1)

            def gcn(g, name, t, i):
                if name == "split":
                    split(1, g, t)
                if name == "asplit":
                    act.wait_ge(s["adj_loaded"], 32 * (GROUPS + 1) + 32 * g)
                    if first(g):
                        act.wait_ge(s0["adjb"], n(FULL, t))
                    else:
                        act.wait_ge(s1["adj2"], i - SLOTS)
                    copy(adj_hi[:, t, :], adj_in[:, t, :]).then_inc(s1["asplit_hi"], 1)
                if name in ("adj0", "adj1", "adj2"):
                    act.wait_ge(s1[name], i)
                    copy(blocks(wide[:, t, F:HID]), halves(t)[1]).then_inc(s1[name + "_rest"], 1)
                if name in ("adj0hi", "adj1hi", "adj2hi"):
                    act.wait_ge(s1[name[:4] + "_sum"], i)
                    copy(col_hi[:, t, :], wide[:, t, F:HID]).then_inc(s1[name[:4] + "_hi"], 1)
                if name in ("lin0hi", "lin1hi"):
                    c = int(name[3])
                    act.wait_ge(s1[f"bias{c}"], i)
                    relu(row_hi[:, t, :], wide[:, t, 0:F]).then_inc(s1[f"row{c}_hi"], 1)

            def diffuse(g, name, t, i):
                if name == "tr":
                    act.wait_ge(s2["tr"], i)
                    relu(col_hi[:, t, :], ps[:, t, 0, :]).then_inc(s2["tr_hi"], 1)
                if name == "lin2":
                    act.wait_ge(s2["lin2"], i)
                    copy(row_hi[:, t, :], ps[:, t, 1, :]).then_inc(s2["row2_hi"], 1)
                if name == "sj":
                    act.wait_ge(s2["leak"], i)
                    nc.scalar.activation(edge(t), edge(t), ACT.Exp).then_inc(s2["exp"], 1)
                if name == "tt":
                    act.wait_ge(s2["tt"], i)
                    copy(adj_hi[:, t, :], ps[:, t, 0, 0:P]).then_inc(s2["tt_hi"], 1)
                if name == "adj1":
                    act.wait_ge(s2["adj1"], i)
                    copy(row_hi[:, t, :], ps[:, t, 0, :]).then_inc(s2["row1_hi"], 1)

            def mean(g, name, t, i):
                if name == "tr":
                    act.wait_ge(s3["tr"], i)
                    relu(col_hi[:, t, :], ps[:, t, 0, :]).then_inc(s3["tr_hi"], 1)
                if name == "wb":
                    act.wait_ge(s3["wb"], i)
                    copy(row_hi[:, t, :], ps[:, t, 1, :]).then_inc(s3["row_hi"], 1)
                if name == "asplit":
                    act.wait_ge(s["adj_loaded"], 32 * (3 * GROUPS + 1) + 32 * g)
                    if first(g):
                        act.wait_ge(s2["adj0"], n(FULL, t))
                    else:
                        act.wait_ge(s3["ag"], i - SLOTS)
                    copy(adj_hi[:, t, :], adj_in[:, t, :]).then_inc(s3["asplit_hi"], 1)

            WORK = [hyper, gcn, diffuse, mean]

            def body(layer, g, order):
                last = isinstance(g, int) and g == GROUPS - 1 and layer < 3
                b = block_end[layer]
                if last:
                    if layer == 1:
                        act.wait_ge(s0["linb"], TILES)
                    if layer == 2:
                        act.wait_ge(s1["lin1"], TILES)
                    start_block(act, loads(b))
                for name, t in order:
                    L, G = target(layer, g, name)
                    WORK[L](G, name.removesuffix("_n"), t, n(G, t))
                    if last and layer == 0 and (name, t) == ("mid", 3):
                        for c in range(2):
                            act.dma_start(b0a_bc[:, c, :], b1[c].to_broadcast([P, F])).then_inc(s["b1_loaded"], 16)
                    if last and (name, t) in SPLIT_AFTER[layer]:
                        if b + 1 < block_end[layer + 1]:
                            start_block(act, loads(b + 1))
                        split_weights(b)
                        b += 1

            for b in range(SLOTS):
                split_weights(b)
            for t in range(SLOTS):
                hyper(0, "split", t, n(0, t))
                hyper(0, "hyp", t, n(0, t))
                split_weights(SLOTS + t)
            for t in range(SLOTS - 1):
                hyper(0, "adj0", t, n(0, t))
                hyper(0, "adj0hi", t, n(0, t))
            for b in range(BETA0, block_end[0]):
                split_weights(b)
            for layer in range(4):
                groups(act, layer, body)

        @block.vector
        def _(dve):
            V = nc.vector

            def lo_of(out_ap, full, hi):
                return V.tensor_tensor(out_ap, full, f32(hi), ALU.subtract)

            def carry_wait():
                V.memset(consts[:, 3:4], 0.0)

            def statistics(layer, g, t):
                dve.wait_ge(x_loaded[t], 16 * (layer * GROUPS + 1) + 16 * g)
                V.bn_stats(stats[:, t, 0:6], x_in[:, t, :]).then_inc(s["stats"], 1)
                dve.wait_ge(s["stats"], nl(layer, g, t))
                carry_wait()
                V.bn_aggr(moments[:, t, :], stats[:, t, 0:6]).then_inc(s["moments"], 1)

            def normalise(layer, g, t):
                dve.wait_ge(s["rstd"], nl(layer, g, t))
                i = n(g, t)
                if layer == 0 and not first(g):
                    dve.wait_ge(s["resid"], i - SLOTS)
                if layer == 1 and first(g):
                    dve.wait_ge(s["resid"], n(FULL, t))
                if layer == 1 and not first(g) or layer == 2 and first(g):
                    dve.wait_ge(s["split_lo"], nl(layer, g, t) - SLOTS)
                if layer == 2 and not first(g):
                    dve.wait_ge(s2["tr"], i - SLOTS)
                if layer == 3:
                    dve.wait_ge(s2["tr"] if first(g) else s3["tr"], n(FULL, t) if first(g) else i - SLOTS)
                V.tensor_scalar(normed[:, t, :], x_in[:, t, :], moments[:, t, 0:1], rstd[:, t:t + 1],
                                ALU.subtract, ALU.mult).then_inc(s["norm"], 1)

            def hyper(g, name, t, i):
                if name == "stats":
                    statistics(0, g, t)
                if name == "norm":
                    normalise(0, g, t)
                if name == "hprep":
                    dve.wait_ge(s["adj_loaded"], 32 * (g + 1))
                    if not first(g):
                        dve.wait_ge(s0["hyp"], i - SLOTS)
                    V.tensor_scalar(inc_t[:, t, :], adj_in[:, t, :], 0.0, 0.0, ALU.not_equal, ALU.add,
                                    accum_out=size[:, 0, t:t + 1]).then_inc(s0["inc"], 1)
                if name == "hprep" and t == SLOTS - 1:
                    if not first(g):
                        dve.wait_ge(s0["hyp"], g * SLOTS)
                    V.tensor_tensor(w_sum[:], adj_in[:, :, 0], adj_in[:, :, N], ALU.add).then_inc(s0["w_sum"], 1)
                    dve.wait_ge(s0["inc"], i)
                    V.tensor_scalar_max(size[:, 1, :], size[:, 0, :], 1.0).then_inc(s0["size"], 1)
                    dve.wait_ge(s0["w_sum"], g + 1)
                    V.tensor_copy(w_r[:, :, 0], w_sum[:]).then_inc(s0["w_hi"], 1)
                    dve.wait_ge(s0["size"], 4 * g + 1)
                    V.reciprocal(size[:, 2, :], size[:, 1, :]).then_inc(s0["size"], 1)
                    dve.wait_ge(s0["w_hi"], g + 1)
                    lo_of(w_r[:, :, 1], w_sum[:], w_r[:, :, 0]).then_inc(s0["w_lo"], 1)
                    dve.wait_ge(s0["size"], 4 * g + 2)
                    V.tensor_copy(size_r[:, 0, :], size[:, 2, :]).then_inc(s0["size"], 1)
                    dve.wait_ge(s0["size"], 4 * g + 3)
                    lo_of(size_r[:, 1, :], size[:, 2, :], size_r[:, 0, :]).then_inc(s0["size"], 1)
                if name == "binc":
                    dve.wait_ge(s0["size"], 4 * g + 4)
                    V.tensor_scalar(binc_hi[:, t, :], f32(inc_t[:, t, :]), f32(size_r[:, 0, t:t + 1]), None, ALU.mult)
                    V.tensor_scalar(binc_lo[:, t, :], f32(inc_t[:, t, :]), f32(size_r[:, 1, t:t + 1]), None, ALU.mult
                                    ).then_inc(s0["binc"], 1)
                if name == "hyp":
                    dve.wait_ge(s0["m_hi"], i)
                    lo_of(adj_lo[:, t, :], ps[:, t, 0, 0:P], adj_hi[:, t, :])
                    V.reduce_sum(deg[:, D_SUM, t:t + 1], ps[:, t, 0, P:P + 2], AX_X).then_inc(s0["d_sum"], 1)
                if name == "deg":
                    dve.wait_ge(s0["d_sum"], (g + 1) * SLOTS)
                    V.tensor_scalar(deg[:, D_POS, :], deg[:, D_SUM, :], 0.0, None, ALU.is_gt).then_inc(s0["degree"], 1)
                    dve.wait_ge(s0["degree"], 5 * g + 1)
                    V.tensor_scalar(deg[:, D_ZERO, :], deg[:, D_POS, :], -1.0, 1.0, ALU.mult, ALU.add
                                    ).then_inc(s0["degree"], 1)
                    dve.wait_ge(s0["degree"], 5 * g + 2)
                    V.scalar_tensor_tensor(deg[:, D_SAFE, :], deg[:, D_SUM, :], 0.0, deg[:, D_ZERO, :],
                                           ALU.max, ALU.add).then_inc(s0["degree"], 1)
                    dve.wait_ge(s0["degree"], 5 * g + 3)
                    V.reciprocal(deg[:, D_INV, :], deg[:, D_SAFE, :]).then_inc(s0["degree"], 1)
                    dve.wait_ge(s0["degree"], 5 * g + 4)
                    V.tensor_tensor(deg[:, D_OUT, :], deg[:, D_INV, :], deg[:, D_POS, :], ALU.mult
                                    ).then_inc(s0["degree"], 1)
                    dve.wait_ge(s0["degree"], 5 * g + 5)
                    V.tensor_tensor(deg[:, DM_SUM, :], deg[:, D_OUT, :], deg[:, M_SUM, :], ALU.mult
                                    ).then_inc(s0["dm_sum"], 1)
                if name in ("adj0", "adja"):
                    dve.wait_ge(s0[name + "_rest"], i)
                    V.tensor_tensor(blocks(wide[:, t, 0:F]), halves(t)[0], blocks(wide[:, t, 0:F]), ALU.add).then_inc(s0[name + "_sum"], 1)
                if name in ("adj0hi", "adjahi"):
                    dve.wait_ge(s0[name[:4] + "_hi"], i)
                    lo_of(col_lo[:, t, :], wide[:, t, 0:F], col_hi[:, t, :]).then_inc(s0[name[:4] + "_lo"], 1)
                if name == "adjb":
                    dve.wait_ge(s0["adjb_rest"], i)
                    V.tensor_tensor(blocks(wide[:, t, F:HID]), halves(t)[0], blocks(wide[:, t, F:HID]), ALU.add
                                    ).then_inc(s0["adjb_sum"], 1)
                if name == "adjbhi":
                    dve.wait_ge(s0["adjb_hi"], i)
                    lo_of(col_lo[:, t, :], wide[:, t, F:HID], col_hi[:, t, :]).then_inc(s0["adjb_lo"], 1)
                if name == "lin1":
                    dve.wait_ge(s0["lin1"], i)
                    if first(g):
                        dve.wait_ge(s["vec_loaded"], 64)
                    else:
                        dve.wait_ge(s0["adjb_lo"], i - SLOTS)
                    V.scalar_tensor_tensor(wide[:, t, :], ps[:, t, :, :].rearrange("p a f -> p (a f)"),
                                           deg[:, D_OUT, t:t + 1], b0a_bc[:].rearrange("p a f -> p (a f)"),
                                           ALU.mult, ALU.add).then_inc(s0["affine"], 1)
                if name == "mid":
                    dve.wait_ge(s0["relu2"], i)
                    for h in range(2):
                        V.bn_stats(stats2[:, t, 6 * h:6 * h + 6], wide[:, t, h * F:(h + 1) * F]).then_inc(s0["stats2"], 1)
                    dve.wait_ge(s0["stats2"], 2 * i)
                    carry_wait()
                    V.bn_aggr(moments2[:, t, :], stats2[:, t, :]).then_inc(s0["moments2"], 1)
                if name == "midnorm":
                    dve.wait_ge(s0["rstd2"], i)
                    V.tensor_scalar(wide[:, t, :], wide[:, t, :], moments2[:, t, 0:1], rstd2[:, t:t + 1],
                                    ALU.subtract, ALU.mult).then_inc(s0["norm2"], 1)
                if name == "residb":
                    dve.wait_ge(s0["res_b"], i)
                    dve.wait_ge(s0["dm_sum"], g + 1)
                    V.scalar_tensor_tensor(x_res[:, t, :], beta_bc[:], deg[:, DM_SUM, t:t + 1], x_res[:, t, :],
                                           ALU.mult, ALU.add).then_inc(s0["res_beta"], 1)
                if name == "linb":
                    dve.wait_ge(s0["linb"], i)
                    dve.wait_ge(s0["res_beta"], i)
                    V.scalar_tensor_tensor(x_res[:, t, :], ps[:, t, 1, :], deg[:, D_OUT, t:t + 1], x_res[:, t, :],
                                           ALU.mult, ALU.add).then_inc(s["final"], 1)

            def gcn(g, name, t, i):
                if name == "stats":
                    statistics(1, g, t)
                if name == "norm":
                    normalise(1, g, t)
                if name in ("adj0", "adj1", "adj2"):
                    dve.wait_ge(s1[name + "_rest"], i)
                    V.tensor_tensor(blocks(wide[:, t, F:HID]), halves(t)[0], blocks(wide[:, t, F:HID]), ALU.add).then_inc(s1[name + "_sum"], 1)
                if name in ("lin0", "lin1"):
                    c = int(name[3])
                    dve.wait_ge(s1[name], i)
                    if c == 0 and first(g):
                        dve.wait_ge(s["b1_loaded"], 32)
                        dve.wait_ge(s0["rowb_lo"], n(FULL, t))
                    V.tensor_tensor(wide[:, t, 0:F], ps[:, t, 1, :], b0a_bc[:, c, :], ALU.add).then_inc(s1[f"bias{c}"], 1)
                if name in ("lin0hi", "lin1hi"):
                    c = int(name[3])
                    dve.wait_ge(s1[f"row{c}_hi"], i)
                    V.scalar_tensor_tensor(row_lo[:, t, :], wide[:, t, 0:F], 0.0, f32(row_hi[:, t, :]),
                                           ALU.max, ALU.subtract).then_inc(s1[f"row{c}_lo"], 1)
                if name == "lin2":
                    dve.wait_ge(s1[name], i)
                    dve.wait_ge(s["resid"], nl(1, g, t))
                    V.tensor_tensor(x_res[:, t, :], ps[:, t, 1, :], x_res[:, t, :], ALU.add).then_inc(s["final"], 1)

            def diffuse(g, name, t, i):
                if name == "stats":
                    statistics(2, g, t)
                if name == "norm":
                    normalise(2, g, t)
                if name == "score":
                    if first(g):
                        dve.wait_ge(s["final"], nl(2, g, t) - SLOTS)
                    dve.wait_ge(s["norm"], nl(2, g, t))
                    for v, at, done in ((vj_bc, S_J, "s_j"), (vi_bc, S_I, "s_i")):
                        V.scalar_tensor_tensor(wide[:, t, 0:F], normed[:, t, :], 0.0, v[:], ALU.max, ALU.mult,
                                               accum_out=score[:, at, t:t + 1]).then_inc(s2[done], 1)
                        dve.wait_ge(s2[done], i)
                if name == "tr":
                    dve.wait_ge(s2["tr_hi"], i)
                    V.scalar_tensor_tensor(col_lo[:, t, :], ps[:, t, 0, :], 0.0, f32(col_hi[:, t, :]),
                                           ALU.max, ALU.subtract).then_inc(s2["tr_lo"], 1)
                if name == "diag":
                    dve.wait_ge(s2["s_i"], i)
                    if not first(g):
                        dve.wait_ge(s2["sj"], i - SLOTS)
                    V.tensor_scalar(diag_hi[:, t, :], ident[:], score[:, S_J, t:t + 1], None, ALU.mult
                                    ).then_inc(s2["diag"], 1)
                    dve.wait_ge(s2["diag"], i)
                    V.scalar_tensor_tensor(diag_lo[:, t, :], ident[:], score[:, S_J, t:t + 1], f32(diag_hi[:, t, :]),
                                           ALU.mult, ALU.subtract)
                    V.tensor_tensor(score[:, S_IB, t:t + 1], score[:, S_I, t:t + 1], c_bias, ALU.add
                                    ).then_inc(s2["s_ib"], 1)
                if name == "lin2":
                    dve.wait_ge(s2["row2_hi"], i)
                    lo_of(row_lo[:, t, :], ps[:, t, 1, :], row_hi[:, t, :]).then_inc(s2["row2_lo"], 1)
                if name == "sj":
                    dve.wait_ge(s2["sj"], i)
                    dve.wait_ge(s2["s_ib"], i)
                    if not first(g):
                        dve.wait_ge(s2["tt"], i - SLOTS)
                    V.scalar_tensor_tensor(edge(t), ps[:, t, 0, 0:P], score[:, S_IB, t:t + 1], f32(block_ones[:]),
                                           ALU.add, ALU.mult).then_inc(s2["score"], 1)
                    dve.wait_ge(s2["score"], i)
                    V.scalar_tensor_tensor(edge(t), edge(t), LEAK, edge(t), ALU.mult, ALU.max).then_inc(s2["leak"], 1)
                if name == "alpha":
                    dve.wait_ge(s2["exp"], i)
                    dve.wait_ge(s["adj_loaded"], 32 * (2 * GROUPS + 1) + 32 * g)
                    V.scalar_tensor_tensor(edge(t), edge(t), 1.0, adj_in[:, t, :], ALU.mult, ALU.mult,
                                           accum_out=score[:, S_SUM, t:t + 1]).then_inc(s2["alpha"], 1)
                    dve.wait_ge(s2["alpha"], i)
                    V.tensor_scalar_add(score[:, S_EPS, t:t + 1], score[:, S_SUM, t:t + 1], EPS_ALPHA
                                        ).then_inc(s2["s_eps"], 1)
                    dve.wait_ge(s2["s_eps"], i)
                    V.reciprocal(score[:, S_INV, t:t + 1], score[:, S_EPS, t:t + 1]).then_inc(s2["s_inv"], 1)
                    dve.wait_ge(s2["s_inv"], i)
                    V.tensor_scalar(edge(t), edge(t), score[:, S_INV, t:t + 1], None, ALU.mult).then_inc(s2["trans"], 1)
                if name == "tt":
                    dve.wait_ge(s2["tt_hi"], i)
                    lo_of(adj_lo[:, t, :], ps[:, t, 0, 0:P], adj_hi[:, t, :]).then_inc(s2["tt_lo"], 1)
                if name == "adj1":
                    dve.wait_ge(s2["row1_hi"], i)
                    lo_of(row_lo[:, t, :], ps[:, t, 0, :], row_hi[:, t, :]).then_inc(s2["row1_lo"], 1)
                if name == "adj0":
                    dve.wait_ge(s2["adj0"], i)
                    V.tensor_tensor(wide[:, t, 0:F], ps[:, t, 1, :], bk_bc[:], ALU.add).then_inc(s2["biased"], 1)
                    dve.wait_ge(s2["biased"], i)
                    dve.wait_ge(s["resid"], nl(2, g, t))
                    V.scalar_tensor_tensor(x_res[:, t, :], wide[:, t, 0:F], 0.0, x_res[:, t, :], ALU.max, ALU.add
                                           ).then_inc(s["final"], 1)

            def mean(g, name, t, i):
                if name == "stats":
                    statistics(3, g, t)
                if name == "norm":
                    normalise(3, g, t)
                if name == "tr":
                    dve.wait_ge(s3["tr_hi"], i)
                    V.scalar_tensor_tensor(col_lo[:, t, :], ps[:, t, 0, :], 0.0, f32(col_hi[:, t, :]),
                                           ALU.max, ALU.subtract).then_inc(s3["tr_lo"], 1)
                if name == "wb":
                    dve.wait_ge(s3["row_hi"], i)
                    lo_of(row_lo[:, t, :], ps[:, t, 1, :], row_hi[:, t, :]).then_inc(s3["row_lo"], 1)
                if name == "asplit":
                    dve.wait_ge(s["rows_loaded"], 32 * (g + 1))
                    V.reduce_sum(deg[:, D_SUM, t:t + 1], edge(t), AX_X).then_inc(s3["deg"], 1)
                if name == "asplit" and t == SLOTS - 1:
                    dve.wait_ge(s3["deg"], i)
                    V.tensor_scalar_max(deg[:, D_SAFE, :], deg[:, D_SUM, :], EPS_DEG).then_inc(s3["deg_max"], 1)
                    dve.wait_ge(s3["deg_max"], g + 1)
                    V.reciprocal(deg[:, D_OUT, :], deg[:, D_SAFE, :]).then_inc(s3["deg_inv"], 1)
                if name == "ag":
                    dve.wait_ge(s3["ag"], i)
                    dve.wait_ge(s3["deg_inv"], g + 1)
                    V.tensor_scalar(wide[:, t, 0:F], ps[:, t, 1, :], deg[:, D_OUT, t:t + 1], None, ALU.mult
                                    ).then_inc(s3["scaled"], 1)
                    dve.wait_ge(s3["scaled"], i)
                    V.tensor_tensor(wide[:, t, 0:F], ps[:, t, 0, :], wide[:, t, 0:F], ALU.add).then_inc(s3["summed"], 1)
                    dve.wait_ge(s3["summed"], i)
                    dve.wait_ge(s["resid"], nl(3, g, t))
                    V.scalar_tensor_tensor(x_res[:, t, :], wide[:, t, 0:F], 0.0, x_res[:, t, :], ALU.max, ALU.add
                                           ).then_inc(s["final"], 1)

            WORK = [hyper, gcn, diffuse, mean]

            def body(layer, g, order):
                for name, t in order:
                    L, G = target(layer, g, name)
                    WORK[L](G, name.removesuffix("_n"), t, n(G, t))

            def split_weights(b):
                place, k, _ = split_blocks[b]
                dve.wait_ge(s["raw_hi"], b + 1)
                lo_of(w_lo[:, place, k, :], raw[:, loads(b) % RAW, :], w_hi[:, place, k, :]).then_inc(s["raw_lo_v"], 1)

            dve.wait_ge(s["ready"], 1)
            V.tensor_copy(block_ones[:], wide[:, 0, F:F + P])
            for t in range(SLOTS):
                hyper(0, "stats", t, n(0, t))
                hyper(0, "hprep", t, n(0, t))
            split_weights(1)
            for t in range(SLOTS):
                hyper(0, "binc", t, n(0, t))
            split_weights(3)
            for t in range(SLOTS):
                hyper(0, "norm", t, n(0, t))
            dve.wait_ge(s["cols_loaded"], 16 * 5)
            V.tensor_tensor(aw_sum[:], aw_col[:, 0:KB], aw_col[:, KB:2 * KB], ALU.add).then_inc(s["aw_sum"], 1)
            dve.wait_ge(s["aw_sum"], 1)
            V.scalar_tensor_tensor(aw_sum[:], aw_sum[:], 1.0, bv_col, ALU.mult, ALU.mult, accum_out=cj_tmp
                                   ).then_inc(s["const_cols"], 1)
            split_weights(5)
            for t in range(SLOTS):
                hyper(0, "hyp", t, n(0, t))
            hyper(0, "deg", 0, n(0, 0))
            dve.wait_ge(s["const_sum"], 1)
            V.tensor_tensor(c_bias, ps[:, 3, 1, 0:1], ab_col, ALU.add).then_inc(s["vec_const"], 1)
            for h in range(2):
                V.tensor_scalar(spread[:, h, :], ones[:], aw_col[:, h * KB:h * KB + 1], None, ALU.mult
                                ).then_inc(s["spread"], 1)
            split_weights(7)
            for t in range(SLOTS - 1):
                hyper(0, "adj0", t, n(0, t))
                hyper(0, "adj0hi", t, n(0, t))
            for b in range(1, KB):
                for h in range(2):
                    dve.wait_ge(s["spread_used"], 2 * (b - 1) + h + 1)
                    V.tensor_scalar(spread[:, h, :], ones[:], aw_col[:, h * KB + b:h * KB + b + 1], None, ALU.mult
                                    ).then_inc(s["spread"], 1)
            for j in range(2):
                dve.wait_ge(s["spread_used"], 2 * KB - 1 + j)
                V.tensor_scalar(spread[:, j, :], ones[:], beta_col[:, j:j + 1], None, ALU.mult).then_inc(s["spread"], 1)
            V.tensor_copy(vj_bc[:], ps[:, 3, 0, :])
            V.tensor_copy(vi_bc[:], ps[:, 3, 1, :]).then_inc(s["vec_out"], 1)
            for j in range(2 * KB):
                q = BETA0 + KB + j
                dve.wait_ge(s["spread_used"], 2 * KB + j + 1)
                if j + 2 < 2 * KB:
                    V.tensor_scalar(spread[:, j % 2, :], ones[:], beta_col[:, j + 2:j + 3], None, ALU.mult
                                    ).then_inc(s["spread"], 1)
                V.tensor_scalar(raw[:, q % RAW, :], raw[:, q % RAW, :], gamma_col[:, j:j + 1], None, ALU.mult
                                ).then_inc(s["raw_scaled"], 1)
                if j >= 2 and j % 2 == 0:
                    split_weights(BETA0 + j - 1)
            V.tensor_copy(beta_bc[:], ps[:, 3, 1, :]).then_inc(s["vec_out"], 1)
            split_weights(block_end[0] - 1)
            for layer in range(4):
                groups(dve, layer, body)

        @block.gpsimd
        def _(pool):
            Q = nc.gpsimd

            def lo_of(out_ap, full, hi):
                return Q.tensor_tensor(out_ap, full, f32(hi), ALU.subtract)

            def split_weights(b):
                place, k, _ = split_blocks[b]
                pool.wait_ge(s["raw_hi"], b + 1)
                lo_of(w_lo[:, place, k, :], raw[:, loads(b) % RAW, :], w_hi[:, place, k, :]).then_inc(s["raw_lo"], 1)

            def reciprocal_deviation(layer, g, t):
                pool.wait_ge(s["moments"], nl(layer, g, t))
                if layer > 0 or not first(g):
                    pool.wait_ge(s["norm"], nl(layer, g, t) - SLOTS)
                Q.tensor_tensor(var_eps[:, t:t + 1], moments[:, t, 1:2], eps_ln[:], ALU.add
                                ).then_inc(s["var_eps"], 1)
                pool.wait_ge(s["var_eps"], nl(layer, g, t))
                Q.tensor_tensor(rstd[:, t:t + 1], var_eps[:, t:t + 1], half_neg, ALU.pow).then_inc(s["rstd"], 1)

            def split(layer, g, t):
                pool.wait_ge(s["split_hi"], nl(layer, g, t))
                lo_of(row_lo[:, t, :], normed[:, t, :], row_hi[:, t, :]).then_inc(s["split_lo"], 1)

            def stored(layer, g, t):
                if layer > 0 or not first(g):
                    pool.wait_ge(x_stored[t], 16 * layer * GROUPS + 16 * g)

            def hyper(g, name, t, i):
                if name == "stats":
                    reciprocal_deviation(0, g, t)
                if name == "split":
                    split(0, g, t)
                if name == "mid":
                    pool.wait_ge(s0["moments2"], i)
                    Q.tensor_tensor(var_eps2[:, t:t + 1], moments2[:, t, 1:2], eps_ln[:], ALU.add
                                    ).then_inc(s0["var_eps2"], 1)
                    pool.wait_ge(s0["var_eps2"], i)
                    Q.tensor_tensor(rstd2[:, t:t + 1], var_eps2[:, t:t + 1], half_neg, ALU.pow).then_inc(s0["rstd2"], 1)
                if name == "midsplit":
                    pool.wait_ge(s0["rowa_hi"], i)
                    lo_of(row_lo[:, t, :], wide[:, t, 0:F], row_hi[:, t, :]).then_inc(s0["rowa_lo"], 1)
                if name == "resid":
                    stored(0, g, t)
                    if first(g) and t == 0:
                        pool.wait_ge(s["vec_loaded"], 64)
                    pool.wait_ge(s["relu"], i)
                    Q.tensor_tensor(x_res[:, t, :], x_in[:, t, :], normed[:, t, :], ALU.add).then_inc(s["resid"], 1)
                    pool.wait_ge(s["resid"], i)
                    Q.tensor_tensor(x_res[:, t, :], x_res[:, t, :], b0b_bc[:], ALU.add).then_inc(s0["res_b"], 1)
                if name == "rowb":
                    pool.wait_ge(s0["rowb_hi"], i)
                    lo_of(row_lo[:, t, :], wide[:, t, F:HID], row_hi[:, t, :]).then_inc(s0["rowb_lo"], 1)

            def gcn(g, name, t, i):
                if name == "stats":
                    reciprocal_deviation(1, g, t)
                if name == "split":
                    split(1, g, t)
                if name == "asplit":
                    pool.wait_ge(s1["asplit_hi"], i)
                    lo_of(adj_lo[:, t, :], adj_in[:, t, :], adj_hi[:, t, :]).then_inc(s1["asplit_lo"], 1)
                if name in ("adj0hi", "adj1hi", "adj2hi"):
                    pool.wait_ge(s1[name[:4] + "_hi"], i)
                    lo_of(col_lo[:, t, :], wide[:, t, F:HID], col_hi[:, t, :]).then_inc(s1[name[:4] + "_lo"], 1)
                if name == "resid":
                    stored(1, g, t)
                    pool.wait_ge(s["norm"], nl(1, g, t))
                    Q.tensor_tensor(x_res[:, t, :], x_in[:, t, :], b1_bc[:], ALU.add).then_inc(s["resid"], 1)

            def diffuse(g, name, t, i):
                if name == "stats":
                    reciprocal_deviation(2, g, t)
                if name == "resid":
                    stored(2, g, t)
                    pool.wait_ge(s["norm"], nl(2, g, t))
                    Q.tensor_tensor(x_res[:, t, :], x_in[:, t, :], ones[:, 0:1].to_broadcast([P, F]), ALU.mult).then_inc(s["resid"], 1)

            def mean(g, name, t, i):
                if name == "stats":
                    reciprocal_deviation(3, g, t)
                if name == "resid":
                    stored(3, g, t)
                    pool.wait_ge(s["norm"], nl(3, g, t))
                    Q.tensor_tensor(x_res[:, t, :], x_in[:, t, :], ones[:, 0:1].to_broadcast([P, F]), ALU.mult).then_inc(s["resid"], 1)
                if name == "asplit":
                    pool.wait_ge(s3["asplit_hi"], i)
                    lo_of(adj_lo[:, t, :], adj_in[:, t, :], adj_hi[:, t, :]).then_inc(s3["asplit_lo"], 1)

            WORK = [hyper, gcn, diffuse, mean]

            def body(layer, g, order):
                last = isinstance(g, int) and g == GROUPS - 1 and layer < 3
                b = block_end[layer]
                for name, t in order:
                    L, G = target(layer, g, name)
                    WORK[L](G, name.removesuffix("_n"), t, n(G, t))
                    if last and (name, t) in SPLIT_AFTER[layer]:
                        split_weights(b)
                        b += 1

            Q.memset(adj_in[:], 0.0)
            Q.memset(ones[:], 1.0)
            Q.memset(eps_ln[:], EPS_LN)
            Q.memset(ident[:], 0.0)
            Q.memset(wide[:, 0, F:F + P], 0.0)
            Q.memset(half_neg, -0.5).then_inc(s["pool_const"], 1)
            pool.wait_ge(s["pool_const"], 1)
            for h in range(2):
                Q.memset(wide[h * N:(h + 1) * N, 0, F + h * N:F + (h + 1) * N], 1.0).then_inc(s["pool_const"], 1)
            pool.wait_ge(s["pool_const"], 3)
            Q.affine_select(out=ident[:], in_=ident[:], compare_op=ALU.not_equal, fill=1.0, base=0,
                            pattern=[[-1, P]], channel_multiplier=1).then_inc(s["ready"], 1)
            split_weights(0)
            split_weights(2)
            for t in range(SLOTS):
                hyper(0, "stats", t, n(0, t))
            for t in range(SLOTS):
                hyper(0, "split", t, n(0, t))
                if t % 2:
                    split_weights(SLOTS + t - 1)
            for b in range(BETA0, block_end[0], 2):
                split_weights(b)
            pool.wait_ge(s["bk_loaded"], 48)
            Q.tensor_tensor(bk_bc[:], x_res[:, 0, :], x_res[:, 1, :], ALU.add).then_inc(s["bk_sum"], 1)
            pool.wait_ge(s["bk_sum"], 1)
            Q.tensor_tensor(bk_bc[:], bk_bc[:], x_res[:, 2, :], ALU.add).then_inc(s["bk_sum"], 1)
            for layer in range(4):
                groups(pool, layer, body)


def kernel(x, adj, L0_gnn_W1, L0_gnn_b1, L0_gnn_gamma, L0_gnn_beta, L0_gnn_W2, L0_gnn_b2, L1_gnn_W1, L1_gnn_b1,
           L1_gnn_W2, L1_gnn_b2, L1_gnn_W3, L1_gnn_b3, L2_gnn_Wv, L2_gnn_bv, L2_gnn_aw, L2_gnn_ab, L2_gnn_Wk,
           L2_gnn_bk, L3_gnn_W):
    import concourse.bacc as bacc
    from concourse.bass_utils import run_bass_kernel_spmd

    def a(v):
        return np.ascontiguousarray(v)

    def row(v):
        return a(np.asarray(v).reshape(1, -1))

    def columns(v):
        return a(np.asarray(v).reshape(-1, P).T)

    x = np.asarray(x)
    arrays = {
        "x": a(x.reshape(-1, x.shape[-1])),
        "adj": a(adj),
        "adj_t": a(np.swapaxes(np.asarray(adj), 1, 2)),
        "w0a": a(np.asarray(L0_gnn_W1).T), "w0b": a(np.asarray(L0_gnn_W2).T),
        "gamma_c": columns(L0_gnn_gamma), "b0a": row(L0_gnn_b1), "beta_c": columns(L0_gnn_beta), "b0b": row(L0_gnn_b2),
        "w1_0": a(L1_gnn_W1), "w1_1": a(L1_gnn_W2), "w1_2": a(L1_gnn_W3),
        "b1_0": row(L1_gnn_b1), "b1_1": row(L1_gnn_b2), "b1_2": row(L1_gnn_b3),
        "wv_t": a(np.asarray(L2_gnn_Wv).T), "bv_c": columns(L2_gnn_bv), "aw_c": columns(L2_gnn_aw),
        "ab": row(L2_gnn_ab), "wk": a(L2_gnn_Wk), "bk": a(L2_gnn_bk),
        "w3_t": a(np.asarray(L3_gnn_W).T),
    }
    nc = bacc.Bacc("TRN2", target_bir_lowering=False, num_devices=1)
    ins = {k: nc.dram_tensor(k, v.shape, mybir.dt.from_np(v.dtype), kind="ExternalInput").ap() for k, v in arrays.items()}
    out = nc.dram_tensor("out", arrays["x"].shape, F32, kind="ExternalOutput").ap()
    graph_stack(nc, ins["x"], ins["adj"], ins["adj_t"], ins["w0a"], ins["w0b"], ins["gamma_c"], ins["b0a"],
                ins["beta_c"], ins["b0b"], [ins[f"w1_{c}"] for c in range(3)], [ins[f"b1_{c}"] for c in range(3)],
                ins["wv_t"], ins["bv_c"], ins["aw_c"], ins["ab"], ins["wk"], ins["bk"], ins["w3_t"], out)
    r = run_bass_kernel_spmd(nc, [arrays], core_ids=[0])
    return r.results[0]["out"].reshape(x.shape)
```

```python
from contextlib import ExitStack

import numpy as np

import concourse.bass as bass
from concourse import mybir

P = 128
SLOTS = 4
F32 = mybir.dt.float32
F32R = mybir.dt.float32r
ALU = mybir.AluOpType
ACT = mybir.ActivationFunctionType
AX_X = mybir.AxisListType.X
EPS_LN = 1e-5
EPS_ALPHA = 1e-12
EPS_DEG = 1e-6
LEAK = 0.2


def order_hyper():
    return [
        ("resid", 0), ("lin1", 0), ("mid", 0), ("lin1", 1), ("hprep_n", 0), ("midnorm", 0), ("mid", 1), ("adj0", 3),
        ("midnorm", 1), ("adj0hi", 3), ("resid", 1), ("hprep_n", 1), ("lin1", 2), ("residb", 0), ("stats_n", 0),
        ("tra", 0), ("mid", 2), ("stats_n", 1), ("resid", 2), ("norm_n", 0), ("tra", 1), ("lin1", 3), ("hprep_n", 2),
        ("midnorm", 2), ("resid", 3), ("trb", 0), ("residb", 1), ("mid", 3), ("residb", 2), ("lina", 0), ("lina", 1),
        ("tra", 2), ("hprep_n", 3), ("trb", 1), ("midnorm", 3), ("stats_n", 2), ("linb", 0), ("norm_n", 1),
        ("trb", 2), ("residb", 3), ("stats_n", 3), ("binc_n", 0), ("lina", 2), ("tra", 3), ("binc_n", 1), ("linb", 1),
        ("binc_n", 2), ("adjb", 0), ("linb", 2), ("lina", 3), ("split_n", 0), ("trb", 3), ("adjb", 1), ("norm_n", 2),
        ("norm_n", 3), ("binc_n", 3), ("split_n", 1), ("hyp_n", 0), ("split_n", 2), ("adjb", 2), ("linb", 3),
        ("hyp_n", 1), ("adj0_n", 0), ("hyp_n", 2), ("adjb", 3), ("adj0hi_n", 0), ("adj0_n", 1), ("adj0_n", 2),
        ("hyp_n", 3), ("split_n", 3), ("adj0hi_n", 1), ("deg_n", 0), ("adj0hi_n", 2),
    ]


def order_gcn():
    return [
        ("lin0", 0), ("resid", 0), ("adj0", 3), ("resid", 1), ("lin0hi", 0), ("adj0hi", 3), ("lin0", 1),
        ("lin0hi", 1), ("adj1", 0), ("lin0", 2), ("adj1hi", 0), ("adj1", 1), ("lin0hi", 2), ("adj1hi", 1),
        ("lin0", 3), ("stats_n", 0), ("lin0hi", 3), ("adj1", 2), ("resid", 2), ("lin1", 0), ("lin1hi", 0),
        ("adj1", 3), ("adj1hi", 2), ("lin1", 1), ("resid", 3), ("adj1hi", 3), ("lin1hi", 1), ("stats_n", 1),
        ("adj2", 0), ("lin1", 2), ("stats_n", 2), ("adj2hi", 0), ("lin1hi", 2), ("adj2", 1), ("adj2hi", 1),
        ("asplit_n", 0), ("stats_n", 3), ("norm_n", 0), ("lin1", 3), ("split_n", 0), ("lin1hi", 3), ("adj2", 2),
        ("adj2hi", 2), ("lin2", 0), ("norm_n", 1), ("norm_n", 2), ("asplit_n", 1), ("asplit_n", 2), ("adj2", 3),
        ("split_n", 1), ("split_n", 2), ("adj2hi", 3), ("lin2", 1), ("norm_n", 3), ("lin2", 2), ("adj0_n", 0),
        ("adj0_n", 1), ("adj0hi_n", 0), ("asplit_n", 3), ("adj0hi_n", 1), ("adj0_n", 2), ("split_n", 3),
        ("adj0hi_n", 2), ("lin2", 3),
    ]


def order_diffuse():
    return [
        ("tr", 3), ("lin2", 0), ("sj", 0), ("diag", 3), ("resid", 0), ("alpha", 0), ("sj", 1), ("lin2", 1),
        ("lin2", 2), ("tt", 0), ("alpha", 1), ("sj", 2), ("alpha", 2), ("stats_n", 0), ("lin2", 3), ("sj", 3),
        ("norm_n", 0), ("resid", 1), ("lin1", 0), ("tt", 1), ("resid", 2), ("adj1", 0), ("lin0", 0), ("score_n", 0),
        ("resid", 3), ("tt", 2), ("lin1", 1), ("adj1", 1), ("lin0", 1), ("stats_n", 1), ("alpha", 3), ("stats_n", 2),
        ("adj0", 0), ("norm_n", 1), ("tr_n", 0), ("lin1", 2), ("tt", 3), ("adj0", 1), ("norm_n", 2), ("tr_n", 1),
        ("diag_n", 0), ("stats_n", 3), ("score_n", 1), ("adj1", 2), ("lin0", 2), ("score_n", 2), ("lin1", 3),
        ("adj1", 3), ("adj0", 2), ("norm_n", 3), ("diag_n", 1), ("tr_n", 2), ("lin0", 3), ("diag_n", 2), ("adj0", 3),
        ("score_n", 3),
    ]


def order_mean():
    return [
        ("asplit", 0), ("resid", 0), ("wb", 0), ("asplit", 1), ("wa", 0), ("asplit", 2), ("tr", 3), ("stats_n", 0),
        ("asplit", 3), ("resid", 1), ("wb", 1), ("ag", 0), ("norm_n", 0), ("wb", 2), ("wb", 3), ("wa", 1),
        ("resid", 2), ("stats_n", 1), ("stats_n", 2), ("ag", 1), ("norm_n", 1), ("norm_n", 2), ("resid", 3),
        ("wa", 2), ("ag", 2), ("tr_n", 0), ("tr_n", 1), ("stats_n", 3), ("wa", 3), ("ag", 3), ("tr_n", 2),
        ("norm_n", 3),
    ]


ORDERS = [order_hyper(), order_gcn(), order_diffuse(), order_mean()]
RENAMED = [
    {"hprep_n": None, "binc_n": None, "hyp_n": None, "deg_n": None},
    {"asplit_n": None, "split_n": None, "adj0_n": "tr_n", "adj0hi_n": "diag_n"},
    {"score_n": None, "diag_n": None},
    {"stats_n": None, "norm_n": None, "tr_n": None},
]
LAST = [[(ren.get(name, name), t) for name, t in order if ren.get(name, name)] for order, ren in zip(ORDERS, RENAMED)]
LAST[1] = [step for name, t in LAST[1] for step in ([("score_n", t)] if name == "diag_n" else []) + [(name, t)]]
LAST[1].append(("score_n", SLOTS - 1))
LAST[0] = [step for name, t in LAST[0] for step in ([("asplit_n", t)] if name == "split_n" else []) + [(name, t)]]
SPLIT_AFTER = [
    [("lin1", 1), ("lin1", 2), ("lin1", 3)] + [(f"tr{h}", t) for h in "ab" for t in range(SLOTS)] + [("linb", 3)],
    [(f"lin{c}", t) for c in range(3) for t in range(SLOTS)],
    [(f"lin{c}", t) for c in (2, 1) for t in range(SLOTS)],
    [],
]
PLACE = [[0, 1, 2, 3], [4, 5, 0], [3, 2, 1], [4, 5]]
RAW = 4


def graph_stack(nc, x, adj, adj_t, w0a, w0b, gamma_c, b0a, beta_c, b0b, w1, b1, wv_t, bv_c, aw_c, ab, wk, bk, w3_t, out):
    rows, F = x.shape
    N = adj.shape[1]
    HID = w0a.shape[1]
    TILES = rows // P
    GROUPS = TILES // SLOTS
    KB = F // P
    assert 2 * N == P and HID == 2 * F and F == 512 and TILES % SLOTS == 0

    with ExitStack() as ctx:
        def sb(name, shape, dt=F32):
            return ctx.enter_context(nc.sbuf_tensor(name, shape, dt))

        def sem(name):
            return ctx.enter_context(nc.semaphore(name))

        def sems(prefix, names):
            return {k: sem(prefix + k) for k in names.split()}

        w_hi = sb("w_hi", [P, 6, KB, F], F32R)
        w_lo = sb("w_lo", [P, 6, KB, F], F32R)
        raw = sb("raw", [P, RAW, F])
        x_in = sb("x_in", [P, SLOTS, F])
        x_res = sb("x_res", [P, SLOTS, F])
        normed = sb("normed", [P, SLOTS, F])
        wide = sb("wide", [P, SLOTS, HID])
        row_hi = sb("row_hi", [P, SLOTS, F], F32R)
        row_lo = sb("row_lo", [P, SLOTS, F], F32R)
        col_hi = sb("col_hi", [P, SLOTS, F], F32R)
        col_lo = sb("col_lo", [P, SLOTS, F], F32R)
        adj_in = sb("adj_in", [P, SLOTS, P])
        adj_both = sb("adj_both", [P, SLOTS, 2, P], F32R)
        adj_hi, adj_lo = adj_both[:, :, 0, :], adj_both[:, :, 1, :]
        inc_t = sb("inc_t", [P, SLOTS, P], F32R)
        binc_w = sb("binc_w", [P, SLOTS, P + 2], F32R)
        binc_hi, w_r = binc_w[:, :, 0:P], binc_w[:, :, P:P + 2]
        binc_lo = sb("binc_lo", [P, SLOTS, P], F32R)
        b0a_bc = sb("b0a_bc", [P, 2, F])
        b0b_bc = sb("b0b_bc", [P, F])
        beta_bc = sb("beta_bc", [P, F])
        b1_bc = sb("b1_bc", [P, F])
        vj_bc = sb("vj_bc", [P, F])
        vi_bc = sb("vi_bc", [P, F])
        bk_bc = sb("bk_bc", [P, F])
        ident = sb("ident", [P, P])
        ones = sb("ones", [P, P])
        block_ones = sb("block_ones", [P, P], F32R)
        aw_sum = sb("aw_sum", [P, KB])
        cols = sb("cols", [P, 29])
        gamma_col, beta_col = cols[:, 0:8], cols[:, 8:16]
        bv_col, aw_col, ab_col = cols[:, 16:20], cols[:, 20:28], cols[:, 28:29]
        consts = sb("consts", [P, 4])
        eps_ln = sb("eps_ln", [P, 1])
        half_neg, c_bias, cj_tmp = consts[:, 0:1], consts[:, 1:2], consts[:, 2:3]
        stats = sb("stats", [P, SLOTS, 12])
        moments = sb("moments", [P, SLOTS, 2])
        var_eps = sb("var_eps", [P, SLOTS])
        rstd = sb("rstd", [P, SLOTS])
        stats2 = sb("stats2", [P, SLOTS, 12])
        moments2 = sb("moments2", [P, SLOTS, 2])
        var_eps2 = sb("var_eps2", [P, SLOTS])
        rstd2 = sb("rstd2", [P, SLOTS])
        size = sb("size", [P, 4, SLOTS])
        w_sum = sb("w_sum", [P, SLOTS])
        size_r = sb("size_r", [P, 2, SLOTS], F32R)
        deg = sb("deg", [P, 8, SLOTS])
        D_SUM, D_POS, D_ZERO, D_SAFE, D_INV, D_OUT, M_SUM, DM_SUM = range(8)
        score = sb("score", [P, 6, SLOTS])
        S_J, S_I, S_IB, S_SUM, S_EPS, S_INV = range(6)
        ps = ctx.enter_context(nc.psum_tensor("ps", [P, SLOTS, 2, F], F32))

        def edge(t):
            return wide[:, t, F:F + P]

        scratch = beta_bc[:]
        diag_hi, diag_lo = inc_t, binc_lo

        def halves(t):
            both = ps[:, t, :, :].rearrange("p a (k h n) -> p (a k) h n", h=2, n=P)
            return both[:, :, 0, :], both[:, :, 1, :]

        def blocks(ap):
            return ap.rearrange("p (k n) -> p k n", n=P)

        aw_spread, beta_spread = blocks(wide[:, 2, :]), blocks(wide[:, 3, :])

        def f32(ap):
            return ap.bitcast(F32)

        x_loaded = [sem(f"x_loaded{t}") for t in range(SLOTS)]
        x_stored = [sem(f"x_stored{t}") for t in range(SLOTS)]
        raw_loaded = [sem(f"raw_loaded{i}") for i in range(RAW)]
        s = sems("", "adj_loaded rows_loaded stats moments var_eps rstd norm relu resid split_hi split_lo "
                     "final raw_hi raw_lo raw_lo_v raw_scaled cols_loaded vec_loaded b1_loaded wv_loaded "
                     "pool_const ready spread spread_used vec_const vec_out aw_sum const_cols const_sum bk_loaded bk_sum")
        s0 = sems("l0_", "inc w_sum w_hi w_lo size binc hyp m_hi d_sum degree dm_sum "
                         "adj0 adj0_rest adj0_sum adj0_hi adj0_lo lin1 affine relu2 stats2 moments2 var_eps2 rstd2 "
                         "norm2 tra tra_hi tra_lo lina trb trb_hi trb_lo linb rowb_hi rowb_lo adjb "
                         "res_b res_beta")
        s1 = sems("l1_", "asplit_hi asplit_lo " + " ".join(
            f"adj{c} adj{c}_rest adj{c}_sum adj{c}_hi adj{c}_lo lin{c} bias{c} row{c}_hi row{c}_lo" for c in range(3)))
        s2 = sems("l2_", "s_j s_i s_ib diag tr tr_hi tr_lo lin2 row2_hi row2_lo sj score leak exp alpha s_eps s_inv trans "
                         "tt tt_hi tt_lo adj1 row1_hi row1_lo adj0 biased")
        s3 = sems("l3_", "asplit_hi asplit_lo deg deg_max deg_inv tr tr_hi tr_lo wb row_hi row_lo ag scaled summed")

        def n(g, t):
            return g * SLOTS + t + 1

        def nl(layer, g, t):
            return g * SLOTS + (layer * TILES + t + 1)

        def target(layer, g, name):
            if not name.endswith("_n"):
                return layer, g
            return (layer + 1, 0) if isinstance(g, int) and g + 1 == GROUPS else (layer, g + 1)

        def first(g):
            return isinstance(g, int) and g == 0

        FULL = GROUPS - 1

        layer_blocks = [
            [(PLACE[0][u], k, w0a[k * P:(k + 1) * P, u * F:(u + 1) * F]) for u in range(2) for k in range(KB)]
            + [(PLACE[0][2 + u], k, w0b[(u * KB + k) * P:(u * KB + k + 1) * P, :]) for u in range(2) for k in range(KB)],
            [(PLACE[1][c], k, w1[c][k * P:(k + 1) * P, :]) for c in range(3) for k in range(KB)],
            [(PLACE[2][c], k, wk[c, k * P:(k + 1) * P, :]) for c in (2, 1, 0) for k in range(KB)],
            [(PLACE[3][u], k, w3_t[(u * KB + k) * P:(u * KB + k + 1) * P, :]) for u in (1, 0) for k in range(KB)],
        ]
        split_blocks = [b for blocks in layer_blocks for b in blocks]
        block_end = [sum(len(b) for b in layer_blocks[:layer + 1]) for layer in range(4)]
        BETA0 = 2 * KB

        def wait_split(eng, blocks):
            by_vector = min(blocks, block_end[0]) // 2
            eng.wait_ge(s["raw_lo"], blocks - by_vector)
            if by_vector:
                eng.wait_ge(s["raw_lo_v"], by_vector)

        def start_block(eng, b):
            if b >= RAW:
                wait_split(eng, b - RAW + 1)
            eng.dma_start(raw[:, b % RAW, :], split_blocks[b][2]).then_inc(raw_loaded[b % RAW], 16)

        def wait_block(eng, b):
            eng.wait_ge(raw_loaded[b % RAW], 16 * (b // RAW + 1))

        block = ctx.enter_context(nc.Block())

        def groups(eng, layer, body):
            body(layer, 0, ORDERS[layer])
            with eng.Fori(1, GROUPS - 1) as g:
                body(layer, g, ORDERS[layer])
            body(layer, GROUPS - 1, LAST[layer])

        x_tiles = x.rearrange("(n p) f -> n p f", p=P)
        out_tiles = out.rearrange("(n p) f -> n p f", p=P)
        adj_rows = adj.rearrange("(n h) i j -> h i n j", h=2)
        adj_cols = adj_t.rearrange("(n h) j i -> h j n i", h=2)

        @block.sync
        def _(sp):
            def load_x(layer, g, t):
                if layer > 0 or not first(g):
                    sp.wait_ge(s["resid"], nl(layer, g, t) - SLOTS)
                if layer > 0:
                    sp.wait_ge(x_stored[t], 16 * ((layer - 1) * GROUPS + 1) + 16 * g)
                src = (x_tiles if layer == 0 else out_tiles)[bass.ds(g * SLOTS + t, 1)]
                sp.dma_start(x_in[:, t, :], src.rearrange("n p f -> p (n f)")).then_inc(x_loaded[t], 16)

            def load_adj(layer, g):
                before = layer - 1 if first(g) else layer
                if before >= 0:
                    groups_before = GROUPS if first(g) else g
                    if before == 0:
                        sp.wait_ge(s0["w_sum"], groups_before)
                    else:
                        used = {1: s1["asplit_lo"], 2: s2["alpha"], 3: s3["asplit_lo"]}[before]
                        sp.wait_ge(used, groups_before * SLOTS)
                src = adj_rows if layer == 2 else adj_cols
                for h in range(2):
                    sp.dma_start(adj_in[h * N:(h + 1) * N, :, h * N:(h + 1) * N],
                                 src[h, :, bass.ds(g * SLOTS, SLOTS), :]).then_inc(s["adj_loaded"], 16)
                if layer == 3:
                    sp.wait_ge(s2["tt"] if first(g) else s3["deg"], TILES if first(g) else g * SLOTS)
                    for h in range(2):
                        sp.dma_start(wide[h * N:(h + 1) * N, :, F + h * N:F + (h + 1) * N],
                                     adj_rows[h, :, bass.ds(g * SLOTS, SLOTS), :]).then_inc(s["rows_loaded"], 16)

            def store_x(layer, g, t):
                sp.wait_ge(s["final"], nl(layer, g, t))
                sp.dma_start(out_tiles[bass.ds(g * SLOTS + t, 1)].rearrange("n p f -> p (n f)"), x_res[:, t, :]
                             ).then_inc(x_stored[t], 16)

            for a, b, v in ((0, 8, gamma_c), (8, 16, beta_c), (16, 20, bv_c), (20, 28, aw_c)):
                sp.dma_start(cols[:, a:b], v).then_inc(s["cols_loaded"], 16)
            sp.dma_start(ab_col, ab.to_broadcast([P, 1])).then_inc(s["cols_loaded"], 16)
            sp.wait_ge(s["ready"], 1)
            load_adj(0, 0)
            for t in range(SLOTS):
                load_x(0, 0, t)
            for k in range(KB):
                sp.dma_start(x_res[:, k, :], wv_t[k * P:(k + 1) * P, :]).then_inc(s["wv_loaded"], 16)
            for b in range(BETA0):
                start_block(sp, b)
            for u in range(2):
                sp.dma_start(b0a_bc[:, u, :], b0a[:, u * F:(u + 1) * F].to_broadcast([P, F])).then_inc(s["vec_loaded"], 16)
            for b in range(BETA0, block_end[0]):
                start_block(sp, b)
            sp.dma_start(b0b_bc[:], b0b.to_broadcast([P, F])).then_inc(s["vec_loaded"], 16)
            sp.dma_start(b1_bc[:], b1[2].to_broadcast([P, F])).then_inc(s["vec_loaded"], 16)
            sp.wait_ge(s["spread_used"], 1)
            for c in range(3):
                sp.dma_start(x_res[:, c, :], bk[c:c + 1, :].to_broadcast([P, F])).then_inc(s["bk_loaded"], 16)

            def body(layer, g, order):
                nxt = target(layer, g, "_n")
                if nxt[0] < 2:
                    load_adj(*nxt)
                if nxt[0] < 4:
                    for t in range(SLOTS):
                        load_x(*nxt, t)
                if nxt[0] in (2, 3):
                    load_adj(*nxt)
                for t in range(SLOTS):
                    store_x(layer, g, t)
            for layer in range(4):
                groups(sp, layer, body)
            for t in range(SLOTS):
                sp.wait_ge(x_stored[t], 16 * 4 * GROUPS)

        @block.tensor
        def _(pe):
            def product(out_ap, lhs_hi, lhs_lo, rhs_hi, rhs_lo, start=True, stop=True):
                nc.tensor.matmul(out_ap, lhs_hi, rhs_hi, start=start, stop=False)
                nc.tensor.matmul(out_ap, lhs_hi, rhs_lo, start=False, stop=False)
                return nc.tensor.matmul(out_ap, lhs_lo, rhs_hi, start=False, stop=stop)

            def linear(bank, t, place, start=True, stop=True):
                for k in range(KB):
                    last = product(ps[:, t, bank, :], col_hi[:, t, k * P:(k + 1) * P], col_lo[:, t, k * P:(k + 1) * P],
                                   w_hi[:, place, k, :], w_lo[:, place, k, :],
                                   start=start and k == 0, stop=stop and k == KB - 1)
                return last

            def mix_transposed(t):
                for k in range(KB):
                    at = ps[:, t, k // 2, (k % 2) * 2 * P:(k % 2 + 1) * 2 * P]
                    nc.tensor.matmul(at, row_hi[:, t, k * P:(k + 1) * P],
                                     adj_both[:, t, :, :].rearrange("p h n -> p (h n)"), start=True, stop=False)
                    last = nc.tensor.matmul(at[:, 0:P], row_lo[:, t, k * P:(k + 1) * P], adj_hi[:, t, :],
                                            start=False, stop=True)
                return last

            def mix(bank, t, start=True):
                return product(ps[:, t, bank, :], adj_hi[:, t, :], adj_lo[:, t, :], row_hi[:, t, :], row_lo[:, t, :],
                               start=start)

            def transposes(t, rows):
                for k in range(KB):
                    last = nc.tensor.transpose(ps[:, t, 0, k * P:(k + 1) * P], rows[:, k * P:(k + 1) * P], ident[:])
                return last

            def hyper(g, name, t, i):
                if name == "hyp":
                    pe.wait_ge(s0["binc"], i)
                    if not first(g):
                        pe.wait_ge(s["final"], i - SLOTS)
                    nc.tensor.matmul(ps[:, t, 0, 0:P + 2], inc_t[:, t, :], binc_w[:, t, :], start=True, stop=False)
                    nc.tensor.matmul(ps[:, t, 0, 0:P], inc_t[:, t, :], binc_lo[:, t, :], start=False, stop=True
                                     ).then_inc(s0["hyp"], 1)
                if name == "adj0":
                    pe.wait_ge(s0["d_sum"], i)
                    pe.wait_ge(s["split_lo"], nl(0, g, t))
                    if first(g) and t == SLOTS - 1:
                        pe.wait_ge(s["vec_out"], 2)
                    mix_transposed(t).then_inc(s0["adj0"], 1)
                if name == "lin1":
                    pe.wait_ge(s0["adj0_lo"], i)
                    if first(g):
                        wait_split(pe, BETA0)
                    linear(0, t, PLACE[0][0])
                    linear(1, t, PLACE[0][1]).then_inc(s0["lin1"], 1)
                if name in ("tra", "trb"):
                    pe.wait_ge(s0["norm2"] if name == "tra" else s0["tra_lo"], i)
                    transposes(t, wide[:, t, 0:F] if name == "tra" else wide[:, t, F:HID]).then_inc(s0[name], 1)
                if name == "lina":
                    pe.wait_ge(s0["tra_lo"], i)
                    if first(g):
                        wait_split(pe, block_end[0])
                    linear(1, t, PLACE[0][2], stop=False).then_inc(s0["lina"], 1)
                if name == "linb":
                    pe.wait_ge(s0["trb_lo"], i)
                    linear(1, t, PLACE[0][3], start=False).then_inc(s0["linb"], 1)
                if name == "adjb":
                    pe.wait_ge(s0["rowb_lo"], i)
                    mix(0, t).then_inc(s0["adjb"], 1)

            def gcn(g, name, t, i):
                c = int(name[3])
                if name == "adj0":
                    pe.wait_ge(s["split_lo"], nl(1, g, t))
                    pe.wait_ge(s1["asplit_lo"], i)
                    pe.wait_ge(s["final"], nl(1, g, t) - SLOTS)
                elif name in ("adj1", "adj2"):
                    pe.wait_ge(s1[f"row{c - 1}_lo"], i)
                if name.startswith("adj"):
                    mix_transposed(t).then_inc(s1[name], 1)
                else:
                    pe.wait_ge(s1[f"adj{c}_lo"], i)
                    if c == 0 and first(g):
                        wait_split(pe, block_end[1])
                    linear(1, t, PLACE[1][c]).then_inc(s1[name], 1)

            def diffuse(g, name, t, i):
                if name == "tr":
                    pe.wait_ge(s["norm"], nl(2, g, t))
                    if first(g):
                        pe.wait_ge(s1["adj2_lo"], n(FULL, t))
                    transposes(t, normed[:, t, :]).then_inc(s2["tr"], 1)
                if name == "lin2":
                    pe.wait_ge(s2["tr_lo"], i)
                    pe.wait_ge(s["final"], nl(2, g, t) - SLOTS)
                    if first(g):
                        wait_split(pe, block_end[2])
                    linear(1, t, PLACE[2][2]).then_inc(s2["lin2"], 1)
                if name == "sj":
                    pe.wait_ge(s2["s_ib"], i)
                    nc.tensor.matmul(ps[:, t, 0, 0:P], block_ones[:], diag_hi[:, t, :], start=True, stop=False)
                    nc.tensor.matmul(ps[:, t, 0, 0:P], block_ones[:], diag_lo[:, t, :], start=False, stop=True
                                     ).then_inc(s2["sj"], 1)
                if name == "tt":
                    pe.wait_ge(s2["trans"], i)
                    nc.tensor.transpose(ps[:, t, 0, 0:P], edge(t), ident[:]).then_inc(s2["tt"], 1)
                if name == "lin1":
                    pe.wait_ge(s2["tt_lo"], i)
                    linear(0, t, PLACE[2][1], stop=False)
                if name == "adj1":
                    pe.wait_ge(s2["row2_lo"], i)
                    mix(0, t, start=False).then_inc(s2["adj1"], 1)
                if name == "lin0":
                    linear(1, t, PLACE[2][0], stop=False)
                if name == "adj0":
                    pe.wait_ge(s2["row1_lo"], i)
                    mix(1, t, start=False).then_inc(s2["adj0"], 1)

            def mean(g, name, t, i):
                if name == "tr":
                    pe.wait_ge(s["norm"], nl(3, g, t))
                    if not first(g):
                        pe.wait_ge(s3["summed"], i - SLOTS)
                    transposes(t, normed[:, t, :]).then_inc(s3["tr"], 1)
                if name == "wb":
                    pe.wait_ge(s3["tr_lo"], i)
                    pe.wait_ge(s["final"], nl(3, g, t) - SLOTS)
                    if first(g):
                        wait_split(pe, block_end[3])
                    linear(1, t, PLACE[3][1]).then_inc(s3["wb"], 1)
                if name == "wa":
                    linear(0, t, PLACE[3][0])
                if name == "ag":
                    pe.wait_ge(s3["row_lo"], i)
                    pe.wait_ge(s3["asplit_lo"], i)
                    mix(1, t).then_inc(s3["ag"], 1)

            WORK = [(hyper, ("hyp", "adj0", "lin1", "tra", "lina", "trb", "linb", "adjb")),
                    (gcn, ("adj0", "adj1", "adj2", "lin0", "lin1", "lin2")),
                    (diffuse, ("tr", "lin2", "sj", "tt", "lin1", "adj1", "lin0", "adj0")),
                    (mean, ("tr", "wb", "wa", "ag"))]

            def body(layer, g, order):
                for name, t in order:
                    L, G = target(layer, g, name)
                    work, names = WORK[L]
                    if name.removesuffix("_n") in names:
                        work(G, name.removesuffix("_n"), t, n(G, t))

            pe.wait_ge(s["const_cols"], 1)
            nc.tensor.matmul(ps[:, 1, 1, 0:1], ones[:], cj_tmp, start=True, stop=True).then_inc(s["const_sum"], 1)
            pe.wait_ge(s["spread"], 1)
            pe.wait_ge(s["wv_loaded"], 16 * KB)
            for h in range(2):
                for k in range(KB):
                    last = nc.tensor.matmul(ps[:, 2, h, :], aw_spread[:, h * KB + k, :], x_res[:, k, :],
                                            start=k == 0, stop=k == KB - 1)
            last.then_inc(s["spread_used"], 1)
            pe.wait_ge(s["vec_const"], 1)
            pe.wait_ge(s["vec_out"], 1)
            for t in range(SLOTS):
                hyper(0, "hyp", t, n(0, t))

            def beta_product(blocks_of_beta):
                for j in blocks_of_beta:
                    wait_block(pe, BETA0 + j)
                    nc.tensor.matmul(ps[:, 3, 1, :], beta_spread[:, j, :], raw[:, (BETA0 + j) % RAW, :],
                                     start=j == 0, stop=j == 2 * KB - 1).then_inc(s["spread_used"], 1)

            pe.wait_ge(s["spread"], 2)
            beta_product(range(KB))
            for t in range(SLOTS - 1):
                hyper(0, "adj0", t, n(0, t))
            beta_product(range(KB, 2 * KB))
            for layer in range(4):
                groups(pe, layer, body)

        @block.scalar
        def _(act):
            def relu(out_ap, in_ap):
                return nc.scalar.activation(out_ap, in_ap, ACT.Relu)

            def copy(out_ap, in_ap):
                return nc.scalar.activation(out_ap, in_ap, ACT.Copy)

            def split_weights(b):
                place, k, _ = split_blocks[b]
                if BETA0 <= b < block_end[0]:
                    act.wait_ge(s["raw_scaled"], b - BETA0 + 1)
                else:
                    wait_block(act, b)
                copy(w_hi[:, place, k, :], raw[:, b % RAW, :]).then_inc(s["raw_hi"], 1)

            def split(layer, g, t):
                act.wait_ge(s["norm"], nl(layer, g, t))
                relu(normed[:, t, :], normed[:, t, :]).then_inc(s["relu"], 1)
                act.wait_ge(s["relu"], nl(layer, g, t))
                if layer == 0 and not first(g):
                    act.wait_ge(s0["adjb"], n(g, t) - SLOTS)
                elif layer == 1 and first(g):
                    act.wait_ge(s0["adjb"], n(FULL, t))
                elif layer == 1:
                    act.wait_ge(s1["adj2"], n(g, t) - SLOTS)
                copy(row_hi[:, t, :], normed[:, t, :]).then_inc(s["split_hi"], 1)

            def hyper(g, name, t, i):
                if name == "split":
                    split(0, g, t)
                if name == "hyp":
                    act.wait_ge(s0["hyp"], i)
                    if not first(g):
                        act.wait_ge(s0["dm_sum"], g)
                    nc.scalar.activation(adj_hi[:, t, :], ps[:, t, 0, 0:P], ACT.Copy,
                                         accum_out=deg[:, M_SUM, t:t + 1]).then_inc(s0["m_hi"], 1)
                if name == "adj0":
                    act.wait_ge(s0["adj0"], i)
                    if not first(g):
                        act.wait_ge(s0["tra"], i - SLOTS)
                    copy(blocks(wide[:, t, 0:F]), halves(t)[1]).then_inc(s0["adj0_rest"], 1)
                if name == "adj0hi":
                    act.wait_ge(s0["adj0_sum"], i)
                    copy(col_hi[:, t, :], wide[:, t, 0:F]).then_inc(s0["adj0_hi"], 1)
                if name in ("tra", "trb"):
                    act.wait_ge(s0[name], i)
                    if name == "trb":
                        act.wait_ge(s0["lina"], i)
                    copy(col_hi[:, t, :], ps[:, t, 0, :]).then_inc(s0[name + "_hi"], 1)
                if name == "linb":
                    act.wait_ge(s0["linb"], i)
                    copy(row_hi[:, t, :], ps[:, t, 1, :]).then_inc(s0["rowb_hi"], 1)
                if name == "lin1":
                    act.wait_ge(s0["affine"], i)
                    relu(wide[:, t, :], wide[:, t, :]).then_inc(s0["relu2"], 1)

            def gcn(g, name, t, i):
                if name == "split":
                    split(1, g, t)
                if name == "asplit":
                    act.wait_ge(s["adj_loaded"], 32 * (GROUPS + 1) + 32 * g)
                    if first(g):
                        act.wait_ge(s0["adjb"], n(FULL, t))
                    else:
                        act.wait_ge(s1["adj2"], i - SLOTS)
                    copy(adj_hi[:, t, :], adj_in[:, t, :]).then_inc(s1["asplit_hi"], 1)
                if name in ("adj0", "adj1", "adj2"):
                    act.wait_ge(s1[name], i)
                    copy(blocks(wide[:, t, F:HID]), halves(t)[1]).then_inc(s1[name + "_rest"], 1)
                if name in ("adj0hi", "adj1hi", "adj2hi"):
                    act.wait_ge(s1[name[:4] + "_sum"], i)
                    copy(col_hi[:, t, :], wide[:, t, F:HID]).then_inc(s1[name[:4] + "_hi"], 1)
                if name in ("lin0hi", "lin1hi"):
                    c = int(name[3])
                    act.wait_ge(s1[f"bias{c}"], i)
                    relu(row_hi[:, t, :], wide[:, t, 0:F]).then_inc(s1[f"row{c}_hi"], 1)

            def diffuse(g, name, t, i):
                if name == "tr":
                    act.wait_ge(s2["tr"], i)
                    relu(col_hi[:, t, :], ps[:, t, 0, :]).then_inc(s2["tr_hi"], 1)
                if name == "lin2":
                    act.wait_ge(s2["lin2"], i)
                    copy(row_hi[:, t, :], ps[:, t, 1, :]).then_inc(s2["row2_hi"], 1)
                if name == "sj":
                    act.wait_ge(s2["leak"], i)
                    nc.scalar.activation(edge(t), edge(t), ACT.Exp).then_inc(s2["exp"], 1)
                if name == "tt":
                    act.wait_ge(s2["tt"], i)
                    copy(adj_hi[:, t, :], ps[:, t, 0, 0:P]).then_inc(s2["tt_hi"], 1)
                if name == "adj1":
                    act.wait_ge(s2["adj1"], i)
                    copy(row_hi[:, t, :], ps[:, t, 0, :]).then_inc(s2["row1_hi"], 1)

            def mean(g, name, t, i):
                if name == "tr":
                    act.wait_ge(s3["tr"], i)
                    relu(col_hi[:, t, :], ps[:, t, 0, :]).then_inc(s3["tr_hi"], 1)
                if name == "wb":
                    act.wait_ge(s3["wb"], i)
                    copy(row_hi[:, t, :], ps[:, t, 1, :]).then_inc(s3["row_hi"], 1)
                if name == "asplit":
                    act.wait_ge(s["adj_loaded"], 32 * (3 * GROUPS + 1) + 32 * g)
                    if first(g):
                        act.wait_ge(s2["adj0"], n(FULL, t))
                    else:
                        act.wait_ge(s3["ag"], i - SLOTS)
                    copy(adj_hi[:, t, :], adj_in[:, t, :]).then_inc(s3["asplit_hi"], 1)

            WORK = [hyper, gcn, diffuse, mean]

            def body(layer, g, order):
                last = isinstance(g, int) and g == GROUPS - 1 and layer < 3
                b = block_end[layer]
                if last:
                    if layer == 1:
                        act.wait_ge(s0["linb"], TILES)
                    if layer == 2:
                        act.wait_ge(s1["lin1"], TILES)
                    start_block(act, b)
                for name, t in order:
                    L, G = target(layer, g, name)
                    WORK[L](G, name.removesuffix("_n"), t, n(G, t))
                    if last and layer == 0 and (name, t) == ("mid", 3):
                        for c in range(2):
                            act.dma_start(b0a_bc[:, c, :], b1[c].to_broadcast([P, F])).then_inc(s["b1_loaded"], 16)
                    if last and (name, t) in SPLIT_AFTER[layer]:
                        if b + 1 < block_end[layer + 1]:
                            start_block(act, b + 1)
                        split_weights(b)
                        b += 1

            for b in range(SLOTS):
                split_weights(b)
            for t in range(SLOTS):
                hyper(0, "split", t, n(0, t))
                split_weights(SLOTS + t)
            for t in range(SLOTS):
                hyper(0, "hyp", t, n(0, t))
            for b in range(BETA0, BETA0 + KB):
                split_weights(b)
            for t in range(SLOTS - 1):
                hyper(0, "adj0", t, n(0, t))
                hyper(0, "adj0hi", t, n(0, t))
            for b in range(BETA0 + KB, block_end[0]):
                split_weights(b)
            for layer in range(4):
                groups(act, layer, body)

        @block.vector
        def _(dve):
            V = nc.vector

            def lo_of(out_ap, full, hi):
                return V.tensor_tensor(out_ap, full, f32(hi), ALU.subtract)

            def carry_wait():
                V.memset(consts[:, 3:4], 0.0)

            def statistics(layer, g, t):
                dve.wait_ge(x_loaded[t], 16 * (layer * GROUPS + 1) + 16 * g)
                V.bn_stats(stats[:, t, 0:6], x_in[:, t, :]).then_inc(s["stats"], 1)
                dve.wait_ge(s["stats"], nl(layer, g, t))
                carry_wait()
                V.bn_aggr(moments[:, t, :], stats[:, t, 0:6]).then_inc(s["moments"], 1)

            def normalise(layer, g, t):
                dve.wait_ge(s["rstd"], nl(layer, g, t))
                i = n(g, t)
                if layer == 0 and not first(g):
                    dve.wait_ge(s["resid"], i - SLOTS)
                if layer == 1 and first(g):
                    dve.wait_ge(s["resid"], n(FULL, t))
                if layer == 1 and not first(g) or layer == 2 and first(g):
                    dve.wait_ge(s["split_lo"], nl(layer, g, t) - SLOTS)
                if layer == 2 and not first(g):
                    dve.wait_ge(s2["tr"], i - SLOTS)
                if layer == 3:
                    dve.wait_ge(s2["tr"] if first(g) else s3["tr"], n(FULL, t) if first(g) else i - SLOTS)
                V.tensor_scalar(normed[:, t, :], x_in[:, t, :], moments[:, t, 0:1], rstd[:, t:t + 1],
                                ALU.subtract, ALU.mult).then_inc(s["norm"], 1)

            def hyper(g, name, t, i):
                if name == "stats":
                    statistics(0, g, t)
                if name == "norm":
                    normalise(0, g, t)
                if name == "hprep":
                    dve.wait_ge(s["adj_loaded"], 32 * (g + 1))
                    if not first(g):
                        dve.wait_ge(s0["hyp"], i - SLOTS)
                    V.tensor_scalar(inc_t[:, t, :], adj_in[:, t, :], 0.0, 0.0, ALU.not_equal, ALU.add,
                                    accum_out=size[:, 0, t:t + 1]).then_inc(s0["inc"], 1)
                if name == "hprep" and t == SLOTS - 1:
                    if not first(g):
                        dve.wait_ge(s0["hyp"], g * SLOTS)
                    V.tensor_tensor(w_sum[:], adj_in[:, :, 0], adj_in[:, :, N], ALU.add).then_inc(s0["w_sum"], 1)
                    dve.wait_ge(s0["inc"], i)
                    V.tensor_scalar_max(size[:, 1, :], size[:, 0, :], 1.0).then_inc(s0["size"], 1)
                    dve.wait_ge(s0["w_sum"], g + 1)
                    V.tensor_copy(w_r[:, :, 0], w_sum[:]).then_inc(s0["w_hi"], 1)
                    dve.wait_ge(s0["size"], 4 * g + 1)
                    V.reciprocal(size[:, 2, :], size[:, 1, :]).then_inc(s0["size"], 1)
                    dve.wait_ge(s0["w_hi"], g + 1)
                    lo_of(w_r[:, :, 1], w_sum[:], w_r[:, :, 0]).then_inc(s0["w_lo"], 1)
                    dve.wait_ge(s0["size"], 4 * g + 2)
                    V.tensor_copy(size_r[:, 0, :], size[:, 2, :]).then_inc(s0["size"], 1)
                    dve.wait_ge(s0["size"], 4 * g + 3)
                    lo_of(size_r[:, 1, :], size[:, 2, :], size_r[:, 0, :]).then_inc(s0["size"], 1)
                if name == "binc":
                    dve.wait_ge(s0["size"], 4 * g + 4)
                    V.tensor_scalar(binc_hi[:, t, :], f32(inc_t[:, t, :]), f32(size_r[:, 0, t:t + 1]), None, ALU.mult)
                    V.tensor_scalar(binc_lo[:, t, :], f32(inc_t[:, t, :]), f32(size_r[:, 1, t:t + 1]), None, ALU.mult
                                    ).then_inc(s0["binc"], 1)
                if name == "hyp":
                    dve.wait_ge(s0["m_hi"], i)
                    lo_of(adj_lo[:, t, :], ps[:, t, 0, 0:P], adj_hi[:, t, :])
                    V.reduce_sum(deg[:, D_SUM, t:t + 1], ps[:, t, 0, P:P + 2], AX_X).then_inc(s0["d_sum"], 1)
                if name == "deg":
                    dve.wait_ge(s0["d_sum"], (g + 1) * SLOTS)
                    V.tensor_scalar(deg[:, D_POS, :], deg[:, D_SUM, :], 0.0, None, ALU.is_gt).then_inc(s0["degree"], 1)
                    dve.wait_ge(s0["degree"], 5 * g + 1)
                    V.tensor_scalar(deg[:, D_ZERO, :], deg[:, D_POS, :], -1.0, 1.0, ALU.mult, ALU.add
                                    ).then_inc(s0["degree"], 1)
                    dve.wait_ge(s0["degree"], 5 * g + 2)
                    V.scalar_tensor_tensor(deg[:, D_SAFE, :], deg[:, D_SUM, :], 0.0, deg[:, D_ZERO, :],
                                           ALU.max, ALU.add).then_inc(s0["degree"], 1)
                    dve.wait_ge(s0["degree"], 5 * g + 3)
                    V.reciprocal(deg[:, D_INV, :], deg[:, D_SAFE, :]).then_inc(s0["degree"], 1)
                    dve.wait_ge(s0["degree"], 5 * g + 4)
                    V.tensor_tensor(deg[:, D_OUT, :], deg[:, D_INV, :], deg[:, D_POS, :], ALU.mult
                                    ).then_inc(s0["degree"], 1)
                    dve.wait_ge(s0["degree"], 5 * g + 5)
                    V.tensor_tensor(deg[:, DM_SUM, :], deg[:, D_OUT, :], deg[:, M_SUM, :], ALU.mult
                                    ).then_inc(s0["dm_sum"], 1)
                if name == "adj0":
                    dve.wait_ge(s0["adj0_rest"], i)
                    V.tensor_tensor(blocks(wide[:, t, 0:F]), halves(t)[0], blocks(wide[:, t, 0:F]), ALU.add
                                    ).then_inc(s0["adj0_sum"], 1)
                if name == "adj0hi":
                    dve.wait_ge(s0["adj0_hi"], i)
                    lo_of(col_lo[:, t, :], wide[:, t, 0:F], col_hi[:, t, :]).then_inc(s0["adj0_lo"], 1)
                if name in ("tra", "trb"):
                    dve.wait_ge(s0[name + "_hi"], i)
                    lo_of(col_lo[:, t, :], ps[:, t, 0, :], col_hi[:, t, :]).then_inc(s0[name + "_lo"], 1)
                if name == "lin1":
                    dve.wait_ge(s0["lin1"], i)
                    if first(g):
                        dve.wait_ge(s["vec_loaded"], 64)
                    else:
                        dve.wait_ge(s0["trb"], i - SLOTS)
                    V.scalar_tensor_tensor(wide[:, t, :], ps[:, t, :, :].rearrange("p a f -> p (a f)"),
                                           deg[:, D_OUT, t:t + 1], b0a_bc[:].rearrange("p a f -> p (a f)"),
                                           ALU.mult, ALU.add).then_inc(s0["affine"], 1)
                if name == "mid":
                    dve.wait_ge(s0["relu2"], i)
                    for h in range(2):
                        V.bn_stats(stats2[:, t, 6 * h:6 * h + 6], wide[:, t, h * F:(h + 1) * F]).then_inc(s0["stats2"], 1)
                    dve.wait_ge(s0["stats2"], 2 * i)
                    carry_wait()
                    V.bn_aggr(moments2[:, t, :], stats2[:, t, :]).then_inc(s0["moments2"], 1)
                if name == "midnorm":
                    dve.wait_ge(s0["rstd2"], i)
                    V.tensor_scalar(wide[:, t, :], wide[:, t, :], moments2[:, t, 0:1], rstd2[:, t:t + 1],
                                    ALU.subtract, ALU.mult).then_inc(s0["norm2"], 1)
                if name == "residb":
                    dve.wait_ge(s0["res_b"], i)
                    dve.wait_ge(s0["dm_sum"], g + 1)
                    V.scalar_tensor_tensor(x_res[:, t, :], beta_bc[:], deg[:, DM_SUM, t:t + 1], x_res[:, t, :],
                                           ALU.mult, ALU.add).then_inc(s0["res_beta"], 1)
                if name == "linb":
                    dve.wait_ge(s0["rowb_hi"], i)
                    lo_of(row_lo[:, t, :], ps[:, t, 1, :], row_hi[:, t, :]).then_inc(s0["rowb_lo"], 1)
                if name == "adjb":
                    dve.wait_ge(s0["adjb"], i)
                    dve.wait_ge(s0["res_beta"], i)
                    V.scalar_tensor_tensor(x_res[:, t, :], ps[:, t, 0, :], deg[:, D_OUT, t:t + 1], x_res[:, t, :],
                                           ALU.mult, ALU.add).then_inc(s["final"], 1)

            def gcn(g, name, t, i):
                if name == "stats":
                    statistics(1, g, t)
                if name == "norm":
                    normalise(1, g, t)
                if name in ("adj0", "adj1", "adj2"):
                    dve.wait_ge(s1[name + "_rest"], i)
                    V.tensor_tensor(blocks(wide[:, t, F:HID]), halves(t)[0], blocks(wide[:, t, F:HID]), ALU.add).then_inc(s1[name + "_sum"], 1)
                if name in ("lin0", "lin1"):
                    c = int(name[3])
                    dve.wait_ge(s1[name], i)
                    if c == 0 and first(g):
                        dve.wait_ge(s["b1_loaded"], 32)
                        dve.wait_ge(s0["trb"], n(FULL, t))
                    V.tensor_tensor(wide[:, t, 0:F], ps[:, t, 1, :], b0a_bc[:, c, :], ALU.add).then_inc(s1[f"bias{c}"], 1)
                if name in ("lin0hi", "lin1hi"):
                    c = int(name[3])
                    dve.wait_ge(s1[f"row{c}_hi"], i)
                    V.scalar_tensor_tensor(row_lo[:, t, :], wide[:, t, 0:F], 0.0, f32(row_hi[:, t, :]),
                                           ALU.max, ALU.subtract).then_inc(s1[f"row{c}_lo"], 1)
                if name == "lin2":
                    dve.wait_ge(s1[name], i)
                    dve.wait_ge(s["resid"], nl(1, g, t))
                    V.tensor_tensor(x_res[:, t, :], ps[:, t, 1, :], x_res[:, t, :], ALU.add).then_inc(s["final"], 1)

            def diffuse(g, name, t, i):
                if name == "stats":
                    statistics(2, g, t)
                if name == "norm":
                    normalise(2, g, t)
                if name == "score":
                    dve.wait_ge(s["norm"], nl(2, g, t))
                    for v, at, done in ((vj_bc, S_J, "s_j"), (vi_bc, S_I, "s_i")):
                        V.scalar_tensor_tensor(scratch, normed[:, t, :], 0.0, v[:], ALU.max, ALU.mult,
                                               accum_out=score[:, at, t:t + 1]).then_inc(s2[done], 1)
                        dve.wait_ge(s2[done], i)
                if name == "tr":
                    dve.wait_ge(s2["tr_hi"], i)
                    V.scalar_tensor_tensor(col_lo[:, t, :], ps[:, t, 0, :], 0.0, f32(col_hi[:, t, :]),
                                           ALU.max, ALU.subtract).then_inc(s2["tr_lo"], 1)
                if name == "diag":
                    dve.wait_ge(s2["s_i"], i)
                    if not first(g):
                        dve.wait_ge(s2["sj"], i - SLOTS)
                    V.tensor_scalar(diag_hi[:, t, :], ident[:], score[:, S_J, t:t + 1], None, ALU.mult
                                    ).then_inc(s2["diag"], 1)
                    dve.wait_ge(s2["diag"], i)
                    V.scalar_tensor_tensor(diag_lo[:, t, :], ident[:], score[:, S_J, t:t + 1], f32(diag_hi[:, t, :]),
                                           ALU.mult, ALU.subtract)
                    V.tensor_tensor(score[:, S_IB, t:t + 1], score[:, S_I, t:t + 1], c_bias, ALU.add
                                    ).then_inc(s2["s_ib"], 1)
                if name == "lin2":
                    dve.wait_ge(s2["row2_hi"], i)
                    lo_of(row_lo[:, t, :], ps[:, t, 1, :], row_hi[:, t, :]).then_inc(s2["row2_lo"], 1)
                if name == "sj":
                    dve.wait_ge(s2["sj"], i)
                    dve.wait_ge(s2["s_ib"], i)
                    if not first(g):
                        dve.wait_ge(s2["tt"], i - SLOTS)
                    V.scalar_tensor_tensor(edge(t), ps[:, t, 0, 0:P], score[:, S_IB, t:t + 1], f32(block_ones[:]),
                                           ALU.add, ALU.mult).then_inc(s2["score"], 1)
                    dve.wait_ge(s2["score"], i)
                    V.scalar_tensor_tensor(edge(t), edge(t), LEAK, edge(t), ALU.mult, ALU.max).then_inc(s2["leak"], 1)
                if name == "alpha":
                    dve.wait_ge(s2["exp"], i)
                    dve.wait_ge(s["adj_loaded"], 32 * (2 * GROUPS + 1) + 32 * g)
                    V.scalar_tensor_tensor(edge(t), edge(t), 1.0, adj_in[:, t, :], ALU.mult, ALU.mult,
                                           accum_out=score[:, S_SUM, t:t + 1]).then_inc(s2["alpha"], 1)
                    dve.wait_ge(s2["alpha"], i)
                    V.tensor_scalar_add(score[:, S_EPS, t:t + 1], score[:, S_SUM, t:t + 1], EPS_ALPHA
                                        ).then_inc(s2["s_eps"], 1)
                    dve.wait_ge(s2["s_eps"], i)
                    V.reciprocal(score[:, S_INV, t:t + 1], score[:, S_EPS, t:t + 1]).then_inc(s2["s_inv"], 1)
                    dve.wait_ge(s2["s_inv"], i)
                    V.tensor_scalar(edge(t), edge(t), score[:, S_INV, t:t + 1], None, ALU.mult).then_inc(s2["trans"], 1)
                if name == "tt":
                    dve.wait_ge(s2["tt_hi"], i)
                    lo_of(adj_lo[:, t, :], ps[:, t, 0, 0:P], adj_hi[:, t, :]).then_inc(s2["tt_lo"], 1)
                if name == "adj1":
                    dve.wait_ge(s2["row1_hi"], i)
                    lo_of(row_lo[:, t, :], ps[:, t, 0, :], row_hi[:, t, :]).then_inc(s2["row1_lo"], 1)
                if name == "adj0":
                    dve.wait_ge(s2["adj0"], i)
                    V.tensor_tensor(wide[:, t, 0:F], ps[:, t, 1, :], bk_bc[:], ALU.add).then_inc(s2["biased"], 1)
                    dve.wait_ge(s2["biased"], i)
                    dve.wait_ge(s["resid"], nl(2, g, t))
                    V.scalar_tensor_tensor(x_res[:, t, :], wide[:, t, 0:F], 0.0, x_res[:, t, :], ALU.max, ALU.add
                                           ).then_inc(s["final"], 1)

            def mean(g, name, t, i):
                if name == "stats":
                    statistics(3, g, t)
                if name == "norm":
                    normalise(3, g, t)
                if name == "tr":
                    dve.wait_ge(s3["tr_hi"], i)
                    V.scalar_tensor_tensor(col_lo[:, t, :], ps[:, t, 0, :], 0.0, f32(col_hi[:, t, :]),
                                           ALU.max, ALU.subtract).then_inc(s3["tr_lo"], 1)
                if name == "wb":
                    dve.wait_ge(s3["row_hi"], i)
                    lo_of(row_lo[:, t, :], ps[:, t, 1, :], row_hi[:, t, :]).then_inc(s3["row_lo"], 1)
                if name == "asplit":
                    dve.wait_ge(s["rows_loaded"], 32 * (g + 1))
                    V.reduce_sum(deg[:, D_SUM, t:t + 1], edge(t), AX_X).then_inc(s3["deg"], 1)
                if name == "asplit" and t == SLOTS - 1:
                    dve.wait_ge(s3["deg"], i)
                    V.tensor_scalar_max(deg[:, D_SAFE, :], deg[:, D_SUM, :], EPS_DEG).then_inc(s3["deg_max"], 1)
                    dve.wait_ge(s3["deg_max"], g + 1)
                    V.reciprocal(deg[:, D_OUT, :], deg[:, D_SAFE, :]).then_inc(s3["deg_inv"], 1)
                if name == "ag":
                    dve.wait_ge(s3["ag"], i)
                    dve.wait_ge(s3["deg_inv"], g + 1)
                    V.tensor_scalar(wide[:, t, 0:F], ps[:, t, 1, :], deg[:, D_OUT, t:t + 1], None, ALU.mult
                                    ).then_inc(s3["scaled"], 1)
                    dve.wait_ge(s3["scaled"], i)
                    V.tensor_tensor(wide[:, t, 0:F], ps[:, t, 0, :], wide[:, t, 0:F], ALU.add).then_inc(s3["summed"], 1)
                    dve.wait_ge(s3["summed"], i)
                    dve.wait_ge(s["resid"], nl(3, g, t))
                    V.scalar_tensor_tensor(x_res[:, t, :], wide[:, t, 0:F], 0.0, x_res[:, t, :], ALU.max, ALU.add
                                           ).then_inc(s["final"], 1)

            WORK = [hyper, gcn, diffuse, mean]

            def body(layer, g, order):
                for name, t in order:
                    L, G = target(layer, g, name)
                    WORK[L](G, name.removesuffix("_n"), t, n(G, t))

            def split_weights(b):
                place, k, _ = split_blocks[b]
                dve.wait_ge(s["raw_hi"], b + 1)
                lo_of(w_lo[:, place, k, :], raw[:, b % RAW, :], w_hi[:, place, k, :]).then_inc(s["raw_lo_v"], 1)

            dve.wait_ge(s["ready"], 1)
            V.tensor_copy(block_ones[:], wide[:, 0, F:F + P])
            dve.wait_ge(s["cols_loaded"], 16 * 5)
            V.tensor_tensor(aw_sum[:], aw_col[:, 0:KB], aw_col[:, KB:2 * KB], ALU.add).then_inc(s["aw_sum"], 1)
            dve.wait_ge(s["aw_sum"], 1)
            V.scalar_tensor_tensor(aw_sum[:], aw_sum[:], 1.0, bv_col, ALU.mult, ALU.mult, accum_out=cj_tmp
                                   ).then_inc(s["const_cols"], 1)

            def spread_blocks(vector, spread):
                for j in range(2 * KB):
                    last = V.tensor_scalar(spread[:, j, :], ones[:], vector[:, j:j + 1], None, ALU.mult)
                last.then_inc(s["spread"], 1)

            spread_blocks(aw_col, aw_spread)
            spread_blocks(beta_col, beta_spread)
            dve.wait_ge(s["const_sum"], 1)
            V.tensor_tensor(c_bias, ps[:, 1, 1, 0:1], ab_col, ALU.add).then_inc(s["vec_const"], 1)
            for t in range(SLOTS):
                hyper(0, "hprep", t, n(0, t))
            hyper(0, "stats", 0, n(0, 0))
            hyper(0, "stats", 1, n(0, 1))
            for t in range(SLOTS):
                hyper(0, "binc", t, n(0, t))
            hyper(0, "norm", 0, n(0, 0))
            hyper(0, "stats", 2, n(0, 2))
            hyper(0, "norm", 1, n(0, 1))
            hyper(0, "stats", 3, n(0, 3))
            hyper(0, "norm", 2, n(0, 2))
            split_weights(1)
            hyper(0, "norm", 3, n(0, 3))
            split_weights(3)
            dve.wait_ge(s["spread_used"], 1)
            V.tensor_copy(vj_bc[:], ps[:, 2, 0, :])
            V.tensor_copy(vi_bc[:], ps[:, 2, 1, :]).then_inc(s["vec_out"], 1)
            split_weights(5)
            for t in range(SLOTS):
                hyper(0, "hyp", t, n(0, t))
            split_weights(7)
            hyper(0, "deg", 0, n(0, 0))

            def scale_blocks(blocks_of_gamma):
                for j in blocks_of_gamma:
                    b = BETA0 + j
                    dve.wait_ge(s["spread_used"], j + 2)
                    V.tensor_scalar(raw[:, b % RAW, :], raw[:, b % RAW, :], gamma_col[:, j:j + 1], None, ALU.mult
                                    ).then_inc(s["raw_scaled"], 1)
                    if j % KB == KB - 2:
                        split_weights(b - 1)
                split_weights(b)

            scale_blocks(range(KB))
            for t in range(SLOTS - 1):
                hyper(0, "adj0", t, n(0, t))
                hyper(0, "adj0hi", t, n(0, t))
            scale_blocks(range(KB, 2 * KB))
            V.tensor_copy(beta_bc[:], ps[:, 3, 1, :]).then_inc(s["vec_out"], 1)
            for layer in range(4):
                groups(dve, layer, body)

        @block.gpsimd
        def _(pool):
            Q = nc.gpsimd

            def lo_of(out_ap, full, hi):
                return Q.tensor_tensor(out_ap, full, f32(hi), ALU.subtract)

            def split_weights(b):
                place, k, _ = split_blocks[b]
                pool.wait_ge(s["raw_hi"], b + 1)
                lo_of(w_lo[:, place, k, :], raw[:, b % RAW, :], w_hi[:, place, k, :]).then_inc(s["raw_lo"], 1)

            def reciprocal_deviation(layer, g, t):
                pool.wait_ge(s["moments"], nl(layer, g, t))
                if layer > 0 or not first(g):
                    pool.wait_ge(s["norm"], nl(layer, g, t) - SLOTS)
                Q.tensor_tensor(var_eps[:, t:t + 1], moments[:, t, 1:2], eps_ln[:], ALU.add
                                ).then_inc(s["var_eps"], 1)
                pool.wait_ge(s["var_eps"], nl(layer, g, t))
                Q.tensor_tensor(rstd[:, t:t + 1], var_eps[:, t:t + 1], half_neg, ALU.pow).then_inc(s["rstd"], 1)

            def split(layer, g, t):
                pool.wait_ge(s["split_hi"], nl(layer, g, t))
                lo_of(row_lo[:, t, :], normed[:, t, :], row_hi[:, t, :]).then_inc(s["split_lo"], 1)

            def stored(layer, g, t):
                if layer > 0 or not first(g):
                    pool.wait_ge(x_stored[t], 16 * layer * GROUPS + 16 * g)

            def hyper(g, name, t, i):
                if name == "stats":
                    reciprocal_deviation(0, g, t)
                if name == "split":
                    split(0, g, t)
                if name == "mid":
                    pool.wait_ge(s0["moments2"], i)
                    Q.tensor_tensor(var_eps2[:, t:t + 1], moments2[:, t, 1:2], eps_ln[:], ALU.add
                                    ).then_inc(s0["var_eps2"], 1)
                    pool.wait_ge(s0["var_eps2"], i)
                    Q.tensor_tensor(rstd2[:, t:t + 1], var_eps2[:, t:t + 1], half_neg, ALU.pow).then_inc(s0["rstd2"], 1)
                if name == "resid":
                    stored(0, g, t)
                    if first(g) and t == 0:
                        pool.wait_ge(s["vec_loaded"], 64)
                    pool.wait_ge(s["relu"], i)
                    Q.tensor_tensor(x_res[:, t, :], x_in[:, t, :], normed[:, t, :], ALU.add).then_inc(s["resid"], 1)
                    pool.wait_ge(s["resid"], i)
                    Q.tensor_tensor(x_res[:, t, :], x_res[:, t, :], b0b_bc[:], ALU.add).then_inc(s0["res_b"], 1)

            def gcn(g, name, t, i):
                if name == "stats":
                    reciprocal_deviation(1, g, t)
                if name == "split":
                    split(1, g, t)
                if name == "asplit":
                    pool.wait_ge(s1["asplit_hi"], i)
                    lo_of(adj_lo[:, t, :], adj_in[:, t, :], adj_hi[:, t, :]).then_inc(s1["asplit_lo"], 1)
                if name in ("adj0hi", "adj1hi", "adj2hi"):
                    pool.wait_ge(s1[name[:4] + "_hi"], i)
                    lo_of(col_lo[:, t, :], wide[:, t, F:HID], col_hi[:, t, :]).then_inc(s1[name[:4] + "_lo"], 1)
                if name == "resid":
                    stored(1, g, t)
                    pool.wait_ge(s["norm"], nl(1, g, t))
                    Q.tensor_tensor(x_res[:, t, :], x_in[:, t, :], b1_bc[:], ALU.add).then_inc(s["resid"], 1)

            def diffuse(g, name, t, i):
                if name == "stats":
                    reciprocal_deviation(2, g, t)
                if name == "resid":
                    stored(2, g, t)
                    pool.wait_ge(s["norm"], nl(2, g, t))
                    Q.tensor_tensor(x_res[:, t, :], x_in[:, t, :], ones[:, 0:1].to_broadcast([P, F]), ALU.mult).then_inc(s["resid"], 1)

            def mean(g, name, t, i):
                if name == "stats":
                    reciprocal_deviation(3, g, t)
                if name == "resid":
                    stored(3, g, t)
                    pool.wait_ge(s["norm"], nl(3, g, t))
                    Q.tensor_tensor(x_res[:, t, :], x_in[:, t, :], ones[:, 0:1].to_broadcast([P, F]), ALU.mult).then_inc(s["resid"], 1)
                if name == "asplit":
                    pool.wait_ge(s3["asplit_hi"], i)
                    lo_of(adj_lo[:, t, :], adj_in[:, t, :], adj_hi[:, t, :]).then_inc(s3["asplit_lo"], 1)

            WORK = [hyper, gcn, diffuse, mean]

            def body(layer, g, order):
                last = isinstance(g, int) and g == GROUPS - 1 and layer < 3
                b = block_end[layer]
                for name, t in order:
                    L, G = target(layer, g, name)
                    WORK[L](G, name.removesuffix("_n"), t, n(G, t))
                    if last and (name, t) in SPLIT_AFTER[layer]:
                        split_weights(b)
                        b += 1

            Q.memset(adj_in[:], 0.0)
            Q.memset(ones[:], 1.0)
            Q.memset(eps_ln[:], EPS_LN)
            Q.memset(ident[:], 0.0)
            Q.memset(wide[:, 0, F:F + P], 0.0)
            Q.memset(half_neg, -0.5).then_inc(s["pool_const"], 1)
            pool.wait_ge(s["pool_const"], 1)
            for h in range(2):
                Q.memset(wide[h * N:(h + 1) * N, 0, F + h * N:F + (h + 1) * N], 1.0).then_inc(s["pool_const"], 1)
            pool.wait_ge(s["pool_const"], 3)
            Q.affine_select(out=ident[:], in_=ident[:], compare_op=ALU.not_equal, fill=1.0, base=0,
                            pattern=[[-1, P]], channel_multiplier=1).then_inc(s["ready"], 1)
            split_weights(0)
            split_weights(2)
            for t in range(SLOTS):
                hyper(0, "stats", t, n(0, t))
            for t in range(SLOTS):
                hyper(0, "split", t, n(0, t))
                if t < 2:
                    split_weights(SLOTS + 2 * t)
            for b in range(BETA0, block_end[0], 2):
                split_weights(b)
            pool.wait_ge(s["bk_loaded"], 48)
            Q.tensor_tensor(bk_bc[:], x_res[:, 0, :], x_res[:, 1, :], ALU.add).then_inc(s["bk_sum"], 1)
            pool.wait_ge(s["bk_sum"], 1)
            Q.tensor_tensor(bk_bc[:], bk_bc[:], x_res[:, 2, :], ALU.add).then_inc(s["bk_sum"], 1)
            for layer in range(4):
                groups(pool, layer, body)


def kernel(x, adj, L0_gnn_W1, L0_gnn_b1, L0_gnn_gamma, L0_gnn_beta, L0_gnn_W2, L0_gnn_b2, L1_gnn_W1, L1_gnn_b1,
           L1_gnn_W2, L1_gnn_b2, L1_gnn_W3, L1_gnn_b3, L2_gnn_Wv, L2_gnn_bv, L2_gnn_aw, L2_gnn_ab, L2_gnn_Wk,
           L2_gnn_bk, L3_gnn_W):
    import concourse.bacc as bacc
    from concourse.bass_utils import run_bass_kernel_spmd

    def a(v):
        return np.ascontiguousarray(v)

    def row(v):
        return a(np.asarray(v).reshape(1, -1))

    def columns(v):
        return a(np.asarray(v).reshape(-1, P).T)

    x = np.asarray(x)
    arrays = {
        "x": a(x.reshape(-1, x.shape[-1])),
        "adj": a(adj),
        "adj_t": a(np.swapaxes(np.asarray(adj), 1, 2)),
        "w0a": a(np.asarray(L0_gnn_W1).T), "w0b": a(np.asarray(L0_gnn_W2).T),
        "gamma_c": columns(L0_gnn_gamma), "b0a": row(L0_gnn_b1), "beta_c": columns(L0_gnn_beta), "b0b": row(L0_gnn_b2),
        "w1_0": a(L1_gnn_W1), "w1_1": a(L1_gnn_W2), "w1_2": a(L1_gnn_W3),
        "b1_0": row(L1_gnn_b1), "b1_1": row(L1_gnn_b2), "b1_2": row(L1_gnn_b3),
        "wv_t": a(np.asarray(L2_gnn_Wv).T), "bv_c": columns(L2_gnn_bv), "aw_c": columns(L2_gnn_aw),
        "ab": row(L2_gnn_ab), "wk": a(L2_gnn_Wk), "bk": a(L2_gnn_bk),
        "w3_t": a(np.asarray(L3_gnn_W).T),
    }
    nc = bacc.Bacc("TRN2", target_bir_lowering=False, num_devices=1)
    ins = {k: nc.dram_tensor(k, v.shape, mybir.dt.from_np(v.dtype), kind="ExternalInput").ap() for k, v in arrays.items()}
    out = nc.dram_tensor("out", arrays["x"].shape, F32, kind="ExternalOutput").ap()
    graph_stack(nc, ins["x"], ins["adj"], ins["adj_t"], ins["w0a"], ins["w0b"], ins["gamma_c"], ins["b0a"],
                ins["beta_c"], ins["b0b"], [ins[f"w1_{c}"] for c in range(3)], [ins[f"b1_{c}"] for c in range(3)],
                ins["wv_t"], ins["bv_c"], ins["aw_c"], ins["ab"], ins["wk"], ins["bk"], ins["w3_t"], out)
    r = run_bass_kernel_spmd(nc, [arrays], core_ids=[0])
    return r.results[0]["out"].reshape(x.shape)
```
